# Optimizing a Trainium2 kernel written in Bass

```python
import numpy as np
import jax
import jax.numpy as jnp

def _softmax(x, axis=-1):
    return jax.nn.softmax(x, axis=axis)

def _gelu(x):
    return jax.nn.gelu(x, approximate=True)

def _silu(x):
    return jax.nn.silu(x)

def _sigmoid(x):
    return jax.nn.sigmoid(x)

def _layernorm(x, axis=-1, eps=1e-05):
    m = jnp.mean(x, axis=axis, keepdims=True)
    v = jnp.var(x, axis=axis, keepdims=True)
    return (x - m) / jnp.sqrt(v + eps)

def _scatter_add(tgt, idx, src, axis=0):
    return tgt.at[idx].add(src)

def _segment_sum(src, seg, n):
    return jax.ops.segment_sum(src, seg, n)
kernel_name = 'mk_flamingo_gated_d2_seqx_r4_f7f04f'

def setup_inputs(seed: int=0):
    np.random.seed(seed)
    _w = jnp.asarray

    def _rec_inputs():
        import jax
        import jax.numpy as jnp
        _rk = jax.random.key(seed)
        x = 0.0002279 + 0.9999 * jax.random.normal(jax.random.fold_in(_rk, 1), (1, 2048, 256), jnp.float32)
        _lenS = 2048 - jax.random.randint(jax.random.fold_in(_rk, 7), (1,), 0, max(1, 2048 // 4) + 1, jnp.int32)
        _lenS2 = 1601 - jax.random.randint(jax.random.fold_in(_rk, 8), (1,), 0, max(1, 1601 // 4) + 1, jnp.int32)
        _ctx_1024P = jax.random.normal(jax.random.fold_in(_rk, 11), (1, 16, 256), jnp.float32)
        _ctx_1024c = jax.random.dirichlet(jax.random.fold_in(_rk, 511), 0.3 * jnp.ones((16,), jnp.float32), (1, 1601))
        _ctx_1024t = jnp.einsum('bsk,bkd->bsd', _ctx_1024c, _ctx_1024P)
        _ctx_1024t = _ctx_1024t * jax.lax.rsqrt(jnp.mean(jnp.square(_ctx_1024t)) + 1e-12) * 0.953939
        ctx_1024 = -7.10856e-05 + 0.999911 * (_ctx_1024t + 0.3 * jax.random.normal(jax.random.fold_in(_rk, 611), (1, 1601, 256), jnp.float32))
        _validS = jnp.arange(2048)[None, :] < _lenS[:, None]
        _validS2 = jnp.arange(1601)[None, :] < _lenS2[:, None]
        _causal = jnp.tril(jnp.ones((2048, 2048), dtype=bool))
        mask_BxS2_bf1 = jnp.ones((1, 1601), dtype=bool)
        _g = jax.random.normal(jax.random.fold_in(_rk, 9001), (2, 2), jnp.float32)
        _g = jnp.sign(_g) * jnp.maximum(jnp.abs(_g), 1.0) + (_g == 0) * 1.0
        g_xattn = _g[0]
        g_ffn = _g[1]
        return (x, ctx_1024, mask_BxS2_bf1, g_xattn, g_ffn)
    x, ctx_1024, mask_BxS2_bf1, g_xattn, g_ffn = _rec_inputs()

    def _L0_xattn_setup():
        import jax, jax.numpy as jnp
        import numpy as np
        DIM = 256
        HEADS = 16
        DIM_HEAD = 64
        INNER = HEADS * DIM_HEAD
        B, F, Q = (16, 1024, 64)
        EPS = 1e-05
        SCALE = DIM_HEAD ** (-0.5)

        def _layernorm(x, gamma, beta):
            mu = jnp.mean(x, axis=-1, keepdims=True)
            var = jnp.var(x, axis=-1, keepdims=True)
            return (x - mu) * jax.lax.rsqrt(var + EPS) * gamma + beta
        key = jax.random.key(seed)
        ks = jax.random.split(key, 8)
        features = jax.random.normal(ks[0], (B, F, DIM), dtype=jnp.float32)
        masks = jnp.ones((B, F), dtype=bool)
        latents = jax.random.normal(ks[1], (B, Q, DIM), dtype=jnp.float32)
        Wq = jax.random.normal(ks[2], (DIM, INNER), dtype=jnp.float32) / np.sqrt(DIM)
        Wk = jax.random.normal(ks[3], (DIM, INNER), dtype=jnp.float32) / np.sqrt(DIM)
        Wv = jax.random.normal(ks[4], (DIM, INNER), dtype=jnp.float32) / np.sqrt(DIM)
        Wo = jax.random.normal(ks[5], (INNER, DIM), dtype=jnp.float32) / np.sqrt(INNER)
        gm = jnp.ones((DIM,), jnp.float32)
        bm = jnp.zeros((DIM,), jnp.float32)
        gl = jnp.ones((DIM,), jnp.float32)
        bl = jnp.zeros((DIM,), jnp.float32)
        return {'features': features, 'masks': masks, 'latents': latents, 'gm': gm, 'bm': bm, 'gl': gl, 'bl': bl, 'Wq': Wq, 'Wk': Wk, 'Wv': Wv, 'Wo': Wo}
    _L0_xattn_all = _L0_xattn_setup()
    _L0_xattn_in = {k: v for k, v in _L0_xattn_all.items() if k in ('gm', 'bm', 'gl', 'bl', 'Wq', 'Wk', 'Wv', 'Wo')}
    del _L0_xattn_all

    def _L0_ffn_setup():
        import jax, jax.numpy as jnp
        import numpy as np
        LORA_DIM = 16
        LORA_TOKEN_INDEX = 1
        B, S, D, H = (4, 512, 256, 1024)
        key = jax.random.key(seed)
        ks = jax.random.split(key, 6)
        x = jax.random.normal(ks[0], (B, S, D), dtype=jnp.float32)
        W1 = jax.random.normal(ks[1], (H, D), dtype=jnp.float32) * 0.02
        b1 = jnp.zeros((H,), dtype=jnp.float32)
        W2 = jax.random.normal(ks[2], (D, H), dtype=jnp.float32) * 0.02
        b2 = jnp.zeros((D,), dtype=jnp.float32)
        scale = jnp.asarray(0.001, dtype=jnp.float32)
        return {'x': x, 'W1': W1, 'b1': b1, 'W2': W2, 'b2': b2, 'scale': scale}
    _L0_ffn_all = _L0_ffn_setup()
    _L0_ffn_in = {k: v for k, v in _L0_ffn_all.items() if k in ('W1', 'b1', 'W2', 'b2', 'scale')}
    del _L0_ffn_all

    def _L1_xattn_setup():
        import jax, jax.numpy as jnp
        import numpy as np
        D_MODEL = 256
        NUM_HEADS = 16
        D_K = D_MODEL // NUM_HEADS

        def _split_heads(x):
            B, S, _ = x.shape
            return x.reshape(B, S, NUM_HEADS, D_K).transpose(0, 2, 1, 3)
        key = jax.random.key(seed)
        ks = jax.random.split(key, 11)
        B, S = (2, 512)
        scale = 1.0 / np.sqrt(D_MODEL)
        inp = {'Q': jax.random.normal(ks[0], (B, S, D_MODEL), jnp.float32), 'K': jax.random.normal(ks[1], (B, S, D_MODEL), jnp.float32), 'V': jax.random.normal(ks[2], (B, S, D_MODEL), jnp.float32), 'Wq': jax.random.normal(ks[3], (D_MODEL, D_MODEL), jnp.float32) * scale, 'bq': jnp.zeros((D_MODEL,), jnp.float32), 'Wk': jax.random.normal(ks[4], (D_MODEL, D_MODEL), jnp.float32) * scale, 'bk': jnp.zeros((D_MODEL,), jnp.float32), 'Wv': jax.random.normal(ks[5], (D_MODEL, D_MODEL), jnp.float32) * scale, 'bv': jnp.zeros((D_MODEL,), jnp.float32), 'Wo': jax.random.normal(ks[6], (D_MODEL, D_MODEL), jnp.float32) * scale, 'bo': jnp.zeros((D_MODEL,), jnp.float32)}
        return inp
    _L1_xattn_all = _L1_xattn_setup()
    _L1_xattn_in = {k: v for k, v in _L1_xattn_all.items() if k in ('Wq', 'bq', 'Wk', 'bk', 'Wv', 'bv', 'Wo', 'bo')}
    del _L1_xattn_all

    def _L1_ffn_setup():
        import jax, jax.numpy as jnp
        import numpy as np
        DIM = 256
        DEPTH = 2
        HEADS = 8
        DIM_HEAD = 64
        WINDOW = 128
        INNER = HEADS * DIM_HEAD
        HID = int(DIM * 4 * 2 / 3)
        B, N = (2, 2048)
        QK_SCALE = 8.0

        def shift_token(t):
            t1, t2 = jnp.split(t, 2, axis=-1)
            t2 = jnp.pad(t2, ((0, 0), (1, 0), (0, 0)))[:, :-1]
            return jnp.concatenate([t1, t2], axis=-1)

        def l2norm(t):
            return t / jnp.clip(jnp.linalg.norm(t, axis=-1, keepdims=True), 1e-12)

        def rotate_half(x):
            x1, x2 = jnp.split(x, 2, axis=-1)
            return jnp.concatenate([-x2, x1], axis=-1)

        def rotary_xpos(q, k):
            n = q.shape[-2]
            half_idx = jnp.arange(0, DIM_HEAD, 2, dtype=jnp.float32)
            inv_freq = 1.0 / 10000.0 ** (half_idx / DIM_HEAD)
            t = jnp.arange(n, dtype=jnp.float32)
            freqs = t[:, None] * inv_freq[None, :]
            freqs = jnp.concatenate([freqs, freqs], axis=-1)
            base = (half_idx + 0.4 * DIM_HEAD) / (1.4 * DIM_HEAD)
            power = (t - n // 2) / float(WINDOW // 2)
            scale = base[None, :] ** power[:, None]
            scale = jnp.concatenate([scale, scale], axis=-1)
            cos, sin = (jnp.cos(freqs), jnp.sin(freqs))
            q = q * cos * scale + rotate_half(q) * sin * scale
            k = k * cos / scale + rotate_half(k) * sin / scale
            return (q, k)

        def local_attention(q, k, v):
            b, h, n, d = q.shape
            w = n // WINDOW
            bq = q.reshape(b, h, w, WINDOW, d) * QK_SCALE
            bk = k.reshape(b, h, w, WINDOW, d)
            bv = v.reshape(b, h, w, WINDOW, d)

            def look_around(t):
                p = jnp.pad(t, ((0, 0), (0, 0), (1, 0), (0, 0), (0, 0)))
                return jnp.concatenate([p[:, :, :w], p[:, :, 1:]], axis=3)
            bk, bv = (look_around(bk), look_around(bv))
            bt = jnp.arange(n).reshape(w, WINDOW)
            btp = jnp.pad(bt, ((1, 0), (0, 0)), constant_values=-1)
            btk = jnp.concatenate([btp[:w], btp[1:]], axis=1)
            sim = jnp.einsum('bhwid,bhwjd->bhwij', bq, bk)
            i = bt[:, :, None]
            j = btk[:, None, :]
            mask = (i < j) | (i > j + WINDOW) | (j == -1)
            sim = jnp.where(mask, -jnp.finfo(sim.dtype).max, sim)
            attn = jax.nn.softmax(sim, axis=-1)
            out = jnp.einsum('bhwij,bhwjd->bhwid', attn, bv)
            return out.reshape(b, h, n, d)

        def _layer(x, wqkv, qs, ksc, wo, lg, lb, w1, b1, w2, b2):
            b, n, _ = x.shape
            h = shift_token(x)
            qkv = h @ wqkv
            q, k, v = jnp.split(qkv, 3, axis=-1)
            to_heads = lambda t: t.reshape(b, n, HEADS, DIM_HEAD).transpose(0, 2, 1, 3)
            q, k, v = (to_heads(q), to_heads(k), to_heads(v))
            q = l2norm(q) * qs
            k = l2norm(k) * ksc
            q, k = rotary_xpos(q, k)
            o = local_attention(q, k, v)
            o = o.transpose(0, 2, 1, 3).reshape(b, n, INNER)
            x = x + o @ wo
            h = shift_token(x)
            mu = h.mean(-1, keepdims=True)
            var = h.var(-1, keepdims=True)
            h = (h - mu) / jnp.sqrt(var + 1e-05) * lg + lb
            h = h @ w1 + b1
            a, g = jnp.split(h, 2, axis=-1)
            h = a * jax.nn.gelu(g, approximate=False)
            x = x + h @ w2 + b2
            return x
        key = jax.random.key(seed)
        ks = jax.random.split(key, 6)
        return {'x': jax.random.normal(ks[0], (B, N, DIM), jnp.float32), 'wqkv': jax.random.normal(ks[1], (DEPTH, DIM, 3 * INNER), jnp.float32) * 0.02, 'q_scale': jnp.ones((DEPTH, DIM_HEAD), jnp.float32), 'k_scale': jnp.ones((DEPTH, DIM_HEAD), jnp.float32), 'wo': jax.random.normal(ks[2], (DEPTH, INNER, DIM), jnp.float32) * 0.02, 'ln_g': jnp.ones((DEPTH, DIM), jnp.float32), 'ln_b': jnp.zeros((DEPTH, DIM), jnp.float32), 'w1': jax.random.normal(ks[3], (DEPTH, DIM, 2 * HID), jnp.float32) * 0.02, 'b1': jnp.zeros((DEPTH, 2 * HID), jnp.float32), 'w2': jax.random.normal(ks[4], (DEPTH, HID, DIM), jnp.float32) * 0.02, 'b2': jnp.zeros((DEPTH, DIM), jnp.float32)}
    _L1_ffn_all = _L1_ffn_setup()
    _L1_ffn_in = {k: v for k, v in _L1_ffn_all.items() if k in ('wqkv', 'q_scale', 'k_scale', 'wo', 'ln_g', 'ln_b', 'w1', 'b1', 'w2', 'b2')}
    del _L1_ffn_all
    return {'x': x, 'ctx_1024': ctx_1024, 'mask_BxS2_bf1': mask_BxS2_bf1, 'g_xattn': g_xattn, 'g_ffn': g_ffn, 'L0_xattn_gm': _L0_xattn_in['gm'], 'L0_xattn_bm': _L0_xattn_in['bm'], 'L0_xattn_gl': _L0_xattn_in['gl'], 'L0_xattn_bl': _L0_xattn_in['bl'], 'L0_xattn_Wq': _L0_xattn_in['Wq'], 'L0_xattn_Wk': _L0_xattn_in['Wk'], 'L0_xattn_Wv': _L0_xattn_in['Wv'], 'L0_xattn_Wo': _L0_xattn_in['Wo'], 'L0_ffn_W1': _L0_ffn_in['W1'], 'L0_ffn_b1': _L0_ffn_in['b1'], 'L0_ffn_W2': _L0_ffn_in['W2'], 'L0_ffn_b2': _L0_ffn_in['b2'], 'L0_ffn_scale': _L0_ffn_in['scale'], 'L1_xattn_Wq': _L1_xattn_in['Wq'], 'L1_xattn_bq': _L1_xattn_in['bq'], 'L1_xattn_Wk': _L1_xattn_in['Wk'], 'L1_xattn_bk': _L1_xattn_in['bk'], 'L1_xattn_Wv': _L1_xattn_in['Wv'], 'L1_xattn_bv': _L1_xattn_in['bv'], 'L1_xattn_Wo': _L1_xattn_in['Wo'], 'L1_xattn_bo': _L1_xattn_in['bo'], 'L1_ffn_wqkv': _L1_ffn_in['wqkv'], 'L1_ffn_q_scale': _L1_ffn_in['q_scale'], 'L1_ffn_k_scale': _L1_ffn_in['k_scale'], 'L1_ffn_wo': _L1_ffn_in['wo'], 'L1_ffn_ln_g': _L1_ffn_in['ln_g'], 'L1_ffn_ln_b': _L1_ffn_in['ln_b'], 'L1_ffn_w1': _L1_ffn_in['w1'], 'L1_ffn_b1': _L1_ffn_in['b1'], 'L1_ffn_w2': _L1_ffn_in['w2'], 'L1_ffn_b2': _L1_ffn_in['b2']}

def reference(x, ctx_1024, mask_BxS2_bf1, g_xattn, g_ffn, L0_xattn_gm, L0_xattn_bm, L0_xattn_gl, L0_xattn_bl, L0_xattn_Wq, L0_xattn_Wk, L0_xattn_Wv, L0_xattn_Wo, L0_ffn_W1, L0_ffn_b1, L0_ffn_W2, L0_ffn_b2, L0_ffn_scale, L1_xattn_Wq, L1_xattn_bq, L1_xattn_Wk, L1_xattn_bk, L1_xattn_Wv, L1_xattn_bv, L1_xattn_Wo, L1_xattn_bo, L1_ffn_wqkv, L1_ffn_q_scale, L1_ffn_k_scale, L1_ffn_wo, L1_ffn_ln_g, L1_ffn_ln_b, L1_ffn_w1, L1_ffn_b1, L1_ffn_w2, L1_ffn_b2):
    import jax
    import jax.numpy as jnp

    def _L0_xattn_ref(features, masks, latents, gm, bm, gl, bl, Wq, Wk, Wv, Wo):
        import jax, jax.numpy as jnp
        import numpy as np
        DIM = 256
        HEADS = 16
        DIM_HEAD = 64
        INNER = HEADS * DIM_HEAD
        B, F, Q = (16, 1024, 64)
        EPS = 1e-05
        SCALE = DIM_HEAD ** (-0.5)

        def _layernorm(x, gamma, beta):
            mu = jnp.mean(x, axis=-1, keepdims=True)
            var = jnp.var(x, axis=-1, keepdims=True)
            return (x - mu) * jax.lax.rsqrt(var + EPS) * gamma + beta
        b, f, d = features.shape
        q_len = latents.shape[1]
        x = _layernorm(features, gm, bm)
        lat = _layernorm(latents, gl, bl)
        q = (lat @ Wq).reshape(b, q_len, HEADS, DIM_HEAD).transpose(0, 2, 1, 3)
        kv_input = jnp.concatenate([x, lat], axis=1)
        kv_mask = jnp.concatenate([masks, jnp.ones((b, q_len), dtype=bool)], axis=1)
        kv_mask = kv_mask[:, None, None, :]
        k = (kv_input @ Wk).reshape(b, f + q_len, HEADS, DIM_HEAD).transpose(0, 2, 1, 3)
        v = (kv_input @ Wv).reshape(b, f + q_len, HEADS, DIM_HEAD).transpose(0, 2, 1, 3)
        q = q * SCALE
        sim = jnp.einsum('bhqd,bhfd->bhqf', q, k)
        sim = sim - jax.lax.stop_gradient(jnp.max(sim, axis=-1, keepdims=True))
        sim = jnp.where(kv_mask, sim, -jnp.inf)
        alphas = jax.nn.softmax(sim, axis=-1)
        out = jnp.einsum('bhqf,bhfd->bhqd', alphas, v)
        out = out.transpose(0, 2, 1, 3).reshape(b, q_len, INNER)
        return out @ Wo

    def _L0_ffn_ref(x, W1, b1, W2, b2, scale):
        import jax, jax.numpy as jnp
        import numpy as np
        LORA_DIM = 16
        LORA_TOKEN_INDEX = 1
        B, S, D, H = (4, 512, 256, 1024)
        Bx, Sx, Dx = x.shape
        Hx = W1.shape[0]
        lt = jax.lax.dynamic_slice_in_dim(x, LORA_TOKEN_INDEX, LORA_DIM, axis=1)
        even = lt[:, ::2, :]
        odd = lt[:, 1::2, :]
        m1 = (even[:, :4, :, None] * odd[:, :4, None, :]).reshape(Bx, Hx, Dx)
        m2 = (even[:, 4:, :, None] * odd[:, 4:, None, :]).reshape(Bx, Dx, Hx)
        h = jnp.einsum('bsd,hd->bsh', x, W1) + scale * jnp.einsum('bsd,bhd->bsh', x, m1) + b1
        h = jax.nn.gelu(h, approximate=False)
        out = jnp.einsum('bsh,oh->bso', h, W2) + scale * jnp.einsum('bsh,boh->bso', h, m2) + b2
        return out

    def _L1_xattn_ref(Q, K, V, Wq, bq, Wk, bk, Wv, bv, Wo, bo):
        import jax, jax.numpy as jnp
        import numpy as np
        D_MODEL = 256
        NUM_HEADS = 16
        D_K = D_MODEL // NUM_HEADS

        def _split_heads(x):
            B, S, _ = x.shape
            return x.reshape(B, S, NUM_HEADS, D_K).transpose(0, 2, 1, 3)
        q = _split_heads(Q @ Wq + bq)
        k = _split_heads(K @ Wk + bk)
        v = _split_heads(V @ Wv + bv)
        scores = jnp.einsum('bhqd,bhkd->bhqk', q, k) / np.sqrt(D_K)
        probs = jax.nn.softmax(scores, axis=-1)
        attn = jnp.einsum('bhqk,bhkd->bhqd', probs, v)
        B, H, S, dk = attn.shape
        out = attn.transpose(0, 2, 1, 3).reshape(B, S, D_MODEL)
        return out @ Wo + bo

    def _L1_ffn_ref(x, wqkv, q_scale, k_scale, wo, ln_g, ln_b, w1, b1, w2, b2):
        import jax, jax.numpy as jnp
        import numpy as np
        DIM = 256
        DEPTH = 2
        HEADS = 8
        DIM_HEAD = 64
        WINDOW = 128
        INNER = HEADS * DIM_HEAD
        HID = int(DIM * 4 * 2 / 3)
        B, N = (2, 2048)
        QK_SCALE = 8.0

        def shift_token(t):
            t1, t2 = jnp.split(t, 2, axis=-1)
            t2 = jnp.pad(t2, ((0, 0), (1, 0), (0, 0)))[:, :-1]
            return jnp.concatenate([t1, t2], axis=-1)

        def l2norm(t):
            return t / jnp.clip(jnp.linalg.norm(t, axis=-1, keepdims=True), 1e-12)

        def rotate_half(x):
            x1, x2 = jnp.split(x, 2, axis=-1)
            return jnp.concatenate([-x2, x1], axis=-1)

        def rotary_xpos(q, k):
            n = q.shape[-2]
            half_idx = jnp.arange(0, DIM_HEAD, 2, dtype=jnp.float32)
            inv_freq = 1.0 / 10000.0 ** (half_idx / DIM_HEAD)
            t = jnp.arange(n, dtype=jnp.float32)
            freqs = t[:, None] * inv_freq[None, :]
            freqs = jnp.concatenate([freqs, freqs], axis=-1)
            base = (half_idx + 0.4 * DIM_HEAD) / (1.4 * DIM_HEAD)
            power = (t - n // 2) / float(WINDOW // 2)
            scale = base[None, :] ** power[:, None]
            scale = jnp.concatenate([scale, scale], axis=-1)
            cos, sin = (jnp.cos(freqs), jnp.sin(freqs))
            q = q * cos * scale + rotate_half(q) * sin * scale
            k = k * cos / scale + rotate_half(k) * sin / scale
            return (q, k)

        def local_attention(q, k, v):
            b, h, n, d = q.shape
            w = n // WINDOW
            bq = q.reshape(b, h, w, WINDOW, d) * QK_SCALE
            bk = k.reshape(b, h, w, WINDOW, d)
            bv = v.reshape(b, h, w, WINDOW, d)

            def look_around(t):
                p = jnp.pad(t, ((0, 0), (0, 0), (1, 0), (0, 0), (0, 0)))
                return jnp.concatenate([p[:, :, :w], p[:, :, 1:]], axis=3)
            bk, bv = (look_around(bk), look_around(bv))
            bt = jnp.arange(n).reshape(w, WINDOW)
            btp = jnp.pad(bt, ((1, 0), (0, 0)), constant_values=-1)
            btk = jnp.concatenate([btp[:w], btp[1:]], axis=1)
            sim = jnp.einsum('bhwid,bhwjd->bhwij', bq, bk)
            i = bt[:, :, None]
            j = btk[:, None, :]
            mask = (i < j) | (i > j + WINDOW) | (j == -1)
            sim = jnp.where(mask, -jnp.finfo(sim.dtype).max, sim)
            attn = jax.nn.softmax(sim, axis=-1)
            out = jnp.einsum('bhwij,bhwjd->bhwid', attn, bv)
            return out.reshape(b, h, n, d)

        def _layer(x, wqkv, qs, ksc, wo, lg, lb, w1, b1, w2, b2):
            b, n, _ = x.shape
            h = shift_token(x)
            qkv = h @ wqkv
            q, k, v = jnp.split(qkv, 3, axis=-1)
            to_heads = lambda t: t.reshape(b, n, HEADS, DIM_HEAD).transpose(0, 2, 1, 3)
            q, k, v = (to_heads(q), to_heads(k), to_heads(v))
            q = l2norm(q) * qs
            k = l2norm(k) * ksc
            q, k = rotary_xpos(q, k)
            o = local_attention(q, k, v)
            o = o.transpose(0, 2, 1, 3).reshape(b, n, INNER)
            x = x + o @ wo
            h = shift_token(x)
            mu = h.mean(-1, keepdims=True)
            var = h.var(-1, keepdims=True)
            h = (h - mu) / jnp.sqrt(var + 1e-05) * lg + lb
            h = h @ w1 + b1
            a, g = jnp.split(h, 2, axis=-1)
            h = a * jax.nn.gelu(g, approximate=False)
            x = x + h @ w2 + b2
            return x
        for l in range(DEPTH):
            x = _layer(x, wqkv[l], q_scale[l], k_scale[l], wo[l], ln_g[l], ln_b[l], w1[l], b1[l], w2[l], b2[l])
        return x
    x = x + jnp.tanh(g_xattn[0]) * _L0_xattn_ref(ctx_1024, mask_BxS2_bf1, _layernorm(x, axis=-1), L0_xattn_gm, L0_xattn_bm, L0_xattn_gl, L0_xattn_bl, L0_xattn_Wq, L0_xattn_Wk, L0_xattn_Wv, L0_xattn_Wo)
    x = x + jnp.tanh(g_ffn[0]) * _L0_ffn_ref(_layernorm(x, axis=-1), L0_ffn_W1, L0_ffn_b1, L0_ffn_W2, L0_ffn_b2, L0_ffn_scale)
    x = x + jnp.tanh(g_xattn[1]) * _L1_xattn_ref(_layernorm(x, axis=-1), ctx_1024, ctx_1024, L1_xattn_Wq, L1_xattn_bq, L1_xattn_Wk, L1_xattn_bk, L1_xattn_Wv, L1_xattn_bv, L1_xattn_Wo, L1_xattn_bo)
    x = x + jnp.tanh(g_ffn[1]) * _L1_ffn_ref(_layernorm(x, axis=-1), L1_ffn_wqkv, L1_ffn_q_scale, L1_ffn_k_scale, L1_ffn_wo, L1_ffn_ln_g, L1_ffn_ln_b, L1_ffn_w1, L1_ffn_b1, L1_ffn_w2, L1_ffn_b2)
    return x

_drawn_inputs = setup_inputs


def setup_inputs(seed=0):
    import zlib

    import numpy as np

    out = dict(_drawn_inputs(seed))
    spreads = {'g_ffn': (-1.0, 0.2),
     'L0_xattn_gm': (1.0, 0.596),
     'L0_xattn_bm': (0.0, 0.293),
     'L0_xattn_gl': (1.0, 0.6),
     'L0_xattn_bl': (0.0, 0.1),
     'L0_ffn_b1': (0.0, 0.311),
     'L0_ffn_b2': (0.0, 0.1),
     'L1_xattn_bq': (0.0, 0.51),
     'L1_xattn_bk': (0.0, 2.0),
     'L1_xattn_bv': (0.0, 0.1),
     'L1_xattn_bo': (0.0, 0.1),
     'L1_ffn_q_scale': (1.0, 0.6),
     'L1_ffn_k_scale': (1.0, 0.6),
     'L1_ffn_ln_g': (1.0, 0.2),
     'L1_ffn_ln_b': (0.0, 0.491),
     'L1_ffn_b1': (0.0, 0.1),
     'L1_ffn_b2': (0.0, 0.1)}
    factors = {}
    for name, (base, spread) in spreads.items():
        noise = np.random.default_rng([zlib.crc32(name.encode()), seed]).standard_normal(out[name].shape)
        drawn = base * np.exp(spread * noise) if base else spread * noise
        out[name] = jnp.asarray(drawn.astype(out[name].dtype))
    for name, factor in factors.items():
        out[name] = (out[name] * factor).astype(out[name].dtype)
    return out
```

```python
import numpy as np
import concourse.bass as bass
from concourse import mybir
from contextlib import ExitStack

fp32 = mybir.dt.float32
fp16 = mybir.dt.float16
bf16 = mybir.dt.bfloat16
int32 = mybir.dt.int32
ALU = mybir.AluOpType
ACT = mybir.ActivationFunctionType
AX = mybir.AxisListType

P = 128
S, D = 2048, 256
CTX = 1601
ST = S // P
CT = -(-CTX // P)
CLAST = CTX - (CT - 1) * P
DK = D // P
EPS = 1e-5
BANK = 512

AH, AD = 16, 64
PAIRS = AH // 2
KT = CT + ST
KEYS = KT * P
LAT0 = CT * P
MASKED = -60000.0

SAFE_SCORE = 60.0
SAFE_BITS = int(np.float32(SAFE_SCORE ** 2).view(np.int32))
MAX_ROW = 64

ds = bass.ds


class Memory:

    def __init__(self, nc, ctx):
        self.nc, self.ctx, self.sems = nc, ctx, {}
        self.X = self.sbuf("X", [P, ST, D])
        self.ident = self.sbuf("ident", [P, P])
        self.gate = self.sbuf("gate", [P, 4])
        self.mean = self.sbuf("mean", [P, ST])
        self.rstd = self.sbuf("rstd", [P, ST])
        self.PS = ctx.enter_context(nc.psum_tensor("PS", [P, 8, BANK], fp32))

    def sbuf(self, name, shape, dtype=fp32):
        return self.ctx.enter_context(self.nc.sbuf_tensor(name, shape, dtype))

    def sem(self, name):
        if name not in self.sems:
            self.sems[name] = self.ctx.enter_context(self.nc.semaphore(name))
        return self.sems[name]

    def clear_semaphores(self, prefix):
        with self.nc.Block() as block:
            @block.sync
            def _(sp):
                for name, sem in self.sems.items():
                    if name.startswith(prefix):
                        sp.sem_clear(sem)


def setup(nc, m, x_d, ident_d, gates_d):
    raw = m.sbuf("gate_raw", [P, 4])
    loaded, gates_done = m.sem("setup_loaded"), m.sem("gates_done")
    with nc.Block() as block:
        @block.sync
        def _(sp):
            sp.dma_start(m.X[:], x_d.rearrange("(t p) d -> p t d", p=P)).then_inc(loaded, 16)
            sp.dma_start(m.ident[:], ident_d).then_inc(loaded, 16)
            sp.dma_start(raw[:], gates_d.partition_broadcast(P)).then_inc(loaded, 16)

        @block.scalar
        def _(act):
            act.wait_ge(loaded, 48)
            nc.scalar.activation(m.gate[:], raw[:], ACT.Tanh).then_inc(gates_done, 1)


def token_statistics(nc, m, name, src, T, twice=False, sems=None):
    sems = sems or name
    with ExitStack() as own:
        sb = lambda n, s, d=fp32: own.enter_context(nc.sbuf_tensor(f"{name}_{n}", s, d))
        stats = sb("stats", [P, T, 6])
        work = sb("work", [P, 8, T])
        mean, rstd = m.mean[:, 0:T], m.rstd[:, 0:T]
        stats_done, step = m.sem(f"{sems}_stats"), m.sem(f"{sems}_step")
        root_wanted, root_done = m.sem(f"{sems}_rootw"), m.sem(f"{sems}_root")
        with nc.Block() as block:
            @block.vector
            def _(dve):
                with dve.Fori(0, T) as t:
                    nc.vector.bn_stats(stats[:, ds(t, 1), :].rearrange("p o s -> p (o s)"),
                                       src[:, ds(t, 1), :].rearrange("p o d -> p (o d)")).then_inc(stats_done, 1)
                dve.wait_ge(stats_done, T)
                me, mo = stats[:, :, 1], stats[:, :, 4]
                qe, qo = stats[:, :, 2], stats[:, :, 5]
                done = [0]

                def chain(ins):
                    done[0] += 1
                    ins.then_inc(step, 1)
                    dve.wait_ge(step, done[0])

                nc.vector.tensor_tensor(work[:, 0, :], me, mo, ALU.add)
                nc.vector.tensor_tensor(work[:, 1, :], me, mo, ALU.subtract)
                nc.vector.tensor_tensor(work[:, 2, :], qe, qo, ALU.add)
                chain(nc.vector.memset(work[:, 3, :], EPS))
                nc.vector.tensor_scalar(mean, work[:, 0, :], 0.5, None, ALU.mult)
                nc.vector.scalar_tensor_tensor(out=work[:, 4, :], in0=work[:, 1, :], scalar=0.25,
                                               in1=work[:, 1, :], op0=ALU.mult, op1=ALU.mult)
                chain(nc.vector.scalar_tensor_tensor(out=work[:, 5, :], in0=work[:, 2, :], scalar=1.0 / D,
                                                     in1=work[:, 3, :], op0=ALU.mult, op1=ALU.add))
                nc.vector.tensor_tensor(work[:, 6, :], work[:, 4, :], work[:, 5, :],
                                        ALU.add).then_inc(root_wanted, 1)
                dve.wait_ge(root_done, 1)
                chain(nc.vector.reciprocal(rstd, work[:, 7, :]))
                if twice:
                    chain(nc.vector.tensor_scalar(work[:, 0, :], work[:, 2, :], 1.0 / D, None, ALU.mult))
                    nc.vector.tensor_tensor(work[:, 5, :], work[:, 0, :], work[:, 4, :], ALU.add)
                    chain(nc.vector.tensor_tensor(work[:, 1, :], rstd, rstd, ALU.mult))
                    chain(nc.vector.tensor_tensor(work[:, 2, :], work[:, 5, :], work[:, 1, :], ALU.mult))
                    nc.vector.tensor_scalar(work[:, 6, :], work[:, 2, :], EPS, None,
                                            ALU.add).then_inc(root_wanted, 1)
                    dve.wait_ge(root_done, 2)
                    chain(nc.vector.reciprocal(work[:, 0, :], work[:, 7, :]))
                    chain(nc.vector.tensor_tensor(rstd, rstd, work[:, 0, :], ALU.mult))

            @block.scalar
            def _(act):
                for i in range(2 if twice else 1):
                    act.wait_ge(root_wanted, i + 1)
                    nc.scalar.activation(work[:, 7, :], work[:, 6, :], ACT.Sqrt).then_inc(root_done, 1)


def layernorm_transposed(nc, m, name, src, dst, dst0, groups, affine=None, twice=False, sems=None):
    token_statistics(nc, m, name, src, groups * 4, twice, sems)
    sems = sems or name
    with ExitStack() as own:
        staged = [own.enter_context(nc.sbuf_tensor(f"{name}_staged{i}", [P, 4, D], fp32)) for i in range(2)]
        normed, transposed, moved = m.sem(f"{sems}_normed"), m.sem(f"{sems}_tr"), m.sem(f"{sems}_mv")
        with nc.Block() as block:
            @block.vector
            def _(dve):
                with dve.Fori(0, groups // 2) as gg:
                    g = gg * 2
                    for half in range(2):
                        dve.wait_ge(transposed, g)
                        for j in range(4):
                            t = g * 4 + (half * 4 + j)
                            last = nc.vector.tensor_scalar(
                                staged[half][:, j, :], src[:, ds(t, 1), :].rearrange("p o d -> p (o d)"),
                                m.mean[:, ds(t, 1)], m.rstd[:, ds(t, 1)], ALU.subtract, ALU.mult)
                        last.then_inc(normed, 1)

            @block.scalar
            def _(act):
                with act.Fori(0, groups) as g:
                    act.wait_ge(transposed, g + 1)
                    for k in range(DK):
                        out = dst[:, k, ds(g * BANK + dst0, BANK)]
                        bank = m.PS[:, ds(g * 2 + k, 1), :].rearrange("p o c -> p (o c)")
                        if affine is None:
                            ins = nc.scalar.activation(out, bank, ACT.Copy)
                        else:
                            ins = nc.scalar.activation(out, bank, ACT.Identity, scale=affine[0][:, k:k + 1],
                                                       bias=affine[1][:, k:k + 1])
                    ins.then_inc(moved, 1)

            @block.tensor
            def _(pe):
                for g in range(groups):
                    pe.wait_ge(normed, g + 1)
                    for k in range(DK):
                        for j in range(4):
                            last = nc.tensor.transpose(m.PS[:, 2 * g + k, j * P:(j + 1) * P],
                                                       staged[g % 2][:, j, k * P:(k + 1) * P], m.ident[:])
                    last.then_inc(transposed, 1)


def score_maxima_pe(nc, m, pe, queries, keys, spans, negated, scored, reduced, base_r, ready=()):
    with pe.Fori(0, ST) as t:
        for sem, value in ready:
            pe.wait_ge(sem, value)
        for s, (c0, n) in enumerate(spans):
            pe.wait_ge(reduced, base_r + t * len(spans) + s)
            for b in range(-(-n // BANK)):
                k0, w = c0 + b * BANK, min(BANK, n - b * BANK)
                for i, (q, k) in enumerate(zip(queries, keys)):
                    last = nc.tensor.matmul(m.PS[:, b, 0:w], q[:, ds(t * P, P)], k[:, k0:k0 + w],
                                            start=(i == 0), stop=(i == len(keys) - 1))
            last.then_inc(scored, 1)
    pe.wait_ge(reduced, base_r + (ST * len(spans) + 1))
    for t in range(ST):
        last = nc.tensor.matmul(m.PS[MAX_ROW:MAX_ROW + 1, t // 4, (t % 4) * P:(t % 4 + 1) * P], negated[:, t:t + 1],
                                m.ident[:], start=True, stop=True)
    last.then_inc(scored, 1)


def score_maxima_dve(nc, m, dve, spans, partial, negated, row, scored, reduced, base_s, base_r):
    with dve.Fori(0, ST) as t:
        for s, (c0, n) in enumerate(spans):
            dve.wait_ge(scored, base_s + t * len(spans) + (s + 1))
            nb = n // BANK
            out = partial[:, s, 0:1, ds(t, 1)].rearrange("p a b -> p (a b)")
            nc.vector.tensor_reduce(out, m.PS[:, 0:nb, :].rearrange("p b c -> p (b c)"), AX.X, ALU.max)
            out = partial[:, s, 1:2, ds(t, 1)].rearrange("p a b -> p (a b)")
            w = n - nb * BANK if n % BANK else BANK
            nc.vector.tensor_reduce(out, m.PS[:, -(-n // BANK) - 1, 0:w], AX.X, ALU.max).then_inc(reduced, 1)
    dve.wait_ge(reduced, base_r + ST * len(spans))
    nc.vector.tensor_reduce(negated[:], partial[:].rearrange("p s a t -> p t (s a)"), AX.X, ALU.max,
                            negate=True).then_inc(reduced, 1)
    dve.wait_ge(scored, base_s + (ST * len(spans) + 1))
    nc.vector.tensor_copy(row, m.PS[MAX_ROW:MAX_ROW + 1, 0:4, :].rearrange("p b c -> p (b c)")).then_inc(reduced, 1)


def context_attention(nc, m, ctx_d, mask_d, affines_d, wq_d, wk_d, wv_d, wo_d):
    with ExitStack() as own:
        sb = lambda n, s, d=fp32: own.enter_context(nc.sbuf_tensor(f"a_{n}", s, d))
        kvT = sb("kvT", [P, DK, KEYS + (4 * -(-CT // 4) - CT) * P])
        aff = sb("aff", [P, 4, DK])
        masked = sb("masked", [P, LAT0], fp16)
        with nc.sbuf_tensor("a_ctx", [P, 16, D], fp32) as ctx_tok:
            with nc.sbuf_tensor("a_mask", [P, LAT0], mybir.dt.uint8) as mask_f:
                loaded, cleared, bias_done = m.sem("a_loaded"), m.sem("a_cleared"), m.sem("a_bias_done")
                with nc.Block() as block:
                    @block.gpsimd
                    def _(pool):
                        nc.gpsimd.memset(ctx_tok[:, CT - 1:16, :], 0.0).then_inc(cleared, 1)

                    @block.sync
                    def _(sp):
                        sp.dma_start(ctx_tok[:, 0:CT - 1, :],
                                     ctx_d[0:(CT - 1) * P, :].rearrange("(t p) d -> p t d", p=P)).then_inc(loaded, 16)
                        sp.dma_start(aff[:], affines_d).then_inc(loaded, 16)
                        sp.wait_ge(cleared, 2)
                        sp.dma_start(ctx_tok[0:CLAST, CT - 1, :], ctx_d[(CT - 1) * P:CTX, :]).then_inc(loaded, 16)
                        sp.dma_start(mask_f[96:97, 0:CTX], mask_d).then_inc(loaded, 16)
                        sp.wait_ge(loaded, 64)

                    @block.vector
                    def _(dve):
                        nc.vector.memset(mask_f[96:97, :], 0).then_inc(cleared, 1)
                        dve.wait_ge(loaded, 64)
                        nc.vector.tensor_scalar(masked[96:97, :], mask_f[96:97, :], -MASKED, MASKED,
                                                ALU.mult, ALU.add).then_inc(bias_done, 1)
            layernorm_transposed(nc, m, "a_ctx", ctx_tok, kvT, 0, 4, (aff[:, 0, :], aff[:, 1, :]))
        layernorm_transposed(nc, m, "a_lat", m.X, kvT, LAT0, 4, (aff[:, 2, :], aff[:, 3, :]), twice=True)

        K1 = [sb(f"K1_{h}", [P, KEYS], fp16) for h in range(2)]
        K2 = [sb(f"K2_{h}", [P, KEYS], fp16) for h in range(2)]
        Q1 = [sb(f"Q1_{h}", [P, S], fp16) for h in range(2)]
        Q2 = [sb(f"Q2_{h}", [P, S], fp16) for h in range(2)]
        V = [sb(f"V_{h}", [P, KT, AD]) for h in range(2)]
        probs = [sb(f"probs{i}", [P, 2 * BANK]) for i in range(3)]
        prob_sums = [sb(f"prob_sums{i}", [P, 2 * BANK]) for i in range(2)]
        ones = sb("ones", [P, AD])
        wqkv = [sb(f"w{n}", [P, DK, P]) for n in "qkv"]
        wo = sb("wo", [P, D])
        heads_outT = sb("heads_outT", [P, S])
        inverse = [sb(f"inverse{i}", [P, BANK]) for i in range(2)]
        squares = [sb(f"squares{i}", [P, BANK], bf16) for i in range(2)]
        head_ones = sb("head_ones", [P, 32], bf16)
        peaks, top, bound = sb("peaks", [P, 3]), sb("top", [1, 3]), sb("bound", [1, 1])
        spans = [(0, 4 * BANK), (4 * BANK, KEYS - 4 * BANK)]
        partial, negated = sb("partial", [P, len(spans), 2, ST]), sb("negated", [P, ST])

        rows_set, ones_cleared = m.sem("a_rows_set"), m.sem("a_ones_cleared")
        with nc.Block() as block:
            @block.gpsimd
            def _(pool):
                nc.gpsimd.memset(ones[:], 1.0)
                nc.gpsimd.memset(head_ones[:], 0.0).then_inc(ones_cleared, 1)
                pool.wait_ge(ones_cleared, 1)
                for h in range(2):
                    nc.gpsimd.memset(head_ones[64 * h:64 * h + 64, h:h + 1], 1.0)

            @block.vector
            def _(dve):
                for h in range(2):
                    nc.vector.memset(K2[h][64:128, :], 0.0)
                    nc.vector.memset(Q2[h][64:128, :], 0.0).then_inc(rows_set, 1)
                dve.wait_ge(rows_set, 2)
                for h in range(2):
                    nc.vector.memset(K2[h][64:65, :], 1.0)
                    nc.vector.memset(Q2[h][96:97, :], 1.0)
                    nc.vector.tensor_copy(K2[h][96:97, 0:LAT0], masked[96:97, :])

        NKU, NQU, NVU = -(-KEYS // BANK), S // BANK, -(-KT // 4)
        UNITS = NKU + NQU + NVU
        BLOCKS = 4
        STEPS = BLOCKS * KT
        HALF = S // 2
        w_loaded, wo_loaded = m.sem("a_w_loaded"), m.sem("a_wo_loaded")
        projected, split_hi, unit_free = (m.sem(f"a_{n}") for n in ("projected", "hi", "unit_free"))
        scored, exped, applied, summed = (m.sem(f"a_{n}") for n in ("scored", "exped", "applied", "summed"))
        totalled, inverted, block_out = (m.sem(f"a_{n}") for n in ("totalled", "inverted", "block_out"))
        mixed, added = (m.sem(f"a_{n}") for n in ("mixed", "added"))
        squared, normed, peaked, peaks_turned, topped, bounded = (
            m.sem(f"a_{n}") for n in ("squared", "normed", "peaked", "peaks_turned", "topped", "bounded"))
        max_scored, max_reduced = (m.sem(f"a_{n}") for n in ("max_scored", "max_reduced"))
        SCALE = AD ** -0.5
        NORMS = NKU + NQU
        MAX_SCORED, MAX_REDUCED = ST * len(spans) + 1, ST * len(spans) + 2
        kcols = [(u * BANK, min(BANK, KEYS - u * BANK)) for u in range(NKU)]

        with nc.Block() as block:
            @block.sync
            def _(sp):
                with sp.Fori(0, PAIRS) as i:
                    sp.wait_ge(projected, i * UNITS)
                    for w, w_d in zip(wqkv, (wq_d, wk_d, wv_d)):
                        sp.dma_start(w[:], w_d[ds(i, 1)].rearrange("o p k n -> p (o k) n")).then_inc(w_loaded, 16)
                    sp.wait_ge(mixed, i * 8)
                    sp.dma_start(wo[:], wo_d[ds(i, 1)].rearrange("o p n -> p (o n)")).then_inc(wo_loaded, 16)

            @block.tensor
            def _(pe):
                def project(i, u):
                    if u >= 4:
                        pe.wait_ge(unit_free, i * UNITS + (u - 3))
                    bank = m.PS[:, u % 4, :]
                    if u < NKU + NQU:
                        c0, n = kcols[u] if u < NKU else (LAT0 + (u - NKU) * BANK, BANK)
                        w = wqkv[1] if u < NKU else wqkv[0]
                        for k in range(DK):
                            last = nc.tensor.matmul(bank[:, 0:n], w[:, k, :], kvT[:, k, c0:c0 + n],
                                                    start=(k == 0), stop=(k == DK - 1))
                    else:
                        t0 = (u - NKU - NQU) * 4
                        for t in range(t0, min(t0 + 4, KT)):
                            for k in range(DK):
                                last = nc.tensor.matmul(bank[:, (t - t0) * P:(t - t0 + 1) * P],
                                                        kvT[:, k, t * P:(t + 1) * P], wqkv[2][:, k, :],
                                                        start=(k == 0), stop=(k == DK - 1))
                    last.then_inc(projected, 1)

                def norm(i, u):
                    if u == NKU:
                        pe.wait_ge(added, i * 8)
                    pe.wait_ge(squared, i * NORMS + (u + 1))
                    bank = 6 if u >= NKU else 5 + 2 * (u // 4)
                    g = 32 * (u % 4)
                    n = kcols[u][1] if u < NKU else BANK
                    for r in range(BANK // n):
                        last = nc.tensor.matmul(m.PS[g:g + 32, bank, r * n:(r + 1) * n], head_ones[:],
                                                squares[u % 2][:, 0:n], start=True, stop=True, tile_position=(0, g))
                    last.then_inc(normed, 1)

                def turn_peaks(i):
                    pe.wait_ge(peaked, i + 1)
                    for c in range(3):
                        last = nc.tensor.matmul(m.PS[0:1, 4, c * P:(c + 1) * P], peaks[:, c:c + 1], m.ident[:],
                                                start=True, stop=True)
                    last.then_inc(peaks_turned, 1)

                def score(i, n):
                    b, s = n // KT, n % KT
                    half, h = b // 2, b % 2
                    if n >= 2:
                        pe.wait_ge(exped, i * STEPS + (n - 1))
                    for c in range(2):
                        q0 = half * HALF + c * BANK
                        out = m.PS[:, 2 * (n % 2) + c, :]
                        nc.tensor.matmul(out, K1[h][:, s * P:(s + 1) * P], Q1[h][:, q0:q0 + BANK], start=True, stop=False)
                        last = nc.tensor.matmul(out, K2[h][:, s * P:(s + 1) * P], Q2[h][:, q0:q0 + BANK],
                                                start=False, stop=True)
                    last.then_inc(scored, 1)

                def apply(i, n):
                    b, s = n // KT, n % KT
                    if s == 0 and b >= 2:
                        pe.wait_ge(block_out, i * BLOCKS + (b - 1))
                    pe.wait_ge(exped, i * STEPS + (n + 1))
                    for c in range(2):
                        last = nc.tensor.matmul(m.PS[64 * c:64 * c + 64, 4 + b % 2, :], V[b % 2][:, s, :],
                                                probs[n % 3][:, c * BANK:(c + 1) * BANK],
                                                start=(s == 0), stop=(s == KT - 1))
                    last.then_inc(applied, 1)

                def total(i, b):
                    pe.wait_ge(summed, i * STEPS + (b + 1) * KT)
                    for c in range(2):
                        last = nc.tensor.matmul(m.PS[64 * c:64 * c + 64, 6 + b % 2, :], ones[:],
                                                prob_sums[b % 2][:, c * BANK:(c + 1) * BANK], start=True, stop=True)
                    last.then_inc(totalled, 1)

                with pe.Fori(0, PAIRS) as i:
                    pe.wait_ge(w_loaded, (i + 1) * 48)
                    for u in range(UNITS):
                        if u == UNITS - 1:
                            pe.wait_ge(bounded, i + 1)
                        project(i, u)
                        if 2 <= u < NORMS + 2:
                            norm(i, u - 2)
                        if u == UNITS - 4:
                            turn_peaks(i)
                    bits = pe.value_load(bound[0:1, 0:1].bitcast(int32))
                    pe.wait_ge(unit_free, (i + 1) * UNITS)
                    with pe.If(bits > SAFE_BITS):
                        for h in range(2):
                            score_maxima_pe(nc, m, pe, (Q1[h], Q2[h]), (K1[h], K2[h]), spans, negated,
                                            max_scored, max_reduced, (i * 2 + h) * MAX_REDUCED)
                    with pe.Else():
                        nc.tensor.matmul(m.PS[0:1, 4, 0:1], peaks[:, 0:1], m.ident[:, 0:1], start=True,
                                         stop=True).then_inc(max_scored, 2 * MAX_SCORED)
                    pe.wait_ge(max_reduced, (i + 1) * (2 * MAX_REDUCED))
                    score(i, 0)
                    for n in range(STEPS):
                        if n + 1 < STEPS:
                            score(i, n + 1)
                        apply(i, n)
                        if n % KT == 1 and n > KT:
                            total(i, n // KT - 1)
                    pe.wait_ge(wo_loaded, (i + 1) * 16)
                    for u in range(ST // 2):
                        if u == 2:
                            total(i, BLOCKS - 1)
                        if u == 0:
                            pe.wait_ge(block_out, i * BLOCKS + 3)
                        if u == 1:
                            pe.wait_ge(block_out, i * BLOCKS + 3)
                        if u == ST // 4:
                            pe.wait_ge(block_out, (i + 1) * BLOCKS)
                        if u >= 2:
                            pe.wait_ge(added, i * 8 + (u - 1))
                        for e in range(2):
                            t = 2 * u + e
                            last = nc.tensor.matmul(m.PS[:, 4 + 2 * (u % 2), e * D:(e + 1) * D],
                                                    heads_outT[:, t * P:(t + 1) * P], wo[:], start=True, stop=True)
                        last.then_inc(mixed, 1)

            @block.scalar
            def _(act):
                nc.scalar.preload_act_table(ACT.Exp)
                with act.Fori(0, PAIRS) as i:
                    for u in range(NKU + NQU):
                        act.wait_ge(projected, i * UNITS + (u + 1))
                        act.wait_ge(normed, i * NORMS + max(u - 1, 0))
                        n = kcols[u][1] if u < NKU else BANK
                        nc.scalar.activation(squares[u % 2][:, 0:n], m.PS[:, u % 4, 0:n], ACT.Square,
                                             scale=1.0 if u < NKU else SCALE).then_inc(squared, 1)
                        for h in range(2):
                            rows = slice(64 * h, 64 * h + 64)
                            if u < NKU:
                                c0, n = kcols[u]
                                last = nc.scalar.activation(K1[h][0:64, c0:c0 + n], m.PS[rows, u % 4, 0:n], ACT.Copy)
                            else:
                                c0 = (u - NKU) * BANK
                                for half in range(2):
                                    last = nc.scalar.activation(Q1[h][64 * half:64 * half + 64, c0:c0 + BANK],
                                                                m.PS[rows, u % 4, :], ACT.Copy, scale=SCALE)
                        last.then_inc(split_hi, 1)

                    for n in range(STEPS):
                        act.wait_ge(scored, i * STEPS + (n + 1))
                        if n >= 3:
                            act.wait_ge(applied, i * STEPS + (n - 2))
                            act.wait_ge(summed, i * STEPS + (n - 2))
                        b0 = 2 * (n % 2)
                        nc.scalar.activation(probs[n % 3][:], m.PS[:, b0:b0 + 2, :].rearrange("p b c -> p (b c)"),
                                             ACT.Exp).then_inc(exped, 1)

            @block.vector
            def _(dve):
                with dve.Fori(0, PAIRS) as i:
                    for u in range(UNITS):
                        if u < NKU + NQU:
                            dve.wait_ge(split_hi, i * (NKU + NQU) + (u + 1))
                        else:
                            dve.wait_ge(projected, i * UNITS + (u + 1))
                        for h in range(2):
                            rows = slice(64 * h, 64 * h + 64)
                            if u < NKU:
                                c0, n = kcols[u]
                                nc.vector.tensor_copy(K2[h][0:64, c0:c0 + n], K1[h][0:64, c0:c0 + n])
                                last = nc.vector.tensor_tensor(K1[h][64:128, c0:c0 + n], m.PS[rows, u % 4, 0:n],
                                                               K1[h][0:64, c0:c0 + n], ALU.subtract)
                            elif u < NKU + NQU:
                                c0 = (u - NKU) * BANK
                                last = nc.vector.scalar_tensor_tensor(
                                    out=Q2[h][0:64, c0:c0 + BANK], in0=m.PS[rows, u % 4, :], scalar=SCALE,
                                    in1=Q1[h][0:64, c0:c0 + BANK], op0=ALU.mult, op1=ALU.subtract)
                            else:
                                t0 = (u - NKU - NQU) * 4
                                n = min(4, KT - t0)
                                last = nc.vector.tensor_copy(
                                    V[h][:, t0:t0 + n, :],
                                    m.PS[:, u % 4, 0:n * P].rearrange("p (t c) -> p t c", c=P)[:, :, 64 * h:64 * h + 64])
                        if u == NORMS:
                            for h in range(2):
                                last = nc.vector.memset(Q2[h][MAX_ROW:MAX_ROW + 1, :], 0.0)
                        last.then_inc(unit_free, 1)
                        if u == NORMS + 2:
                            dve.wait_ge(normed, (i + 1) * NORMS)
                            nc.vector.tensor_reduce(peaks[:], m.PS[:, 5:8, :], AX.X, ALU.max).then_inc(peaked, 1)
                        if u == UNITS - 3:
                            dve.wait_ge(peaks_turned, i + 1)
                            nc.vector.tensor_reduce(top[:], m.PS[0:1, 4, 0:3 * P].rearrange("p (c n) -> p c n", n=P),
                                                    AX.X, ALU.max).then_inc(topped, 1)
                            dve.wait_ge(topped, i + 1)
                            nc.vector.scalar_tensor_tensor(out=bound[:], in0=top[:, 0:1], scalar=top[:, 2:3],
                                                           in1=top[:, 1:2], op0=ALU.max, op1=ALU.mult).then_inc(bounded, 1)
                    dve.wait_ge(rows_set, 2)
                    dve.wait_ge(bounded, i + 1)
                    bits = dve.value_load(bound[0:1, 0:1].bitcast(int32))
                    with dve.If(bits > SAFE_BITS):
                        for h in range(2):
                            score_maxima_dve(nc, m, dve, spans, partial, negated, Q2[h][MAX_ROW:MAX_ROW + 1, :],
                                             max_scored, max_reduced, (i * 2 + h) * MAX_SCORED, (i * 2 + h) * MAX_REDUCED)
                    with dve.Else():
                        nc.vector.memset(top[:], 0.0).then_inc(max_reduced, 2 * MAX_REDUCED)

                    def block_output(b):
                        half, h = b // 2, b % 2
                        dve.wait_ge(totalled, i * BLOCKS + (b + 1))
                        nc.vector.reciprocal(inverse[b % 2][:], m.PS[:, 6 + b % 2, :]).then_inc(inverted, 1)
                        dve.wait_ge(inverted, i * BLOCKS + (b + 1))
                        for c in range(2):
                            rows, q0 = slice(64 * c, 64 * c + 64), half * HALF + c * BANK
                            last = nc.vector.tensor_tensor(heads_outT[64 * h:64 * h + 64, q0:q0 + BANK],
                                                           m.PS[rows, 4 + b % 2, :], inverse[b % 2][rows, :], ALU.mult)
                        last.then_inc(block_out, 1)

                    for n in range(STEPS):
                        b, s = n // KT, n % KT
                        dve.wait_ge(exped, i * STEPS + (n + 1))
                        if s:
                            dve.wait_ge(summed, i * STEPS + n)
                        if s == 0:
                            nc.vector.tensor_copy(prob_sums[b % 2][:], probs[n % 3][:]).then_inc(summed, 1)
                        else:
                            nc.vector.tensor_tensor(prob_sums[b % 2][:], prob_sums[b % 2][:], probs[n % 3][:],
                                                    ALU.add).then_inc(summed, 1)
                        if s == 3 and b:
                            block_output(b - 1)
                    for u in range(ST // 2):
                        if u == 2:
                            block_output(BLOCKS - 1)
                        dve.wait_ge(mixed, i * 8 + (u + 1))
                        nc.vector.scalar_tensor_tensor(
                            out=m.X[:, 2 * u:2 * u + 2, :].rearrange("p t d -> p (t d)"), in0=m.PS[:, 4 + 2 * (u % 2), :],
                            scalar=m.gate[:, 0:1], in1=m.X[:, 2 * u:2 * u + 2, :].rearrange("p t d -> p (t d)"),
                            op0=ALU.mult, op1=ALU.add).then_inc(added, 1)


H = 1024
HT = H // P


def lora_ffn(nc, m, w1_d, b1_d, w2_d, b2_d, scale_d):
    with ExitStack() as own:
        sb = lambda n, s, d=fp32: own.enter_context(nc.sbuf_tensor(f"b_{n}", s, d))
        yT = sb("yT", [P, DK, S])
        W1T, W2T = sb("W1T", [P, DK, H]), sb("W2T", [P, HT, D])
        b1, b2, scale = sb("b1", [P, HT]), sb("b2", [P, 2, D]), sb("scale", [P, 1])
        layernorm_transposed(nc, m, "b_ln", m.X, yT, 0, 4)
        first, rows = sb("first", [P, D]), sb("rows", [1, 16, D])
        loaded, first_done, rows_in = m.sem("b_loaded"), m.sem("b_first"), m.sem("b_rows")
        outer, updated = m.sem("b_outer"), m.sem("b_updated")
        with nc.Block() as block:
            @block.sync
            def _(sp):
                sp.dma_start(W1T[:], w1_d).then_inc(loaded, 16)
                sp.dma_start(W2T[:], w2_d).then_inc(loaded, 16)
                sp.dma_start(b1[:], b1_d).then_inc(loaded, 16)
                sp.dma_start(b2[:], b2_d.partition_broadcast(P)).then_inc(loaded, 16)
                sp.dma_start(scale[:], scale_d.partition_broadcast(P)).then_inc(loaded, 16)
                sp.wait_ge(first_done, 1)
                sp.dma_start(rows[:], first[1:17, :]).then_inc(rows_in, 16)

            @block.vector
            def _(dve):
                nc.vector.tensor_scalar(first[:], m.X[:, 0, :], m.mean[:, 0:1], m.rstd[:, 0:1],
                                        ALU.subtract, ALU.mult).then_inc(first_done, 1)
                dve.wait_ge(loaded, 80)
                for u in range(8):
                    dve.wait_ge(outer, u + 1)
                    w = (W1T[:, u // 2, (u % 2) * BANK:(u % 2 + 1) * BANK] if u < 4 else
                         W2T[:, 2 * (u - 4):2 * (u - 4) + 2, :].rearrange("p t o -> p (t o)"))
                    nc.vector.scalar_tensor_tensor(out=w, in0=m.PS[:, u, :], scalar=scale[:], in1=w,
                                                   op0=ALU.mult, op1=ALU.add).then_inc(updated, 1)

            @block.tensor
            def _(pe):
                pe.wait_ge(rows_in, 16)
                for u in range(4):
                    k = u // 2
                    for e in range(2):
                        i = 2 * (u % 2) + e
                        last = nc.tensor.matmul(m.PS[:, u, e * D:(e + 1) * D], rows[:, 2 * i + 1, k * P:(k + 1) * P],
                                                rows[:, 2 * i, :], start=True, stop=True)
                    last.then_inc(outer, 1)
                for u in range(4):
                    for e in range(2):
                        r, half = divmod(2 * u + e, 2)
                        for i in range(4):
                            last = nc.tensor.matmul(
                                m.PS[:, 4 + u, e * D + 64 * i:e * D + 64 * i + 64],
                                rows[:, 2 * (i + 4) + 1, half * P:(half + 1) * P],
                                rows[:, 2 * (i + 4), :].rearrange("p (a r) -> p r a", r=4)[:, r, :],
                                start=True, stop=True)
                    last.then_inc(outer, 1)

        hidden = [sb(f"hidden{i}", [P, HT, BANK]) for i in range(2)]
        out_b = [sb(f"out{i}", [P, BANK]) for i in range(2)]
        CH = S // BANK
        up, acted, down, biased, added = (m.sem(f"b_{n}") for n in ("up", "acted", "down", "biased", "added"))
        with nc.Block() as block:
            @block.tensor
            def _(pe):
                with pe.Fori(0, CH // 2) as cc:
                    for e in range(2):
                        c = cc * 2 + e
                        for t in range(HT):
                            if t >= 4:
                                pe.wait_ge(acted, c * HT + (t - 3))
                            elif e:
                                pe.wait_ge(acted, c * HT + (t - 3))
                            for k in range(DK):
                                last = nc.tensor.matmul(m.PS[:, t % 4, :], W1T[:, k, t * P:(t + 1) * P],
                                                        yT[:, k, ds(c * BANK, BANK)], start=(k == 0), stop=(k == DK - 1))
                            last.then_inc(up, 1)
                        for u in range(2):
                            pe.wait_ge(acted, (c + 1) * HT)
                            pe.wait_ge(biased, c * 2)
                            for t in range(2):
                                for h in range(HT):
                                    last = nc.tensor.matmul(m.PS[:, 4 + u, t * D:(t + 1) * D],
                                                            hidden[e][:, h, (2 * u + t) * P:(2 * u + t + 1) * P],
                                                            W2T[:, h, :], start=(h == 0), stop=(h == HT - 1))
                            last.then_inc(down, 1)

            @block.scalar
            def _(act):
                nc.scalar.preload_act_table(ACT.Gelu)
                with act.Fori(0, CH // 2) as cc:
                    for e in range(2):
                        c = cc * 2 + e
                        for t in range(HT):
                            act.wait_ge(up, c * HT + (t + 1))
                            nc.scalar.activation(hidden[e][:, t, :], m.PS[:, t % 4, :], ACT.Gelu,
                                                 bias=b1[:, t:t + 1]).then_inc(acted, 1)

            @block.vector
            def _(dve):
                with dve.Fori(0, CH) as c:
                    for u in range(2):
                        dve.wait_ge(down, c * 2 + (u + 1))
                        dve.wait_ge(added, c * 2)
                        nc.vector.tensor_tensor(out_b[u][:], m.PS[:, 4 + u, :],
                                                b2[:].rearrange("p t d -> p (t d)"), ALU.add).then_inc(biased, 1)
                    for u in range(2):
                        dve.wait_ge(biased, c * 2 + (u + 1))
                        x = m.X[:, ds(c * 4 + 2 * u, 2), :].rearrange("p t d -> p (t d)")
                        nc.vector.scalar_tensor_tensor(out=x, in0=out_b[u][:], scalar=m.gate[:, 2:3], in1=x,
                                                       op0=ALU.mult, op1=ALU.add).then_inc(added, 1)


CH_HEADS, CH_D = 16, 16
GROUP = 4


def add_projected(nc, m, name, src, w, bias, gate):
    with ExitStack() as own:
        sb = lambda n, s, d=fp32: own.enter_context(nc.sbuf_tensor(f"{name}_{n}", s, d))
        srcT = sb("srcT", [P, DK, S])
        biased_sum = [sb(f"sum{i}", [P, BANK]) for i in range(2)]
        turned, moved, mixed, biased, added = (m.sem(f"{name}_{n}") for n in
                                               ("turned", "moved", "mixed", "biased", "added"))
        with nc.Block() as block:
            @block.tensor
            def _(pe):
                for g in range(ST // 4):
                    for k in range(DK):
                        for j in range(4):
                            last = nc.tensor.transpose(m.PS[:, 2 * g + k, j * P:(j + 1) * P],
                                                       src[:, 4 * g + j, k * P:(k + 1) * P], m.ident[:])
                        last.then_inc(turned, 1)
                for u in range(ST // 2):
                    if u % 2 == 0:
                        pe.wait_ge(moved, u + 2)
                    for t in (2 * u, 2 * u + 1):
                        for k in range(DK):
                            last = nc.tensor.matmul(m.PS[:, u // 2 * 2 + u % 2, (t % 2) * D:(t % 2 + 1) * D],
                                                    srcT[:, k, t * P:(t + 1) * P], w[:, k, :],
                                                    start=(k == 0), stop=(k == DK - 1))
                    last.then_inc(mixed, 1)

            @block.scalar
            def _(act):
                for g in range(ST // 4):
                    for k in range(DK):
                        act.wait_ge(turned, 2 * g + k + 1)
                        nc.scalar.activation(srcT[:, k, g * BANK:(g + 1) * BANK], m.PS[:, 2 * g + k, :],
                                             ACT.Copy).then_inc(moved, 1)

            @block.vector
            def _(dve):
                for u in range(ST // 2):
                    dve.wait_ge(mixed, u + 1)
                    if u >= 2:
                        dve.wait_ge(added, u - 1)
                    nc.vector.tensor_tensor(biased_sum[u % 2][:], m.PS[:, u, :], bias, ALU.add).then_inc(biased, 1)
                    dve.wait_ge(biased, u + 1)
                    x = m.X[:, 2 * u:2 * u + 2, :].rearrange("p t d -> p (t d)")
                    nc.vector.scalar_tensor_tensor(out=x, in0=biased_sum[u % 2][:], scalar=gate, in1=x,
                                                   op0=ALU.mult, op1=ALU.add).then_inc(added, 1)


def narrow_attention(nc, m, ctxT_d, wq_d, wk_d, wv_d, wo_d, bqk_d, bv_d, bo_d, q_parts, k_parts):
    SCALE = CH_D ** -0.5
    with ExitStack() as own:
        sb = lambda n, s, d=fp32: own.enter_context(nc.sbuf_tensor(f"c_{n}", s, d))
        wo, bo = sb("wo", [P, DK, D]), sb("bo", [P, 2, D])
        attended = sb("attended", [P, ST, D])
        bound = sb("bound", [1, 1])
        with ExitStack() as inner:
            si = lambda n, s, d=fp32: inner.enter_context(nc.sbuf_tensor(f"c_{n}", s, d))
            V = si("V", [P, CT, CH_HEADS, 32])
            xT = si("xT", [P, DK, S])
            layernorm_transposed(nc, m, "c_ln", m.X, xT, 0, 4)
            with ExitStack() as proj:
                sp_ = lambda n, s, d=fp32: proj.enter_context(nc.sbuf_tensor(f"c_{n}", s, d))
                cT = sp_("cT", [P, DK, CTX])
                w = [sp_(f"w{n}", [P, DK, D]) for n in "qkv"]
                bqk, bv = sp_("bqk", [P, 2, 2]), sp_("bv", [P, D])
                full = [sp_("q", [P, 2, S]), sp_("k", [P, 2, CTX])]
                hi = [sp_("qh", [P, 2, S], fp16), sp_("kh", [P, 2, CTX], fp16)]
                lo = [sp_("ql", [P, 2, S], fp16), sp_("kl", [P, 2, CTX], fp16)]
                loaded, kept = m.sem("c_loaded"), m.sem("c_kept")
                projected, acted, split_hi, used = (m.sem(f"c_{n}") for n in ("projected", "acted", "hi", "used"))
                vcleared = m.sem("c_vcleared")
                units = [(qk, j, c0, min(BANK, n - c0)) for qk, n in ((1, CTX), (0, S)) for j in range(2)
                         for c0 in range(0, n, BANK)]
                NU = len(units)
                NV = -(-CT // 2)
                RING = 6
                squares = [sp_("q_squares", [P, 2, S], bf16), sp_("k_squares", [P, 2, CTX], bf16)]
                head_ones = sp_("head_ones", [P, 2, 32], bf16)
                peaks, top = sp_("peaks", [P, 2]), sp_("top", [1, 2])
                squared, normed, peaked, peaks_turned, topped = (
                    m.sem(f"c_{n}") for n in ("squared", "lengths", "peaked", "peaks_turned", "topped"))
                ones_set = m.sem("c_ones_set")
                with nc.Block() as block:
                    @block.sync
                    def _(sp):
                        sp.dma_start(cT[:], ctxT_d).then_inc(loaded, 16)
                        for w_sb, w_dram in zip(w, (wq_d, wk_d, wv_d)):
                            sp.dma_start(w_sb[:], w_dram).then_inc(loaded, 16)
                        sp.dma_start(wo[:], wo_d).then_inc(loaded, 16)
                        sp.dma_start(bqk[:], bqk_d).then_inc(loaded, 16)
                        sp.dma_start(bv[:], bv_d.partition_broadcast(P)).then_inc(loaded, 16)
                        sp.dma_start(bo[:], bo_d.partition_broadcast(P)).then_inc(loaded, 16)
                        for qk, n_used in ((1, NU // 2), (0, NU)):
                            sp.wait_ge(used, n_used)
                            parts = k_parts if qk else q_parts
                            sp.dma_start(parts[0], hi[qk][:]).then_inc(kept, 16)
                            sp.dma_start(parts[1], lo[qk][:]).then_inc(kept, 16)
                        sp.wait_ge(kept, 64)

                    @block.tensor
                    def _(pe):
                        pe.wait_ge(loaded, 128)
                        for u, (qk, j, c0, n) in enumerate(units):
                            if u >= RING:
                                pe.wait_ge(acted, u - RING + 1)
                            src = cT if qk else xT
                            for k in range(DK):
                                last = nc.tensor.matmul(m.PS[:, u % RING, 0:n], w[qk][:, k, j * P:(j + 1) * P],
                                                        src[:, k, c0:c0 + n], start=(k == 0), stop=(k == DK - 1))
                            last.then_inc(projected, 1)
                        for v in range(NV):
                            u = NU + v
                            pe.wait_ge(acted, min(u - RING + 1, NU))
                            if u - RING >= NU:
                                pe.wait_ge(used, u - RING + 1)
                            if v == 2:
                                pe.wait_ge(ones_set, 1)
                                pe.wait_ge(squared, NU)
                                for qk, n in ((1, CTX), (0, S)):
                                    for c in range(4):
                                        c0 = min(c * BANK, n - BANK)
                                        for j in range(2):
                                            last = nc.tensor.matmul(
                                                m.PS[32 * c:32 * c + 32, 7 - qk, :], head_ones[:, j, :],
                                                squares[qk][:, j, c0:c0 + BANK], start=(j == 0), stop=(j == 1),
                                                tile_position=(0, 32 * c))
                                last.then_inc(normed, 1)
                            for t in range(2 * v, min(2 * v + 2, CT)):
                                rows = P if t < CT - 1 else CLAST
                                for k in range(DK):
                                    last = nc.tensor.matmul(m.PS[0:rows, u % RING, (t % 2) * D:(t % 2 + 1) * D],
                                                            cT[:, k, t * P:t * P + rows], w[2][:, k, :],
                                                            start=(k == 0), stop=(k == DK - 1))
                            last.then_inc(projected, 1)
                        pe.wait_ge(peaked, 1)
                        for c in range(2):
                            last = nc.tensor.matmul(m.PS[0:1, 6, c * P:(c + 1) * P], peaks[:, c:c + 1], m.ident[:],
                                                    start=True, stop=True)
                        last.then_inc(peaks_turned, 1)

                    @block.scalar
                    def _(act):
                        act.wait_ge(loaded, 128)
                        for u, (qk, j, c0, n) in enumerate(units):
                            act.wait_ge(projected, u + 1)
                            if u == NU // 2:
                                act.wait_ge(vcleared, 3)
                            for dst, func, sem in ((squares, ACT.Square, squared), (full, ACT.Identity, acted)):
                                nc.scalar.activation(dst[qk][:, j, c0:c0 + n], m.PS[:, u % RING, 0:n], func,
                                                     bias=bqk[:, qk, j:j + 1], scale=1.0 if qk else SCALE).then_inc(sem, 1)

                    @block.vector
                    def _(dve):
                        nc.vector.memset(V[:], 0.0)
                        nc.vector.memset(head_ones[:], 0.0).then_inc(vcleared, 1)
                        dve.wait_ge(vcleared, 1)
                        nc.vector.memset(V[:, :, :, CH_D:CH_D + 1], 1.0).then_inc(vcleared, 1)
                        for j in range(2):
                            last = nc.vector.tensor_reduce(head_ones[:, j, 8 * j:8 * j + 8],
                                                           m.ident[:].rearrange("p (h d) -> p h d", d=CH_D), AX.X, ALU.max)
                        last.then_inc(ones_set, 1)
                        dve.wait_ge(loaded, 128)
                        nc.vector.tensor_scalar(bqk[:, 0, :], bqk[:, 0, :], SCALE, None, ALU.mult).then_inc(vcleared, 1)
                        for u, (qk, j, c0, n) in enumerate(units):
                            cols = slice(c0, c0 + n)
                            dve.wait_ge(acted, u + 1)
                            nc.vector.tensor_copy(hi[qk][:, j, cols], full[qk][:, j, cols]).then_inc(split_hi, 1)
                            dve.wait_ge(split_hi, u + 1)
                            nc.vector.tensor_tensor(lo[qk][:, j, cols], full[qk][:, j, cols], hi[qk][:, j, cols],
                                                    ALU.subtract).then_inc(used, 1)
                        for v in range(NV):
                            dve.wait_ge(projected, NU + v + 1)
                            for t in range(2 * v, min(2 * v + 2, CT)):
                                rows = P if t < CT - 1 else CLAST
                                ps = m.PS[0:rows, (NU + v) % RING, (t % 2) * D:(t % 2 + 1) * D]
                                last = nc.vector.tensor_tensor(
                                    V[0:rows, t, :, 0:CH_D], ps.rearrange("p (h d) -> p h d", d=CH_D),
                                    bv[0:rows, :].rearrange("p (h d) -> p h d", d=CH_D), ALU.add)
                            last.then_inc(used, 1)
                        dve.wait_ge(normed, 1)
                        nc.vector.tensor_reduce(peaks[:], m.PS[:, 6:8, :], AX.X, ALU.max).then_inc(peaked, 1)
                        dve.wait_ge(peaks_turned, 1)
                        nc.vector.tensor_reduce(top[:], m.PS[0:1, 6, 0:2 * P].rearrange("p (c n) -> p c n", n=P),
                                                AX.X, ALU.max).then_inc(topped, 1)
                        dve.wait_ge(topped, 1)
                        nc.vector.tensor_tensor(bound[:], top[:, 0:1], top[:, 1:2], ALU.mult)

            Kop = [si(f"Kop{i}", [P, CTX], fp16) for i in range(2)]
            Qop = [si(f"Qop{i}", [P, S], fp16) for i in range(2)]
            Vh = [si(f"Vh{i}", [P, CT, 32]) for i in range(2)]
            probs = [si(f"probs{i}", [P, 2 * BANK]) for i in range(4)]
            outT = [si(f"outT{i}", [P, BANK]) for i in range(2)]
            inverse = [si(f"inverse{i}", [P, 4, 4]) for i in range(2)]
            TILES = 2 * CT
            partial, negated = si("partial", [P, 1, 2, ST]), si("negated", [P, ST])
            spans = [(0, CTX)]
            MAX_SCORED, MAX_REDUCED = ST * len(spans) + 1, ST * len(spans) + 2
            row_cleared, max_scored, max_reduced = (m.sem(f"c_{n}") for n in ("row_cleared", "max_scored", "max_reduced"))
            rows_set, rows_cleared = m.sem("c_rows_set"), m.sem("c_rows_cleared")
            ops_in = [m.sem(f"c_ops_in{i}") for i in range(2)]
            scored, exped, applied, copied = (m.sem(f"c_{n}") for n in ("scored", "exped", "applied", "copied"))
            turned, inverted, normed, values_in = (m.sem(f"c_{n}") for n in ("turned", "inverted", "normed", "values_in"))
            krows = lambda t: P if t % CT < CT - 1 else CLAST
            with nc.Block() as block:
                @block.sync
                def _(sp):
                    sp.wait_ge(rows_set, 2)
                    for h in range(CH_HEADS):
                        if h >= 2:
                            sp.wait_ge(applied, (h - 1) * CT)
                        row = 16 * (h % 8)
                        for op, parts, order in ((Kop[h % 2], k_parts, (0, 1, 0, 1)), (Qop[h % 2], q_parts, (0, 0, 1, 1))):
                            for r, part in enumerate(order):
                                sp.dma_start(op[16 * r:16 * r + 16, :],
                                             parts[part][row:row + 16, h // 8, :]).then_inc(ops_in[h % 2], 16)

                @block.gpsimd
                def _(pool):
                    for e in range(2):
                        for op in (Kop[e], Qop[e]):
                            nc.gpsimd.memset(op[MAX_ROW:P, :], 0.0).then_inc(rows_cleared, 1)
                    pool.wait_ge(rows_cleared, 4)
                    nc.gpsimd.memset(Kop[0][MAX_ROW:MAX_ROW + 1, :], 1.0).then_inc(rows_set, 1)
                    pool.wait_ge(rows_set, 1)
                    nc.gpsimd.memset(Kop[1][MAX_ROW:MAX_ROW + 1, :], 1.0).then_inc(rows_set, 1)

                @block.tensor
                def _(pe):
                    bits = pe.value_load(bound[0:1, 0:1].bitcast(int32))
                    with pe.Fori(0, CH_HEADS // 2) as i:
                        def score(t):
                            e, r, c0 = t // CT, krows(t), t % CT * P
                            if t % CT == 0:
                                pe.wait_ge(ops_in[e], (i + 1) * (8 * 16))
                            for hp in range(2):
                                if t:
                                    pe.wait_ge(exped, i * (2 * TILES) + (2 * t + hp - 1))
                                for b in range(2):
                                    q0 = (2 * hp + b) * BANK
                                    last = nc.tensor.matmul(m.PS[0:r, 2 * hp + b, :], Kop[e][:, c0:c0 + r],
                                                            Qop[e][:, q0:q0 + BANK], start=True, stop=True)
                                last.then_inc(scored, 1)

                        def apply(t):
                            e, r = t // CT, krows(t)
                            if t % CT == 0:
                                pe.wait_ge(values_in, i * 2 + (e + 1))
                            pe.wait_ge(exped, i * (2 * TILES) + (2 * t + 2))
                            for q in range(4):
                                last = nc.tensor.matmul(m.PS[32 * q:32 * q + 32, 4 + e, :], Vh[e][0:r, t % CT, :],
                                                        probs[2 * (t % 2) + q // 2][0:r, (q % 2) * BANK:(q % 2 + 1) * BANK],
                                                        start=(t % CT == 0), stop=(t % CT == CT - 1),
                                                        tile_position=(0, 32 * q))
                            last.then_inc(applied, 1)

                        def turn(e):
                            pe.wait_ge(copied, i * 2 + (e + 1))
                            for j in range(4):
                                last = nc.tensor.transpose(m.PS[:, 6 + e, j * P:(j + 1) * P], outT[e][:, j * P:(j + 1) * P],
                                                           m.ident[:])
                            last.then_inc(turned, 1)

                        with pe.If(bits > SAFE_BITS):
                            for e in range(2):
                                score_maxima_pe(nc, m, pe, (Qop[e],), (Kop[e],), spans, negated, max_scored, max_reduced,
                                                (i * 2 + e) * MAX_REDUCED,
                                                ready=((row_cleared, i + 1), (exped, i * (2 * TILES)),
                                                       (ops_in[e], (i + 1) * (8 * 16))))
                            pe.wait_ge(max_reduced, (i + 1) * (2 * MAX_REDUCED))
                        score(0)
                        for t in range(TILES):
                            if t + 1 < TILES:
                                score(t + 1)
                            apply(t)
                            if t == CT + 1:
                                turn(0)
                        turn(1)

                @block.scalar
                def _(act):
                    nc.scalar.preload_act_table(ACT.Exp)
                    with act.Fori(0, CH_HEADS // 2) as i:
                        for n in range(2 * TILES):
                            t, hp = n // 2, n % 2
                            act.wait_ge(scored, i * (2 * TILES) + (n + 1))
                            act.wait_ge(applied, i * TILES + max(t - 1, 0))
                            r = krows(t)
                            nc.scalar.activation(probs[2 * (t % 2) + hp][0:r, :],
                                                 m.PS[0:r, 2 * hp:2 * hp + 2, :].rearrange("p b c -> p (b c)"),
                                                 ACT.Exp).then_inc(exped, 1)

                @block.vector
                def _(dve):
                    bits = dve.value_load(bound[0:1, 0:1].bitcast(int32))
                    with dve.Fori(0, CH_HEADS // 2) as i:
                        def place_values(e):
                            nc.vector.tensor_copy(Vh[e][:], V[:, :, ds(i * 2 + e, 1), :].rearrange("p t o c -> p (t o) c")
                                                  ).then_inc(values_in, 1)

                        def output(e):
                            dve.wait_ge(applied, i * TILES + (e + 1) * CT)
                            nc.vector.tensor_copy(outT[e][:], m.PS[:, 4 + e, :]).then_inc(copied, 1)
                            dve.wait_ge(turned, i * 2 + (e + 1))
                            out = m.PS[:, 6 + e, :].rearrange("p (j q d) -> p j q d", q=4, d=32)
                            nc.vector.reciprocal(inverse[e][:], out[:, :, :, CH_D]).then_inc(inverted, 1)
                            dve.wait_ge(inverted, i * 2 + (e + 1))
                            dst = attended[:, :, ds((i * 2 + e) * CH_D, CH_D)].rearrange("p (q j) d -> p j q d", q=4)
                            nc.vector.tensor_tensor(dst, out[:, :, :, 0:CH_D],
                                                    inverse[e][:].unsqueeze(3).to_broadcast([P, 4, 4, CH_D]),
                                                    ALU.mult).then_inc(normed, 1)

                        with dve.If(bits > SAFE_BITS):
                            dve.wait_ge(rows_set, 2)
                            for e in range(2):
                                last = nc.vector.memset(Qop[e][MAX_ROW:MAX_ROW + 1, :], 0.0)
                            last.then_inc(row_cleared, 1)
                            for e in range(2):
                                score_maxima_dve(nc, m, dve, spans, partial, negated, Qop[e][MAX_ROW:MAX_ROW + 1, :],
                                                 max_scored, max_reduced, (i * 2 + e) * MAX_SCORED, (i * 2 + e) * MAX_REDUCED)
                        for e in range(2):
                            place_values(e)
                        for e in range(2):
                            output(e)
                        dve.wait_ge(normed, i * 2 + 2)

        add_projected(nc, m, "c_out", attended, wo, bo[:].rearrange("p t d -> p (t d)"), m.gate[:, 1:2])


LH, LD = 8, 64
INNER = LH * LD
HID = 682
GT = -(-HID // P)
DEPTH = 2


def local_layer(nc, m, name, Z, t, w):
    with ExitStack() as own:
        sb = lambda n, s, d=fp32: own.enter_context(nc.sbuf_tensor(f"{name}_{n}", s, d))
        with ExitStack() as attn:
            sa = lambda n, s, d=fp32: attn.enter_context(nc.sbuf_tensor(f"{name}_{n}", s, d))
            kT = sa("kT", [P, 4, S + P])
            V = sa("V", [P, ST + 1, LH, LD + 1])
            qT = sa("qT", [P, 4, S])
            with ExitStack() as first:
                sf = lambda n, s, d=fp32: first.enter_context(nc.sbuf_tensor(f"{name}_{n}", s, d))
                zT = sf("zT", [P, DK, S + 1])
                wqkv = sf("wqkv", [P, DK, 3 * INNER])
                tables = sf("tables", [P, 2, ST, 2, LD])
                scales = sf("scales", [P, 2, 2, LD])
                loaded, turned, moved = m.sem(f"layer_loaded"), m.sem(f"layer_turned"), m.sem(f"layer_moved")
                cleared, scaled = m.sem(f"layer_cleared"), m.sem(f"layer_scaled")
                with nc.Block() as block:
                    @block.sync
                    def _(sp):
                        sp.dma_start(wqkv[:], w["wqkv"]).then_inc(loaded, 16)
                        sp.dma_start(tables[:], t["rotary"]).then_inc(loaded, 16)
                        sp.dma_start(scales[:], w["scales"].partition_broadcast(P)).then_inc(loaded, 16)
                        sp.wait_ge(loaded, 48)

                    @block.tensor
                    def _(pe):
                        for g in range(ST // 4):
                            for k in range(DK):
                                for j in range(4):
                                    last = nc.tensor.transpose(m.PS[:, 2 * g + k, j * P:(j + 1) * P],
                                                               Z[:, 4 * g + j, k * P:(k + 1) * P], m.ident[:])
                                last.then_inc(turned, 1)

                    @block.scalar
                    def _(act):
                        act.wait_ge(cleared, 1)
                        for g in range(ST // 4):
                            for k in range(DK):
                                act.wait_ge(turned, 2 * g + k + 1)
                                nc.scalar.activation(zT[:, k, g * BANK + k:(g + 1) * BANK + k], m.PS[:, 2 * g + k, :],
                                                     ACT.Copy).then_inc(moved, 1)

                    @block.gpsimd
                    def _(pool):
                        nc.gpsimd.memset(V[:, 0, :, :], 0.0)
                        nc.gpsimd.memset(V[:, 1:ST + 1, :, LD:LD + 1], 1.0)

                    @block.vector
                    def _(dve):
                        nc.vector.memset(zT[:, 1, 0:1], 0.0).then_inc(cleared, 1)
                        nc.vector.memset(kT[:, :, 0:P], 0.0)
                        dve.wait_ge(loaded, 48)
                        for half in range(2):
                            for qk in range(2):
                                x = tables[:, half, :, qk, :]
                                nc.vector.tensor_tensor(
                                    x, x, scales[:, half, qk, :].unsqueeze(1).to_broadcast([P, ST, LD]), ALU.mult)

                window = [sf(f"window{i}", [P, DK, P]) for i in range(2)]
                squares, unit = sf("squares", [P, 16, LD]), sf("unit", [P, 2, LH, 2, LD // 2])
                straight, crossed = sf("straight", [P, 2, LH, LD]), sf("crossed", [P, 2, LH, 2, LD // 2])
                rotated = [sf(f"rotated{i}", [P, 2 * INNER]) for i in range(2)]
                norms = sf("norms", [P, 4, 16])
                (windowed, projected, squared, valued, summed, rooted, united, crossed_done, rotated_done, step,
                 turned2, moved2) = (m.sem(f"layer_p_{n}") for n in (
                     "windowed", "projected", "squared", "valued", "summed", "rooted", "united", "crossed", "rotated",
                     "step", "turned", "moved"))
                straightened = m.sem(f"layer_p_straightened")
                with nc.Block() as block:
                    @block.tensor
                    def _(pe):
                        def project(wi, e):
                            pe.wait_ge(windowed, wi + 1)
                            for c in range(3):
                                for k in range(DK):
                                    last = nc.tensor.matmul(m.PS[:, 3 * e + c, :], window[e][:, k, :],
                                                            wqkv[:, k, c * BANK:(c + 1) * BANK],
                                                            start=(k == 0), stop=(k == DK - 1))
                            last.then_inc(projected, 1)

                        def turn(wi, e):
                            pe.wait_ge(rotated_done, wi + 1)
                            pe.wait_ge(moved2, wi)
                            for c in range(8):
                                last = nc.tensor.transpose(m.PS[:, 6 + c // 4, (c % 4) * P:(c % 4 + 1) * P],
                                                           rotated[e][:, c * P:(c + 1) * P], m.ident[:])
                            last.then_inc(turned2, 1)

                        project(0, 0)
                        with pe.Fori(0, ST // 2 - 1) as j:
                            for e in (1, 0):
                                wi = j * 2 + (1 if e else 2)
                                project(wi, e)
                                turn(wi - 1, 1 - e)
                        project(ST - 1, 1)
                        turn(ST - 2, 0)
                        turn(ST - 1, 1)

                    @block.scalar
                    def _(act):
                        nc.scalar.preload_act_table(ACT.Sqrt)

                        def values(wi, e):
                            act.wait_ge(projected, wi + 1)
                            nc.scalar.activation(squares[:].rearrange("p h d -> p (h d)"),
                                                 m.PS[:, 3 * e:3 * e + 2, :].rearrange("p b c -> p (b c)"),
                                                 ACT.Square).then_inc(squared, 1)
                            nc.scalar.activation(V[:, ds(wi + 1, 1), :, 0:LD].rearrange("p o h d -> p (o h) d"),
                                                 m.PS[:, 3 * e + 2, :].rearrange("p (h d) -> p h d", d=LD),
                                                 ACT.Copy).then_inc(valued, 1)
                            act.wait_ge(summed, wi + 1)
                            nc.scalar.activation(norms[:, 1, :], norms[:, 0, :], ACT.Sqrt).then_inc(rooted, 1)

                        def move(wi):
                            act.wait_ge(turned2, wi + 1)
                            nc.scalar.activation(qT[:, :, ds(wi * P, P)], m.PS[:, 6, :].rearrange("p (c n) -> p c n", n=P),
                                                 ACT.Copy)
                            nc.scalar.activation(kT[:, :, ds(wi * P + P, P)], m.PS[:, 7, :].rearrange("p (c n) -> p c n", n=P),
                                                 ACT.Copy).then_inc(moved2, 1)

                        values(0, 0)
                        with act.Fori(0, ST // 2 - 1) as j:
                            for e in (1, 0):
                                wi = j * 2 + (1 if e else 2)
                                values(wi, e)
                                move(wi - 1)
                        values(ST - 1, 1)
                        move(ST - 2)
                        move(ST - 1)

                    @block.vector
                    def _(dve):
                        def window_in(wi, e):
                            nc.vector.tensor_copy(window[e][:], zT[:, :, ds(wi * P, P)]).then_inc(windowed, 1)

                        def rotate(wi, e, more=True):
                            dve.wait_ge(squared, wi + 1)
                            nc.vector.tensor_reduce(norms[:, 0, :], squares[:], AX.X, ALU.add).then_inc(summed, 1)
                            dve.wait_ge(rooted, wi + 1)
                            nc.vector.tensor_scalar(norms[:, 2, :], norms[:, 1, :], 1e-12, None, ALU.max).then_inc(step, 1)
                            dve.wait_ge(step, wi * 2 + 1)
                            nc.vector.reciprocal(norms[:, 3, :], norms[:, 2, :]).then_inc(step, 1)
                            dve.wait_ge(step, wi * 2 + 2)
                            nc.vector.tensor_tensor(
                                unit[:].rearrange("p q h a d -> p (q h) (a d)"),
                                m.PS[:, 3 * e:3 * e + 2, :].rearrange("p b (h d) -> p (b h) d", d=LD),
                                norms[:, 3, :].unsqueeze(2).to_broadcast([P, 16, LD]), ALU.mult).then_inc(united, 1)
                            if more:
                                dve.wait_ge(valued, wi + 1)
                                window_in(wi + 2, e)
                            dve.wait_ge(rotated_done, wi)
                            dve.wait_ge(united, wi + 1)
                            for qk in range(2):
                                last = nc.vector.tensor_tensor(
                                    straight[:, qk], unit[:, qk].rearrange("p h a d -> p h (a d)"),
                                    tables[:, 0, ds(wi, 1), qk, :].to_broadcast([P, LH, LD]), ALU.mult)
                            last.then_inc(straightened, 1)
                            dve.wait_ge(straightened, wi + 1)
                            dve.wait_ge(crossed_done, wi + 1)
                            dve.wait_ge(turned2, max(wi - 1, 0) if type(wi) is int else wi - 1)
                            nc.vector.tensor_tensor(rotated[e][:], straight[:].rearrange("p q h d -> p (q h d)"),
                                                    crossed[:].rearrange("p q h a d -> p (q h a d)"),
                                                    ALU.add).then_inc(rotated_done, 1)

                        window_in(0, 0)
                        window_in(1, 1)
                        rotate(0, 0)
                        with dve.Fori(0, ST // 2 - 2) as j:
                            for e in (1, 0):
                                rotate(j * 2 + (1 if e else 2), e)
                        rotate(ST - 3, 1)
                        rotate(ST - 2, 0, more=False)
                        rotate(ST - 1, 1, more=False)

                    @block.gpsimd
                    def _(pool):
                        for wi in range(ST):
                            pool.wait_ge(united, wi + 1)
                            for qk in range(2):
                                for a in range(2):
                                    last = nc.gpsimd.tensor_tensor(
                                        crossed[:, qk, :, a, :], unit[:, qk, :, 1 - a, :],
                                        tables[:, 1, wi, qk, a * 32:a * 32 + 32].unsqueeze(1).to_broadcast([P, LH, LD // 2]),
                                        ALU.mult)
                            last.then_inc(crossed_done, 1)

            masks = sa("masks", [P, ST, 2 * P])
            wo = sa("wo", [P, 4, D])
            qstat = sa("qstat", [P, LH, P])
            scores, probs = sa("scores", [P, LH, 2 * P]), sa("probs", [P, LH, 2 * P])
            probsT = sa("probsT", [P, LH, 2, P])
            minus_max, inverse = sa("minus_max", [P, LH]), sa("inverse", [P, LH])
            heads_out, heads_outT = sa("heads_out", [P, INNER]), sa("heads_outT", [P, 4, P])
            (wloaded, qcleared, queried, scored, masked, maxed, exped, turned3, moved3, applied, inverted, normed,
             turned4, moved4, mixed, added) = (m.sem(f"layer_a_{n}") for n in (
                 "loaded", "qcleared", "queried", "scored", "masked", "maxed", "exped", "turned", "moved", "applied",
                 "inverted", "normed", "oturned", "omoved", "mixed", "added"))
            with nc.Block() as block:
                @block.sync
                def _(sp):
                    sp.dma_start(masks[:], t["masks"]).then_inc(wloaded, 16)
                    sp.dma_start(wo[:], w["wo"]).then_inc(wloaded, 16)
                    sp.wait_ge(wloaded, 32)

                @block.tensor
                def _(pe):
                    def score(wi):
                        pe.wait_ge(queried, wi + 1)
                        pe.wait_ge(masked, wi)
                        for h in range(LH):
                            last = nc.tensor.matmul(m.PS[:, h // 2, (h % 2) * D:(h % 2 + 1) * D], qstat[:, h, :],
                                                    kT[:, h // 2, ds(wi * P, 2 * P)], start=True, stop=True)
                        last.then_inc(scored, 1)

                    def finish_window(wi):
                        pe.wait_ge(exped, wi + 1)
                        pe.wait_ge(added, wi)
                        for h in range(LH):
                            for kt in range(2):
                                last = nc.tensor.transpose(
                                    m.PS[:, 4 + h // 2, (h % 2 * 2 + kt) * P:(h % 2 * 2 + kt + 1) * P],
                                    probs[:, h, kt * P:(kt + 1) * P], m.ident[:])
                            if h % 4 == 3:
                                last.then_inc(turned3, 1)
                        for c in range(2):
                            pe.wait_ge(moved3, wi * 2 + (c + 1))
                            for h in range(4 * c, 4 * c + 4):
                                for kt in range(2):
                                    last = nc.tensor.matmul(
                                        m.PS[:, 4 + c, (h % 4) * (LD + 1):(h % 4 + 1) * (LD + 1)], probsT[:, h, kt, :],
                                        V[:, ds(wi + kt, 1), h, :].rearrange("p o d -> p (o d)"),
                                        start=(kt == 0), stop=(kt == 1))
                        last.then_inc(applied, 1)
                        pe.wait_ge(normed, wi + 1)
                        for c in range(4):
                            last = nc.tensor.transpose(m.PS[:, 6, c * P:(c + 1) * P], heads_out[:, c * P:(c + 1) * P], m.ident[:])
                        last.then_inc(turned4, 1)
                        pe.wait_ge(moved4, wi + 1)
                        for c in range(4):
                            last = nc.tensor.matmul(m.PS[:, 7, 0:D], heads_outT[:, c, :], wo[:, c, :],
                                                    start=(c == 0), stop=(c == 3))
                        last.then_inc(mixed, 1)

                    pe.wait_ge(wloaded, 32)
                    score(0)
                    with pe.Fori(0, ST - 1) as wi:
                        score(wi + 1)
                        finish_window(wi)
                    finish_window(ST - 1)

                @block.scalar
                def _(act):
                    nc.scalar.preload_act_table(ACT.Exp)

                    def expo(wi):
                        act.wait_ge(maxed, wi + 1)
                        for h in range(LH):
                            last = nc.scalar.activation(probs[:, h, :], scores[:, h, :], ACT.Exp, bias=minus_max[:, h:h + 1])
                        last.then_inc(exped, 1)

                    def move(wi):
                        for c in range(2):
                            act.wait_ge(turned3, wi * 2 + (c + 1))
                            nc.scalar.activation(probsT[:, 4 * c:4 * c + 4].rearrange("p h k n -> p (h k n)"),
                                                 m.PS[:, 4 + 2 * c:6 + 2 * c, :].rearrange("p b n -> p (b n)"),
                                                 ACT.Copy).then_inc(moved3, 1)

                    expo(0)
                    with act.Fori(0, ST - 1) as wi:
                        move(wi)
                        expo(wi + 1)
                    move(ST - 1)

                @block.vector
                def _(dve):
                    nc.vector.memset(qstat[:], 0.0).then_inc(qcleared, 1)
                    dve.wait_ge(qcleared, 1)
                    dve.wait_ge(wloaded, 32)

                    def queries(wi):
                        for e in range(2):
                            rows = slice(64 * e, 64 * e + 64)
                            last = nc.vector.tensor_copy(
                                qstat[rows].rearrange("p (c e) n -> p c e n", e=2)[:, :, e, :], qT[rows, :, ds(wi * P, P)])
                        last.then_inc(queried, 1)

                    def mask(wi):
                        dve.wait_ge(scored, wi + 1)
                        dve.wait_ge(exped, wi)
                        nc.vector.tensor_tensor(scores[:], m.PS[:, 0:4, :].rearrange("p b (e n) -> p (b e) n", e=2),
                                                masks[:, ds(wi, 1), :].to_broadcast([P, LH, 2 * P]),
                                                ALU.add).then_inc(masked, 1)
                        dve.wait_ge(masked, wi + 1)
                        nc.vector.tensor_reduce(minus_max[:], scores[:], AX.X, ALU.max, negate=True).then_inc(maxed, 1)

                    def output(wi):
                        dve.wait_ge(applied, wi + 1)
                        acc = m.PS[:, 4:6, 0:4 * (LD + 1)].rearrange("p b (h d) -> p b h d", d=LD + 1)
                        nc.vector.reciprocal(inverse[:].rearrange("p (b h) -> p b h", b=2), acc[:, :, :, LD]).then_inc(inverted, 1)
                        dve.wait_ge(inverted, wi + 1)
                        for c in range(2):
                            last = nc.vector.tensor_tensor(
                                heads_out[:, c * D:(c + 1) * D].rearrange("p (h d) -> p h d", d=LD), acc[:, c, :, 0:LD],
                                inverse[:, 4 * c:4 * c + 4].unsqueeze(2).to_broadcast([P, 4, LD]), ALU.mult)
                        last.then_inc(normed, 1)
                        dve.wait_ge(turned4, wi + 1)
                        nc.vector.tensor_copy(heads_outT[:].rearrange("p c n -> p (c n)"), m.PS[:, 6, :]).then_inc(moved4, 1)
                        dve.wait_ge(mixed, wi + 1)
                        z = Z[:, ds(wi, 1), :].rearrange("p o d -> p (o d)")
                        nc.vector.tensor_tensor(z, z, m.PS[:, 7, 0:D], ALU.add).then_inc(added, 1)

                    queries(0)
                    mask(0)
                    queries(1)
                    with dve.Fori(0, ST - 2) as wi:
                        mask(wi + 1)
                        queries(wi + 2)
                        output(wi)
                    mask(ST - 1)
                    output(ST - 2)
                    output(ST - 1)

        shifted, hT = sb("shifted", [P, ST, D]), sb("hT", [P, DK, S])
        w1, w2 = sb("w1", [P, DK, 2, GT, P]), sb("w2", [P, GT, D])
        b1, b2, aff = sb("b1", [P, 2, GT]), sb("b2", [P, 2, D]), sb("aff", [P, 2, DK])
        moved, zeroed = m.sem(f"layer_shifted"), m.sem(f"layer_zeroed")
        with nc.Block() as block:
            @block.gpsimd
            def _(pool):
                nc.gpsimd.memset(shifted[0:1, 0, P:D], 0.0).then_inc(zeroed, 1)

            @block.sync
            def _(sp):
                sp.dma_start(shifted[1:P, :, P:D], Z[0:P - 1, :, P:D]).then_inc(moved, 16)
                sp.dma_start(shifted[0:1, 1:ST, P:D], Z[P - 1:P, 0:ST - 1, P:D]).then_inc(moved, 16)
                for dst, src in ((w1, "w1"), (w2, "w2"), (b1, "b1"), (aff, "aff")):
                    sp.dma_start(dst[:], w[src]).then_inc(moved, 16)
                sp.dma_start(b2[:], w["b2"].partition_broadcast(P)).then_inc(moved, 16)
                sp.wait_ge(moved, 16 * 7)

            @block.vector
            def _(dve):
                nc.vector.tensor_copy(shifted[:, :, 0:P], Z[:, :, 0:P])

        layernorm_transposed(nc, m, f"{name}_ln", shifted, hT, 0, 4, (aff[:, 0, :], aff[:, 1, :]), sems="layer_ln")

        hidden = [sb(f"hidden{i}", [P, GT, BANK]) for i in range(2)]
        gelus = [sb(f"gelu{i}", [P, BANK]) for i in range(2)]
        out_b = [sb(f"out{i}", [P, BANK]) for i in range(2)]
        CH = S // BANK
        up, acted, gated, down, biased, added = (m.sem(f"layer_f_{n}") for n in
                                                 ("up", "acted", "gated", "down", "biased", "added"))
        with nc.Block() as block:
            @block.tensor
            def _(pe):
                with pe.Fori(0, CH // 2) as cc:
                    for e in range(2):
                        c = cc * 2 + e
                        for t in range(GT):
                            if t >= 2:
                                pe.wait_ge(gated, c * GT + (t - 1))
                            for ag in (1, 0):
                                for k in range(DK):
                                    last = nc.tensor.matmul(m.PS[:, 2 * (t % 2) + ag, :], w1[:, k, ag, t, :],
                                                            hT[:, k, ds(c * BANK, BANK)], start=(k == 0), stop=(k == DK - 1))
                                last.then_inc(up, 1)
                        for u in range(2):
                            pe.wait_ge(gated, (c + 1) * GT)
                            pe.wait_ge(biased, c * 2)
                            for t in range(2):
                                for h in range(GT):
                                    last = nc.tensor.matmul(m.PS[:, 4 + u, t * D:(t + 1) * D],
                                                            hidden[e][:, h, (2 * u + t) * P:(2 * u + t + 1) * P],
                                                            w2[:, h, :], start=(h == 0), stop=(h == GT - 1))
                            last.then_inc(down, 1)

            @block.scalar
            def _(act):
                nc.scalar.preload_act_table(ACT.Gelu)
                with act.Fori(0, CH) as c:
                    for t in range(GT):
                        act.wait_ge(up, c * (2 * GT) + (2 * t + 1))
                        act.wait_ge(gated, c * GT + max(t - 1, 0))
                        nc.scalar.activation(gelus[t % 2][:], m.PS[:, 2 * (t % 2) + 1, :], ACT.Gelu,
                                             bias=b1[:, 1, t:t + 1]).then_inc(acted, 1)

            @block.vector
            def _(dve):
                with dve.Fori(0, CH // 2) as cc:
                    for e in range(2):
                        c = cc * 2 + e
                        for t in range(GT):
                            dve.wait_ge(up, c * (2 * GT) + (2 * t + 2))
                            dve.wait_ge(acted, c * GT + (t + 1))
                            nc.vector.scalar_tensor_tensor(out=hidden[e][:, t, :], in0=m.PS[:, 2 * (t % 2), :],
                                                           scalar=b1[:, 0, t:t + 1], in1=gelus[t % 2][:],
                                                           op0=ALU.add, op1=ALU.mult).then_inc(gated, 1)
                        for u in range(2):
                            dve.wait_ge(down, c * 2 + (u + 1))
                            dve.wait_ge(added, c * 2)
                            nc.vector.tensor_tensor(out_b[u][:], m.PS[:, 4 + u, :],
                                                    b2[:].rearrange("p t d -> p (t d)"), ALU.add).then_inc(biased, 1)
                        for u in range(2):
                            dve.wait_ge(biased, c * 2 + (u + 1))
                            z = Z[:, ds(c * 4 + 2 * u, 2), :].rearrange("p t d -> p (t d)")
                            nc.vector.tensor_tensor(z, z, out_b[u][:], ALU.add).then_inc(added, 1)


def local_transformer(nc, m, tables, layers):
    token_statistics(nc, m, "d_ln", m.X, ST)
    with nc.sbuf_tensor("Z", [P, ST, D], fp32) as Z:
        with nc.Block() as block:
            @block.vector
            def _(dve):
                for t in range(ST):
                    nc.vector.tensor_scalar(Z[:, t, :], m.X[:, t, :], m.mean[:, t:t + 1], m.rstd[:, t:t + 1],
                                            ALU.subtract, ALU.mult)
        for l, w in enumerate(layers):
            if l:
                m.clear_semaphores("layer_")
            local_layer(nc, m, f"d{l}", Z, tables, w)
        with nc.Block() as block:
            @block.vector
            def _(dve):
                for c in range(4):
                    x = m.X[:, 4 * c:4 * c + 4, :].rearrange("p t d -> p (t d)")
                    nc.vector.scalar_tensor_tensor(out=x, in0=Z[:, 4 * c:4 * c + 4, :].rearrange("p t d -> p (t d)"),
                                                   scalar=m.gate[:, 3:4], in1=x, op0=ALU.mult, op1=ALU.add)


def finish(nc, m, out_d):
    stored = m.sem("stored")
    with nc.Block() as block:
        @block.sync
        def _(sp):
            sp.dma_start(out_d.rearrange("(t p) d -> p t d", p=P), m.X[:]).then_inc(stored, 16)
            sp.wait_ge(stored, 16)


LAYER_INPUTS = ("wqkv", "scales", "wo", "w1", "b1", "w2", "b2", "aff")


def flamingo_blocks(nc, d):
    q_parts = [nc.dram_tensor(f"q_part{i}", (P, DK, S), fp16, kind="Internal").ap() for i in range(2)]
    k_parts = [nc.dram_tensor(f"k_part{i}", (P, DK, CTX), fp16, kind="Internal").ap() for i in range(2)]
    layers = [{n: d[f"l1f_{n}{l}"] for n in LAYER_INPUTS} for l in range(DEPTH)]
    with ExitStack() as ctx:
        m = Memory(nc, ctx)
        setup(nc, m, d["x"], d["ident"], d["gates"])
        context_attention(nc, m, d["ctx"], d["mask"], d["l0x_aff"], d["l0x_wq"], d["l0x_wk"], d["l0x_wv"], d["l0x_wo"])
        lora_ffn(nc, m, d["l0f_w1"], d["l0f_b1"], d["l0f_w2"], d["l0f_b2"], d["l0f_scale"])
        narrow_attention(nc, m, d["ctxT"], d["l1x_wq"], d["l1x_wk"], d["l1x_wv"], d["l1x_wo"],
                         d["l1x_bqk"], d["l1x_bv"], d["l1x_bo"], q_parts, k_parts)
        local_transformer(nc, m, dict(rotary=d["rotary"], masks=d["masks"]), layers)
        finish(nc, m, d["out"])


def rotary_tables():
    f = np.float32
    half = np.arange(0, LD, 2, dtype=f)
    inv_freq = (f(1.0) / f(10000.0) ** (half / f(LD))).astype(f)
    pos = np.arange(S, dtype=f)
    angle = np.tile((pos[:, None] * inv_freq[None, :]).astype(f), 2)
    base = ((half + f(0.4 * LD)) / f(1.4 * LD)).astype(f)
    power = ((pos - S // 2) / f(P // 2)).astype(f)
    scale = np.tile((base[None, :] ** power[:, None]).astype(f), 2)
    cos, sin = np.cos(angle), np.sin(angle) * np.repeat(np.array([-1, 1], f), LD // 2)
    table = np.stack([np.stack([8 * cos * scale, cos / scale], 1), np.stack([8 * sin * scale, sin / scale], 1)])
    return table.astype(f).reshape(2, ST, P, 2, LD).transpose(2, 0, 1, 3, 4)


def window_masks():
    i, j = np.arange(P)[:, None], np.arange(P)[None, :]
    big = np.float32(-1e30)
    mask = np.zeros((P, ST, 2 * P), np.float32)
    mask[:, :, 0:P] = np.where(j < i, big, 0)[:, None]
    mask[:, 0, 0:P] = big
    mask[:, :, P:] = np.where(j > i, big, 0)[:, None]
    return mask


def lay_out(a):
    rows = lambda w, n: w.reshape(n, P, -1).transpose(1, 0, 2)
    col = lambda v: v.reshape(-1, P).T
    twice = lambda v: np.stack([v, v])
    d = dict(x=a["x"][0], ident=np.eye(P, dtype=np.float32), gates=np.concatenate([a["g_xattn"], a["g_ffn"]]),
             ctx=a["ctx_1024"][0], mask=a["mask_BxS2_bf1"].view(np.uint8), ctxT=rows(a["ctx_1024"][0].T, DK),
             rotary=rotary_tables(), masks=window_masks())
    d["l0x_aff"] = np.stack([col(a[f"L0_xattn_{n}"]) for n in ("gm", "bm", "gl", "bl")], 1)
    for n in "qkv":
        d[f"l0x_w{n}"] = a[f"L0_xattn_W{n}"].reshape(DK, P, PAIRS, P).transpose(2, 1, 0, 3)
    d["l0x_wo"] = a["L0_xattn_Wo"].reshape(PAIRS, P, D)
    d["l0f_w1"], d["l0f_b1"] = rows(a["L0_ffn_W1"].T, DK), col(a["L0_ffn_b1"])
    d["l0f_w2"], d["l0f_b2"] = rows(a["L0_ffn_W2"].T, HT), twice(a["L0_ffn_b2"])
    d["l0f_scale"] = a["L0_ffn_scale"].reshape(1)
    for n in "qkvo":
        d[f"l1x_w{n}"] = rows(a[f"L1_xattn_W{n}"], DK)
    d["l1x_bqk"] = np.stack([col(a["L1_xattn_bq"]), col(a["L1_xattn_bk"])], 1)
    d["l1x_bv"], d["l1x_bo"] = a["L1_xattn_bv"], twice(a["L1_xattn_bo"])
    for l in range(DEPTH):
        g = lambda n: a[f"L1_ffn_{n}"][l]
        swapped = lambda v: np.concatenate([v[LD // 2:], v[:LD // 2]])
        w1, b1 = np.zeros((D, 2, GT * P), np.float32), np.zeros((2, GT * P), np.float32)
        w2 = np.zeros((GT * P, D), np.float32)
        w1[:, :, :HID], b1[:, :HID], w2[:HID] = g("w1").reshape(D, 2, HID), g("b1").reshape(2, HID), g("w2")
        qk_scales = [g("q_scale"), g("k_scale")]
        layer = dict(wqkv=rows(g("wqkv"), DK), scales=np.stack([np.stack(qk_scales), np.stack([swapped(v) for v in qk_scales])]),
                     wo=rows(g("wo"), INNER // P), w1=w1.reshape(DK, P, 2, GT, P).transpose(1, 0, 2, 3, 4),
                     b1=b1.reshape(2, GT, P).transpose(2, 0, 1), w2=rows(w2, GT), b2=twice(g("b2")),
                     aff=np.stack([col(g("ln_g")), col(g("ln_b"))], 1))
        d.update({f"l1f_{n}{l}": v for n, v in layer.items()})
    return {n: np.ascontiguousarray(v) for n, v in d.items()}


def kernel(**inputs):
    import concourse.bacc as bacc
    from concourse.bass_utils import run_bass_kernel_spmd

    nc = bacc.Bacc("TRN2", target_bir_lowering=False, num_devices=1)
    arrays = lay_out({n: np.asarray(v) for n, v in inputs.items()})
    d = {n: nc.dram_tensor(f"in_{n}_dram", v.shape, mybir.dt.from_np(v.dtype), kind="ExternalInput").ap()
         for n, v in arrays.items()}
    d["out"] = nc.dram_tensor("out_0_dram", (S, D), fp32, kind="ExternalOutput").ap()
    flamingo_blocks(nc, d)
    r = run_bass_kernel_spmd(nc, [{f"in_{n}_dram": v for n, v in arrays.items()}], core_ids=[0])
    return np.asarray(r.results[0]["out_0_dram"]).reshape(1, S, D)
```

```python
import numpy as np
import concourse.bass as bass
from concourse import mybir
from contextlib import ExitStack

fp32 = mybir.dt.float32
fp16 = mybir.dt.float16
bf16 = mybir.dt.bfloat16
fp32r = mybir.dt.float32r
int32 = mybir.dt.int32
ALU = mybir.AluOpType
ACT = mybir.ActivationFunctionType
AX = mybir.AxisListType

P = 128
S, D = 2048, 256
CTX = 1601
ST = S // P
CT = -(-CTX // P)
CLAST = CTX - (CT - 1) * P
DK = D // P
EPS = 1e-5
BANK = 512

AH, AD = 16, 64
PAIRS = AH // 2
KT = CT + ST
KEYS = KT * P
LAT0 = CT * P
MASKED = -60000.0

SAFE_SCORE = 60.0
SAFE_BITS = int(np.float32(SAFE_SCORE ** 2).view(np.int32))
MAX_ROW = 64

LEAD = 2

ds = bass.ds


def take_hi(engine, hi, x):
    return engine.tensor_copy(hi.bitcast(fp32r), x)


def take_lo(engine, lo, x, hi):
    return engine.tensor_tensor(lo.bitcast(fp32r), x, hi, ALU.subtract)


def split_matmul(nc, out, stationary, moving, start, stop):
    (sh, sl), (mh, ml) = stationary, moving
    nc.tensor.matmul(out, sl.bitcast(fp32r), mh.bitcast(fp32r), start=start, stop=False)
    nc.tensor.matmul(out, sh.bitcast(fp32r), ml.bitcast(fp32r), start=False, stop=False)
    return nc.tensor.matmul(out, sh.bitcast(fp32r), mh.bitcast(fp32r), start=False, stop=stop)


def chunk_loop(engine, chunks, lead, body):
    lead(0, 0)
    with engine.Fori(0, chunks // 2 - 1) as cc:
        body(cc * 2, 0, True)
        body(cc * 2 + 1, 1, True)
    body(chunks - 2, 0, True)
    body(chunks - 1, 1, False)


class Memory:

    def __init__(self, nc, ctx):
        self.nc, self.ctx, self.sems, self.free = nc, ctx, {}, []
        self.X = self.sbuf("X", [P, ST, D])
        self.ident = self.sbuf("ident", [P, P])
        self.gate = self.sbuf("gate", [P, 4])
        self.mean = self.sbuf("mean", [P, ST])
        self.rstd = self.sbuf("rstd", [P, ST])
        self.PS = ctx.enter_context(nc.psum_tensor("PS", [P, 8, BANK], fp32))

    def sbuf(self, name, shape, dtype=fp32):
        return self.ctx.enter_context(self.nc.sbuf_tensor(name, shape, dtype))

    def sem(self, name):
        self.sems[name] = self.free.pop() if self.free else self.ctx.enter_context(self.nc.semaphore(name))
        return self.sems[name]

    def give_back(self, prefix):
        ended = [self.sems.pop(name) for name in list(self.sems) if name.startswith(prefix)]
        with self.nc.Block() as block:
            @block.sync
            def _(sp):
                for sem in ended:
                    sp.sem_clear(sem)
        self.free += ended


def setup(nc, m, x_d, ident_d, gates_d):
    raw = m.sbuf("gate_raw", [P, 4])
    loaded, gates_done = m.sem("setup_loaded"), m.sem("gates_done")
    with nc.Block() as block:
        @block.sync
        def _(sp):
            sp.dma_start(m.X[:], x_d.rearrange("(t p) d -> p t d", p=P)).then_inc(loaded, 16)
            sp.dma_start(m.ident[:], ident_d).then_inc(loaded, 16)
            sp.dma_start(raw[:], gates_d.partition_broadcast(P)).then_inc(loaded, 16)

        @block.scalar
        def _(act):
            act.wait_ge(loaded, 48)
            nc.scalar.activation(m.gate[:], raw[:], ACT.Tanh).then_inc(gates_done, 1)


def token_statistics(nc, m, name, src, T, twice=False, sems=None, loads=None):
    sems = sems or name
    with ExitStack() as own:
        sb = lambda n, s, d=fp32: own.enter_context(nc.sbuf_tensor(f"{name}_{n}", s, d))
        stats = sb("stats", [P, T, 6])
        work = sb("work", [P, 8, T])
        mean, rstd = m.mean[:, 0:T], m.rstd[:, 0:T]
        stats_done, step = m.sem(f"{sems}_stats"), m.sem(f"{sems}_step")
        root_wanted, root_done = m.sem(f"{sems}_rootw"), m.sem(f"{sems}_root")
        with nc.Block() as block:
            if loads:
                @block.sync
                def _(sp):
                    loads(sp)

            @block.vector
            def _(dve):
                for t in range(T):
                    nc.vector.bn_stats(stats[:, t, :], src[:, t, :]).then_inc(stats_done, 1)
                dve.wait_ge(stats_done, T)
                me, mo = stats[:, :, 1], stats[:, :, 4]
                qe, qo = stats[:, :, 2], stats[:, :, 5]
                done = [0]

                def chain(ins):
                    done[0] += 1
                    ins.then_inc(step, 1)
                    dve.wait_ge(step, done[0])

                nc.vector.tensor_tensor(work[:, 0, :], me, mo, ALU.add)
                nc.vector.tensor_tensor(work[:, 1, :], me, mo, ALU.subtract)
                nc.vector.tensor_tensor(work[:, 2, :], qe, qo, ALU.add)
                chain(nc.vector.memset(work[:, 3, :], EPS))
                nc.vector.tensor_scalar(mean, work[:, 0, :], 0.5, None, ALU.mult)
                nc.vector.scalar_tensor_tensor(out=work[:, 4, :], in0=work[:, 1, :], scalar=0.25,
                                               in1=work[:, 1, :], op0=ALU.mult, op1=ALU.mult)
                chain(nc.vector.scalar_tensor_tensor(out=work[:, 5, :], in0=work[:, 2, :], scalar=1.0 / D,
                                                     in1=work[:, 3, :], op0=ALU.mult, op1=ALU.add))
                nc.vector.tensor_tensor(work[:, 6, :], work[:, 4, :], work[:, 5, :],
                                        ALU.add).then_inc(root_wanted, 1)
                dve.wait_ge(root_done, 1)
                chain(nc.vector.reciprocal(rstd, work[:, 7, :]))
                if twice:
                    chain(nc.vector.tensor_scalar(work[:, 0, :], work[:, 2, :], 1.0 / D, None, ALU.mult))
                    nc.vector.tensor_tensor(work[:, 5, :], work[:, 0, :], work[:, 4, :], ALU.add)
                    chain(nc.vector.tensor_tensor(work[:, 1, :], rstd, rstd, ALU.mult))
                    chain(nc.vector.tensor_tensor(work[:, 2, :], work[:, 5, :], work[:, 1, :], ALU.mult))
                    nc.vector.tensor_scalar(work[:, 6, :], work[:, 2, :], EPS, None,
                                            ALU.add).then_inc(root_wanted, 1)
                    dve.wait_ge(root_done, 2)
                    chain(nc.vector.reciprocal(work[:, 0, :], work[:, 7, :]))
                    chain(nc.vector.tensor_tensor(rstd, rstd, work[:, 0, :], ALU.mult))

            @block.scalar
            def _(act):
                nc.scalar.preload_act_table(ACT.Sqrt)
                for i in range(2 if twice else 1):
                    act.wait_ge(root_wanted, i + 1)
                    nc.scalar.activation(work[:, 7, :], work[:, 6, :], ACT.Sqrt).then_inc(root_done, 1)


def layernorm_transposed(nc, m, name, src, dst, dst0, groups, affine=None, twice=False, sems=None, loads=None):
    token_statistics(nc, m, name, src, groups * 4, twice, sems, loads)
    sems = sems or name
    with ExitStack() as own:
        staged = [own.enter_context(nc.sbuf_tensor(f"{name}_staged{i}", [P, 4, D], fp32)) for i in range(2)]
        normed, transposed, moved = m.sem(f"{sems}_normed"), m.sem(f"{sems}_tr"), m.sem(f"{sems}_mv")
        with nc.Block() as block:
            @block.vector
            def _(dve):
                for g in range(groups):
                    if g >= 2:
                        dve.wait_ge(transposed, g - 1)
                    for j in range(4):
                        t = g * 4 + j
                        last = nc.vector.tensor_scalar(staged[g % 2][:, j, :], src[:, t, :], m.mean[:, t:t + 1],
                                                       m.rstd[:, t:t + 1], ALU.subtract, ALU.mult)
                    last.then_inc(normed, 1)

            @block.scalar
            def _(act):
                for g in range(groups):
                    act.wait_ge(transposed, g + 1)
                    for k in range(DK):
                        out = dst[:, k, g * BANK + dst0:(g + 1) * BANK + dst0]
                        bank = m.PS[:, 2 * g + k, :]
                        if affine is None:
                            ins = nc.scalar.activation(out, bank, ACT.Copy)
                        else:
                            ins = nc.scalar.activation(out, bank, ACT.Identity, scale=affine[0][:, k:k + 1],
                                                       bias=affine[1][:, k:k + 1])
                    ins.then_inc(moved, 1)

            @block.tensor
            def _(pe):
                for g in range(groups):
                    pe.wait_ge(normed, g + 1)
                    for k in range(DK):
                        for j in range(4):
                            last = nc.tensor.transpose(m.PS[:, 2 * g + k, j * P:(j + 1) * P],
                                                       staged[g % 2][:, j, k * P:(k + 1) * P], m.ident[:])
                    last.then_inc(transposed, 1)


def score_maxima_pe(nc, m, pe, queries, keys, spans, negated, scored, reduced, base_r, ready=()):
    with pe.Fori(0, ST) as t:
        for sem, value in ready:
            pe.wait_ge(sem, value)
        for s, (c0, n) in enumerate(spans):
            pe.wait_ge(reduced, base_r + t * len(spans) + s)
            for b in range(-(-n // BANK)):
                k0, w = c0 + b * BANK, min(BANK, n - b * BANK)
                for i, (q, k) in enumerate(zip(queries, keys)):
                    last = nc.tensor.matmul(m.PS[:, b, 0:w], q[:, ds(t * P, P)], k[:, k0:k0 + w],
                                            start=(i == 0), stop=(i == len(keys) - 1))
            last.then_inc(scored, 1)
    pe.wait_ge(reduced, base_r + (ST * len(spans) + 1))
    for t in range(ST):
        last = nc.tensor.matmul(m.PS[MAX_ROW:MAX_ROW + 1, t // 4, (t % 4) * P:(t % 4 + 1) * P], negated[:, t:t + 1],
                                m.ident[:], start=True, stop=True)
    last.then_inc(scored, 1)


def score_maxima_dve(nc, m, dve, spans, partial, negated, row, scored, reduced, base_s, base_r):
    with dve.Fori(0, ST) as t:
        for s, (c0, n) in enumerate(spans):
            dve.wait_ge(scored, base_s + t * len(spans) + (s + 1))
            nb = n // BANK
            out = partial[:, s, 0:1, ds(t, 1)].rearrange("p a b -> p (a b)")
            nc.vector.tensor_reduce(out, m.PS[:, 0:nb, :].rearrange("p b c -> p (b c)"), AX.X, ALU.max)
            out = partial[:, s, 1:2, ds(t, 1)].rearrange("p a b -> p (a b)")
            w = n - nb * BANK if n % BANK else BANK
            nc.vector.tensor_reduce(out, m.PS[:, -(-n // BANK) - 1, 0:w], AX.X, ALU.max).then_inc(reduced, 1)
    dve.wait_ge(reduced, base_r + ST * len(spans))
    nc.vector.tensor_reduce(negated[:], partial[:].rearrange("p s a t -> p t (s a)"), AX.X, ALU.max,
                            negate=True).then_inc(reduced, 1)
    dve.wait_ge(scored, base_s + (ST * len(spans) + 1))
    nc.vector.tensor_copy(row, m.PS[MAX_ROW:MAX_ROW + 1, 0:4, :].rearrange("p b c -> p (b c)")).then_inc(reduced, 1)


def context_attention(nc, m, ctx_d, mask_d, affines_d, wq_d, wk_d, wv_d, wo_d):
    with ExitStack() as own:
        sb = lambda n, s, d=fp32: own.enter_context(nc.sbuf_tensor(f"a_{n}", s, d))
        kvT = sb("kvT", [P, DK, KEYS + (4 * -(-CT // 4) - CT) * P])
        aff = sb("aff", [P, 4, DK])
        masked = sb("masked", [P, LAT0], fp16)
        with nc.sbuf_tensor("a_ctx", [P, 16, D], fp32) as ctx_tok:
            with nc.sbuf_tensor("a_mask", [P, LAT0], mybir.dt.uint8) as mask_f:
                loaded, cleared, bias_done = m.sem("a_loaded"), m.sem("a_cleared"), m.sem("a_bias_done")
                with nc.Block() as block:
                    @block.gpsimd
                    def _(pool):
                        nc.gpsimd.memset(ctx_tok[:, CT - 1:16, :], 0.0).then_inc(cleared, 1)

                    @block.sync
                    def _(sp):
                        sp.dma_start(ctx_tok[:, 0:CT - 1, :],
                                     ctx_d[0:(CT - 1) * P, :].rearrange("(t p) d -> p t d", p=P)).then_inc(loaded, 16)
                        sp.dma_start(aff[:], affines_d).then_inc(loaded, 16)
                        sp.wait_ge(cleared, 2)
                        sp.dma_start(ctx_tok[0:CLAST, CT - 1, :], ctx_d[(CT - 1) * P:CTX, :]).then_inc(loaded, 16)
                        sp.dma_start(mask_f[96:97, 0:CTX], mask_d).then_inc(loaded, 16)
                        sp.wait_ge(loaded, 64)

                    @block.vector
                    def _(dve):
                        nc.vector.memset(mask_f[96:97, :], 0).then_inc(cleared, 1)
                        dve.wait_ge(loaded, 64)
                        nc.vector.tensor_scalar(masked[96:97, :], mask_f[96:97, :], -MASKED, MASKED,
                                                ALU.mult, ALU.add).then_inc(bias_done, 1)
            layernorm_transposed(nc, m, "a_ctx", ctx_tok, kvT, 0, 4, (aff[:, 0, :], aff[:, 1, :]))
        layernorm_transposed(nc, m, "a_lat", m.X, kvT, LAT0, 4, (aff[:, 2, :], aff[:, 3, :]), twice=True)

        K1 = [sb(f"K1_{h}", [P, KEYS], fp16) for h in range(2)]
        K2 = [sb(f"K2_{h}", [P, KEYS], fp16) for h in range(2)]
        Q1 = [sb(f"Q1_{h}", [P, S], fp16) for h in range(2)]
        Q2 = [sb(f"Q2_{h}", [P, S], fp16) for h in range(2)]
        V = [sb(f"V_{h}", [P, KT, AD]) for h in range(2)]
        probs = [sb(f"probs{i}", [P, 2 * BANK]) for i in range(3)]
        prob_sums = [sb(f"prob_sums{i}", [P, 2 * BANK]) for i in range(2)]
        ones = sb("ones", [P, AD])
        wqkv = [sb(f"w{n}", [P, DK, P]) for n in "qkv"]
        wo = sb("wo", [P, D])
        heads_outT = sb("heads_outT", [P, S])
        inverse = [sb(f"inverse{i}", [P, BANK]) for i in range(2)]
        squares = [sb(f"squares{i}", [P, BANK], bf16) for i in range(2)]
        head_ones = sb("head_ones", [P, 32], bf16)
        peaks, top, bound = sb("peaks", [P, 3]), sb("top", [1, 3]), sb("bound", [1, 1])
        spans = [(0, 4 * BANK), (4 * BANK, KEYS - 4 * BANK)]
        partial, negated = sb("partial", [P, len(spans), 2, ST]), sb("negated", [P, ST])

        rows_set, ones_cleared = m.sem("a_rows_set"), m.sem("a_ones_cleared")
        with nc.Block() as block:
            @block.gpsimd
            def _(pool):
                nc.gpsimd.memset(ones[:], 1.0)
                nc.gpsimd.memset(head_ones[:], 0.0).then_inc(ones_cleared, 1)
                pool.wait_ge(ones_cleared, 1)
                for h in range(2):
                    nc.gpsimd.memset(head_ones[64 * h:64 * h + 64, h:h + 1], 1.0)

            @block.vector
            def _(dve):
                for h in range(2):
                    nc.vector.memset(K2[h][64:128, :], 0.0)
                    nc.vector.memset(Q2[h][64:128, :], 0.0).then_inc(rows_set, 1)
                dve.wait_ge(rows_set, 2)
                for h in range(2):
                    nc.vector.memset(K2[h][64:65, :], 1.0)
                    nc.vector.memset(Q2[h][96:97, :], 1.0)
                    nc.vector.tensor_copy(K2[h][96:97, 0:LAT0], masked[96:97, :])

        NKU, NQU, NVU = -(-KEYS // BANK), S // BANK, -(-KT // 4)
        UNITS = NKU + NQU + NVU
        BLOCKS = 4
        STEPS = BLOCKS * KT
        HALF = S // 2
        w_loaded, wo_loaded = m.sem("a_w_loaded"), m.sem("a_wo_loaded")
        projected, split_hi, unit_free = (m.sem(f"a_{n}") for n in ("projected", "hi", "unit_free"))
        scored, exped, applied, summed = (m.sem(f"a_{n}") for n in ("scored", "exped", "applied", "summed"))
        totalled, inverted, block_out = (m.sem(f"a_{n}") for n in ("totalled", "inverted", "block_out"))
        mixed, added = (m.sem(f"a_{n}") for n in ("mixed", "added"))
        squared, normed, peaked, peaks_turned, topped, bounded = (
            m.sem(f"a_{n}") for n in ("squared", "normed", "peaked", "peaks_turned", "topped", "bounded"))
        max_scored, max_reduced = (m.sem(f"a_{n}") for n in ("max_scored", "max_reduced"))
        SCALE = AD ** -0.5
        NORMS = NKU + NQU
        MAX_SCORED, MAX_REDUCED = ST * len(spans) + 1, ST * len(spans) + 2
        kcols = [(u * BANK, min(BANK, KEYS - u * BANK)) for u in range(NKU)]

        with nc.Block() as block:
            @block.sync
            def _(sp):
                with sp.Fori(0, PAIRS) as i:
                    sp.wait_ge(projected, i * UNITS)
                    for w, w_d in zip(wqkv, (wq_d, wk_d, wv_d)):
                        sp.dma_start(w[:], w_d[ds(i, 1)].rearrange("o p k n -> p (o k) n")).then_inc(w_loaded, 16)
                    sp.wait_ge(mixed, i * 8)
                    sp.dma_start(wo[:], wo_d[ds(i, 1)].rearrange("o p n -> p (o n)")).then_inc(wo_loaded, 16)

            @block.tensor
            def _(pe):
                def project(i, u):
                    if u >= 4:
                        pe.wait_ge(unit_free, i * UNITS + (u - 3))
                    bank = m.PS[:, u % 4, :]
                    if u < NKU + NQU:
                        c0, n = kcols[u] if u < NKU else (LAT0 + (u - NKU) * BANK, BANK)
                        w = wqkv[1] if u < NKU else wqkv[0]
                        for k in range(DK):
                            last = nc.tensor.matmul(bank[:, 0:n], w[:, k, :], kvT[:, k, c0:c0 + n],
                                                    start=(k == 0), stop=(k == DK - 1))
                    else:
                        t0 = (u - NKU - NQU) * 4
                        for t in range(t0, min(t0 + 4, KT)):
                            for k in range(DK):
                                last = nc.tensor.matmul(bank[:, (t - t0) * P:(t - t0 + 1) * P],
                                                        kvT[:, k, t * P:(t + 1) * P], wqkv[2][:, k, :],
                                                        start=(k == 0), stop=(k == DK - 1))
                    last.then_inc(projected, 1)

                def norm(i, u):
                    if u == NKU:
                        pe.wait_ge(added, i * 8)
                    pe.wait_ge(squared, i * NORMS + (u + 1))
                    bank = 6 if u >= NKU else 5 + 2 * (u // 4)
                    g = 32 * (u % 4)
                    n = kcols[u][1] if u < NKU else BANK
                    for r in range(BANK // n):
                        last = nc.tensor.matmul(m.PS[g:g + 32, bank, r * n:(r + 1) * n], head_ones[:],
                                                squares[u % 2][:, 0:n], start=True, stop=True, tile_position=(0, g))
                    last.then_inc(normed, 1)

                def turn_peaks(i):
                    pe.wait_ge(peaked, i + 1)
                    for c in range(3):
                        last = nc.tensor.matmul(m.PS[0:1, 4, c * P:(c + 1) * P], peaks[:, c:c + 1], m.ident[:],
                                                start=True, stop=True)
                    last.then_inc(peaks_turned, 1)

                def score(i, n):
                    b, s = n // KT, n % KT
                    half, h = b // 2, b % 2
                    if n >= 2:
                        pe.wait_ge(exped, i * STEPS + (n - 1))
                    for c in range(2):
                        q0 = half * HALF + c * BANK
                        out = m.PS[:, 2 * (n % 2) + c, :]
                        nc.tensor.matmul(out, K1[h][:, s * P:(s + 1) * P], Q1[h][:, q0:q0 + BANK], start=True, stop=False)
                        last = nc.tensor.matmul(out, K2[h][:, s * P:(s + 1) * P], Q2[h][:, q0:q0 + BANK],
                                                start=False, stop=True)
                    last.then_inc(scored, 1)

                def apply(i, n):
                    b, s = n // KT, n % KT
                    if s == 0 and b >= 2:
                        pe.wait_ge(block_out, i * BLOCKS + (b - 1))
                    pe.wait_ge(exped, i * STEPS + (n + 1))
                    for c in range(2):
                        last = nc.tensor.matmul(m.PS[64 * c:64 * c + 64, 4 + b % 2, :], V[b % 2][:, s, :],
                                                probs[n % 3][:, c * BANK:(c + 1) * BANK],
                                                start=(s == 0), stop=(s == KT - 1))
                    last.then_inc(applied, 1)

                def total(i, b):
                    pe.wait_ge(summed, i * STEPS + (b + 1) * KT)
                    for c in range(2):
                        last = nc.tensor.matmul(m.PS[64 * c:64 * c + 64, 6 + b % 2, :], ones[:],
                                                prob_sums[b % 2][:, c * BANK:(c + 1) * BANK], start=True, stop=True)
                    last.then_inc(totalled, 1)

                with pe.Fori(0, PAIRS) as i:
                    pe.wait_ge(w_loaded, (i + 1) * 48)
                    for u in range(UNITS):
                        if u == UNITS - 1:
                            pe.wait_ge(bounded, i + 1)
                        project(i, u)
                        if 2 <= u < NORMS + 2:
                            norm(i, u - 2)
                        if u == UNITS - 4:
                            turn_peaks(i)
                    bits = pe.value_load(bound[0:1, 0:1].bitcast(int32))
                    pe.wait_ge(unit_free, (i + 1) * UNITS)
                    with pe.If(bits > SAFE_BITS):
                        for h in range(2):
                            score_maxima_pe(nc, m, pe, (Q1[h], Q2[h]), (K1[h], K2[h]), spans, negated,
                                            max_scored, max_reduced, (i * 2 + h) * MAX_REDUCED)
                    with pe.Else():
                        nc.tensor.matmul(m.PS[0:1, 4, 0:1], peaks[:, 0:1], m.ident[:, 0:1], start=True,
                                         stop=True).then_inc(max_scored, 2 * MAX_SCORED)
                    pe.wait_ge(max_reduced, (i + 1) * (2 * MAX_REDUCED))
                    score(i, 0)
                    for n in range(STEPS):
                        if n + 1 < STEPS:
                            score(i, n + 1)
                        apply(i, n)
                        if n % KT == 1 and n > KT:
                            total(i, n // KT - 1)
                    pe.wait_ge(wo_loaded, (i + 1) * 16)
                    for u in range(ST // 2):
                        if u == 2:
                            total(i, BLOCKS - 1)
                        if u == 0:
                            pe.wait_ge(block_out, i * BLOCKS + 3)
                        if u == ST // 4:
                            pe.wait_ge(block_out, (i + 1) * BLOCKS)
                        if u >= 2:
                            pe.wait_ge(added, i * 8 + (u - 1))
                        for e in range(2):
                            t = 2 * u + e
                            last = nc.tensor.matmul(m.PS[:, 4 + 2 * (u % 2), e * D:(e + 1) * D],
                                                    heads_outT[:, t * P:(t + 1) * P], wo[:], start=True, stop=True)
                        last.then_inc(mixed, 1)

            @block.scalar
            def _(act):
                nc.scalar.preload_act_table(ACT.Exp)
                with act.Fori(0, PAIRS) as i:
                    for u in range(NKU + NQU):
                        act.wait_ge(projected, i * UNITS + (u + 1))
                        act.wait_ge(normed, i * NORMS + max(u - 1, 0))
                        n = kcols[u][1] if u < NKU else BANK
                        nc.scalar.activation(squares[u % 2][:, 0:n], m.PS[:, u % 4, 0:n], ACT.Square,
                                             scale=1.0 if u < NKU else SCALE).then_inc(squared, 1)
                        for h in range(2):
                            rows = slice(64 * h, 64 * h + 64)
                            if u < NKU:
                                c0, n = kcols[u]
                                last = nc.scalar.activation(K1[h][0:64, c0:c0 + n], m.PS[rows, u % 4, 0:n], ACT.Copy)
                            else:
                                c0 = (u - NKU) * BANK
                                for half in range(2):
                                    last = nc.scalar.activation(Q1[h][64 * half:64 * half + 64, c0:c0 + BANK],
                                                                m.PS[rows, u % 4, :], ACT.Copy, scale=SCALE)
                        last.then_inc(split_hi, 1)

                    for n in range(STEPS):
                        act.wait_ge(scored, i * STEPS + (n + 1))
                        if n >= 3:
                            act.wait_ge(applied, i * STEPS + (n - 2))
                            act.wait_ge(summed, i * STEPS + (n - 2))
                        b0 = 2 * (n % 2)
                        nc.scalar.activation(probs[n % 3][:], m.PS[:, b0:b0 + 2, :].rearrange("p b c -> p (b c)"),
                                             ACT.Exp).then_inc(exped, 1)

            @block.vector
            def _(dve):
                with dve.Fori(0, PAIRS) as i:
                    for u in range(UNITS):
                        if u < NKU + NQU:
                            dve.wait_ge(split_hi, i * (NKU + NQU) + (u + 1))
                        else:
                            dve.wait_ge(projected, i * UNITS + (u + 1))
                        for h in range(2):
                            rows = slice(64 * h, 64 * h + 64)
                            if u < NKU:
                                c0, n = kcols[u]
                                nc.vector.tensor_copy(K2[h][0:64, c0:c0 + n], K1[h][0:64, c0:c0 + n])
                                last = nc.vector.tensor_tensor(K1[h][64:128, c0:c0 + n], m.PS[rows, u % 4, 0:n],
                                                               K1[h][0:64, c0:c0 + n], ALU.subtract)
                            elif u < NKU + NQU:
                                c0 = (u - NKU) * BANK
                                last = nc.vector.scalar_tensor_tensor(
                                    out=Q2[h][0:64, c0:c0 + BANK], in0=m.PS[rows, u % 4, :], scalar=SCALE,
                                    in1=Q1[h][0:64, c0:c0 + BANK], op0=ALU.mult, op1=ALU.subtract)
                            else:
                                t0 = (u - NKU - NQU) * 4
                                n = min(4, KT - t0)
                                last = nc.vector.tensor_copy(
                                    V[h][:, t0:t0 + n, :],
                                    m.PS[:, u % 4, 0:n * P].rearrange("p (t c) -> p t c", c=P)[:, :, 64 * h:64 * h + 64])
                        if u == NORMS:
                            for h in range(2):
                                last = nc.vector.memset(Q2[h][MAX_ROW:MAX_ROW + 1, :], 0.0)
                        last.then_inc(unit_free, 1)
                        if u == NORMS + 2:
                            dve.wait_ge(normed, (i + 1) * NORMS)
                            nc.vector.tensor_reduce(peaks[:], m.PS[:, 5:8, :], AX.X, ALU.max).then_inc(peaked, 1)
                        if u == UNITS - 3:
                            dve.wait_ge(peaks_turned, i + 1)
                            nc.vector.tensor_reduce(top[:], m.PS[0:1, 4, 0:3 * P].rearrange("p (c n) -> p c n", n=P),
                                                    AX.X, ALU.max).then_inc(topped, 1)
                            dve.wait_ge(topped, i + 1)
                            nc.vector.scalar_tensor_tensor(out=bound[:], in0=top[:, 0:1], scalar=top[:, 2:3],
                                                           in1=top[:, 1:2], op0=ALU.max, op1=ALU.mult).then_inc(bounded, 1)
                    dve.wait_ge(rows_set, 2)
                    dve.wait_ge(bounded, i + 1)
                    bits = dve.value_load(bound[0:1, 0:1].bitcast(int32))
                    with dve.If(bits > SAFE_BITS):
                        for h in range(2):
                            score_maxima_dve(nc, m, dve, spans, partial, negated, Q2[h][MAX_ROW:MAX_ROW + 1, :],
                                             max_scored, max_reduced, (i * 2 + h) * MAX_SCORED, (i * 2 + h) * MAX_REDUCED)
                    with dve.Else():
                        nc.vector.memset(top[:], 0.0).then_inc(max_reduced, 2 * MAX_REDUCED)

                    def block_output(b):
                        half, h = b // 2, b % 2
                        dve.wait_ge(totalled, i * BLOCKS + (b + 1))
                        nc.vector.reciprocal(inverse[b % 2][:], m.PS[:, 6 + b % 2, :]).then_inc(inverted, 1)
                        dve.wait_ge(inverted, i * BLOCKS + (b + 1))
                        for c in range(2):
                            rows, q0 = slice(64 * c, 64 * c + 64), half * HALF + c * BANK
                            last = nc.vector.tensor_tensor(heads_outT[64 * h:64 * h + 64, q0:q0 + BANK],
                                                           m.PS[rows, 4 + b % 2, :], inverse[b % 2][rows, :], ALU.mult)
                        last.then_inc(block_out, 1)

                    for n in range(STEPS):
                        b, s = n // KT, n % KT
                        dve.wait_ge(exped, i * STEPS + (n + 1))
                        if s:
                            dve.wait_ge(summed, i * STEPS + n)
                        if s == 0:
                            nc.vector.tensor_copy(prob_sums[b % 2][:], probs[n % 3][:]).then_inc(summed, 1)
                        else:
                            nc.vector.tensor_tensor(prob_sums[b % 2][:], prob_sums[b % 2][:], probs[n % 3][:],
                                                    ALU.add).then_inc(summed, 1)
                        if s == 3 and b:
                            block_output(b - 1)
                    for u in range(ST // 2):
                        if u == 2:
                            block_output(BLOCKS - 1)
                        dve.wait_ge(mixed, i * 8 + (u + 1))
                        nc.vector.scalar_tensor_tensor(
                            out=m.X[:, 2 * u:2 * u + 2, :].rearrange("p t d -> p (t d)"), in0=m.PS[:, 4 + 2 * (u % 2), :],
                            scalar=m.gate[:, 0:1], in1=m.X[:, 2 * u:2 * u + 2, :].rearrange("p t d -> p (t d)"),
                            op0=ALU.mult, op1=ALU.add).then_inc(added, 1)


H = 1024
HT = H // P


def lora_ffn(nc, m, w1_d, b1_d, w2_d, b2_d, scale_d):
    with ExitStack() as own:
        sb = lambda n, s, d=fp32: own.enter_context(nc.sbuf_tensor(f"b_{n}", s, d))
        yT = sb("yT", [P, DK, S])
        W1T, W2T = sb("W1T", [P, DK, H]), sb("W2T", [P, HT, D])
        b1, b2, scale = sb("b1", [P, HT]), sb("b2", [P, 2, D]), sb("scale", [P, 1])
        loaded, first_done, rows_in = m.sem("b_loaded"), m.sem("b_first"), m.sem("b_rows")

        def loads(sp):
            sp.dma_start(W1T[:], w1_d).then_inc(loaded, 16)
            sp.dma_start(W2T[:], w2_d).then_inc(loaded, 16)
            sp.dma_start(b1[:], b1_d).then_inc(loaded, 16)
            sp.dma_start(b2[:], b2_d.partition_broadcast(P)).then_inc(loaded, 16)
            sp.dma_start(scale[:], scale_d.partition_broadcast(P)).then_inc(loaded, 16)

        layernorm_transposed(nc, m, "b_ln", m.X, yT, 0, 4, loads=loads)
        first, rows = sb("first", [P, D]), sb("rows", [1, 16, D])
        outer, updated = m.sem("b_outer"), m.sem("b_updated")
        with nc.Block() as block:
            @block.sync
            def _(sp):
                sp.wait_ge(first_done, 1)
                sp.dma_start(rows[:], first[1:17, :]).then_inc(rows_in, 16)

            @block.vector
            def _(dve):
                nc.vector.tensor_scalar(first[:], m.X[:, 0, :], m.mean[:, 0:1], m.rstd[:, 0:1],
                                        ALU.subtract, ALU.mult).then_inc(first_done, 1)
                dve.wait_ge(loaded, 80)
                for u in range(8):
                    dve.wait_ge(outer, u + 1)
                    w = (W1T[:, u // 2, (u % 2) * BANK:(u % 2 + 1) * BANK] if u < 4 else
                         W2T[:, 2 * (u - 4):2 * (u - 4) + 2, :].rearrange("p t o -> p (t o)"))
                    nc.vector.scalar_tensor_tensor(out=w, in0=m.PS[:, u, :], scalar=scale[:], in1=w,
                                                   op0=ALU.mult, op1=ALU.add).then_inc(updated, 1)

            @block.tensor
            def _(pe):
                pe.wait_ge(rows_in, 16)
                for u in range(4):
                    k = u // 2
                    for e in range(2):
                        i = 2 * (u % 2) + e
                        last = nc.tensor.matmul(m.PS[:, u, e * D:(e + 1) * D], rows[:, 2 * i + 1, k * P:(k + 1) * P],
                                                rows[:, 2 * i, :], start=True, stop=True)
                    last.then_inc(outer, 1)
                for u in range(4):
                    for e in range(2):
                        r, half = divmod(2 * u + e, 2)
                        for i in range(4):
                            last = nc.tensor.matmul(
                                m.PS[:, 4 + u, e * D + 64 * i:e * D + 64 * i + 64],
                                rows[:, 2 * (i + 4) + 1, half * P:(half + 1) * P],
                                rows[:, 2 * (i + 4), :].rearrange("p (a r) -> p r a", r=4)[:, r, :],
                                start=True, stop=True)
                    last.then_inc(outer, 1)

        hidden = [sb(f"hidden{i}", [P, BANK]) for i in range(4)]
        hidden_hi, hidden_lo = ([sb(f"hidden_{part}{i}", [P, HT, BANK]) for i in range(2)] for part in ("hi", "lo"))
        W1_hi, W2_hi, yT_hi = sb("W1_hi", [P, DK, H]), sb("W2_hi", [P, HT, D]), sb("yT_hi", [P, DK, S])
        W1_lo, W2_lo, yT_lo = sb("W1_lo", [P, DK, H]), sb("W2_lo", [P, HT, D]), sb("yT_lo", [P, DK, S])
        out_b = [sb(f"out{i}", [P, BANK]) for i in range(2)]
        CH = S // BANK
        up, acted, down, biased, added = (m.sem(f"b_{n}") for n in ("up", "acted", "down", "biased", "added"))
        w_hi, w_split, y_hi, y_split, hid_hi, hidden_split = (
            m.sem(f"b_{n}") for n in ("w_hi", "w_split", "y_hi", "y_split", "hid_hi", "hidden_split"))
        with nc.Block() as block:
            @block.gpsimd
            def _(pool):
                pool.wait_ge(w_hi, 1)
                for t in range(HT):
                    cols = slice(t * P, (t + 1) * P)
                    take_lo(nc.gpsimd, W1_lo[:, :, cols], W1T[:, :, cols], W1_hi[:, :, cols]).then_inc(w_split, 1)
                pool.wait_ge(w_hi, 2)
                take_lo(nc.gpsimd, W2_lo[:], W2T[:], W2_hi[:]).then_inc(w_split, 1)

            @block.tensor
            def _(pe):
                def raise_tiles(c, e, tiles):
                    pe.wait_ge(y_split, c + 1)
                    for t in tiles:
                        pe.wait_ge(w_split, t + 1)
                        if t >= 4 or type(c) is not int or c:
                            pe.wait_ge(acted, c * HT + (t - 3))
                        for k in range(DK):
                            cols, tokens = slice(t * P, (t + 1) * P), ds(c * BANK, BANK)
                            last = split_matmul(nc, m.PS[:, t % 4, :], (W1_hi[:, k, cols], W1_lo[:, k, cols]),
                                                (yT_hi[:, k, tokens], yT_lo[:, k, tokens]), k == 0, k == DK - 1)
                        last.then_inc(up, 1)

                def chunk(c, e, more):
                    raise_tiles(c, e, range(LEAD, HT))
                    if more:
                        raise_tiles(c + 1, 1 - e, range(LEAD))
                    pe.wait_ge(w_split, HT + 1)
                    for u in range(2):
                        pe.wait_ge(hidden_split, (c + 1) * HT)
                        pe.wait_ge(biased, c * 2)
                        for t in range(2):
                            tokens = slice((2 * u + t) * P, (2 * u + t + 1) * P)
                            for h in range(HT):
                                last = split_matmul(nc, m.PS[:, 4 + u, t * D:(t + 1) * D],
                                                    (hidden_hi[e][:, h, tokens], hidden_lo[e][:, h, tokens]),
                                                    (W2_hi[:, h, :], W2_lo[:, h, :]), h == 0, h == HT - 1)
                        last.then_inc(down, 1)

                chunk_loop(pe, CH, lambda c, e: raise_tiles(c, e, range(LEAD)), chunk)

            @block.scalar
            def _(act):
                nc.scalar.preload_act_table(ACT.Gelu)
                with act.Fori(0, CH // 2) as cc:
                    for e in range(2):
                        c = cc * 2 + e
                        for t in range(HT):
                            act.wait_ge(up, c * HT + (t + 1))
                            act.wait_ge(hidden_split, c * HT + max(t - 3, 0))
                            nc.scalar.activation(hidden[t % 4][:], m.PS[:, t % 4, :], ACT.Gelu,
                                                 bias=b1[:, t:t + 1]).then_inc(acted, 1)

            @block.vector
            def _(dve):
                take_hi(nc.vector, W1_hi[:], W1T[:]).then_inc(w_hi, 1)
                for c in range(CH):
                    tokens = slice(c * BANK, (c + 1) * BANK)
                    take_hi(nc.vector, yT_hi[:, :, tokens], yT[:, :, tokens]).then_inc(y_hi, 1)
                    dve.wait_ge(y_hi, c + 1)
                    take_lo(nc.vector, yT_lo[:, :, tokens], yT[:, :, tokens], yT_hi[:, :, tokens]).then_inc(y_split, 1)
                    if c == 1:
                        take_hi(nc.vector, W2_hi[:], W2T[:]).then_inc(w_hi, 1)
                def split_tiles(c, e, tiles):
                    for t in tiles:
                        dve.wait_ge(acted, c * HT + (t + 1))
                        take_hi(nc.vector, hidden_hi[e][:, t, :], hidden[t % 4][:]).then_inc(hid_hi, 1)
                        dve.wait_ge(hid_hi, c * HT + (t + 1))
                        take_lo(nc.vector, hidden_lo[e][:, t, :], hidden[t % 4][:],
                                hidden_hi[e][:, t, :]).then_inc(hidden_split, 1)

                def chunk(c, e, more):
                    split_tiles(c, e, range(LEAD, HT))
                    if more:
                        split_tiles(c + 1, 1 - e, range(LEAD))
                    for u in range(2):
                        dve.wait_ge(down, c * 2 + (u + 1))
                        dve.wait_ge(added, c * 2)
                        nc.vector.tensor_tensor(out_b[u][:], m.PS[:, 4 + u, :],
                                                b2[:].rearrange("p t d -> p (t d)"), ALU.add).then_inc(biased, 1)
                    for u in range(2):
                        dve.wait_ge(biased, c * 2 + (u + 1))
                        x = m.X[:, ds(c * 4 + 2 * u, 2), :].rearrange("p t d -> p (t d)")
                        nc.vector.scalar_tensor_tensor(out=x, in0=out_b[u][:], scalar=m.gate[:, 2:3], in1=x,
                                                       op0=ALU.mult, op1=ALU.add).then_inc(added, 1)

                chunk_loop(dve, CH, lambda c, e: split_tiles(c, e, range(LEAD)), chunk)


CH_HEADS, CH_D = 16, 16
GROUP = 4


def add_projected(nc, m, name, src, w, bias, gate):
    with ExitStack() as own:
        sb = lambda n, s, d=fp32: own.enter_context(nc.sbuf_tensor(f"{name}_{n}", s, d))
        srcT = sb("srcT", [P, DK, S])
        biased_sum = [sb(f"sum{i}", [P, BANK]) for i in range(2)]
        turned, moved, mixed, biased, added = (m.sem(f"{name}_{n}") for n in
                                               ("turned", "moved", "mixed", "biased", "added"))
        with nc.Block() as block:
            @block.tensor
            def _(pe):
                for g in range(ST // 4):
                    for k in range(DK):
                        for j in range(4):
                            last = nc.tensor.transpose(m.PS[:, 2 * g + k, j * P:(j + 1) * P],
                                                       src[:, 4 * g + j, k * P:(k + 1) * P], m.ident[:])
                        last.then_inc(turned, 1)
                for u in range(ST // 2):
                    if u % 2 == 0:
                        pe.wait_ge(moved, u + 2)
                    for t in (2 * u, 2 * u + 1):
                        for k in range(DK):
                            last = nc.tensor.matmul(m.PS[:, u // 2 * 2 + u % 2, (t % 2) * D:(t % 2 + 1) * D],
                                                    srcT[:, k, t * P:(t + 1) * P], w[:, k, :],
                                                    start=(k == 0), stop=(k == DK - 1))
                    last.then_inc(mixed, 1)

            @block.scalar
            def _(act):
                for g in range(ST // 4):
                    for k in range(DK):
                        act.wait_ge(turned, 2 * g + k + 1)
                        nc.scalar.activation(srcT[:, k, g * BANK:(g + 1) * BANK], m.PS[:, 2 * g + k, :],
                                             ACT.Copy).then_inc(moved, 1)

            @block.vector
            def _(dve):
                for u in range(ST // 2):
                    dve.wait_ge(mixed, u + 1)
                    if u >= 2:
                        dve.wait_ge(added, u - 1)
                    nc.vector.tensor_tensor(biased_sum[u % 2][:], m.PS[:, u, :], bias, ALU.add).then_inc(biased, 1)
                    dve.wait_ge(biased, u + 1)
                    x = m.X[:, 2 * u:2 * u + 2, :].rearrange("p t d -> p (t d)")
                    nc.vector.scalar_tensor_tensor(out=x, in0=biased_sum[u % 2][:], scalar=gate, in1=x,
                                                   op0=ALU.mult, op1=ALU.add).then_inc(added, 1)


def narrow_attention(nc, m, ctxT_d, wq_d, wk_d, wv_d, wo_d, bqk_d, bv_d, bo_d, q_parts, k_parts):
    SCALE = CH_D ** -0.5
    with ExitStack() as own:
        sb = lambda n, s, d=fp32: own.enter_context(nc.sbuf_tensor(f"c_{n}", s, d))
        wo, bo = sb("wo", [P, DK, D]), sb("bo", [P, 2, D])
        attended = sb("attended", [P, ST, D])
        bound = sb("bound", [1, 1])
        with ExitStack() as inner:
            si = lambda n, s, d=fp32: inner.enter_context(nc.sbuf_tensor(f"c_{n}", s, d))
            V = si("V", [P, CT, CH_HEADS, 32])
            xT = si("xT", [P, DK, S])
            with ExitStack() as proj:
                sp_ = lambda n, s, d=fp32: proj.enter_context(nc.sbuf_tensor(f"c_{n}", s, d))
                cT = sp_("cT", [P, DK, CTX])
                w = [sp_(f"w{n}", [P, DK, D]) for n in "qkv"]
                bqk, bv = sp_("bqk", [P, 2, 2]), sp_("bv", [P, D])
                full = [sp_("q", [P, 2, S]), sp_("k", [P, 2, CTX])]
                hi = [sp_("qh", [P, 2, S], fp16), sp_("kh", [P, 2, CTX], fp16)]
                lo = [sp_("ql", [P, 2, S], fp16), sp_("kl", [P, 2, CTX], fp16)]
                loaded, kept = m.sem("c_loaded"), m.sem("c_kept")

                def loads(sp):
                    sp.dma_start(cT[:], ctxT_d).then_inc(loaded, 16)
                    for w_sb, w_dram in zip(w, (wq_d, wk_d, wv_d)):
                        sp.dma_start(w_sb[:], w_dram).then_inc(loaded, 16)
                    sp.dma_start(wo[:], wo_d).then_inc(loaded, 16)
                    sp.dma_start(bqk[:], bqk_d).then_inc(loaded, 16)
                    sp.dma_start(bv[:], bv_d.partition_broadcast(P)).then_inc(loaded, 16)
                    sp.dma_start(bo[:], bo_d.partition_broadcast(P)).then_inc(loaded, 16)

                layernorm_transposed(nc, m, "c_ln", m.X, xT, 0, 4, loads=loads)
                projected, acted, split_hi, used = (m.sem(f"c_{n}") for n in ("projected", "acted", "hi", "used"))
                vcleared = m.sem("c_vcleared")
                units = [(qk, j, c0, min(BANK, n - c0)) for qk, n in ((1, CTX), (0, S)) for j in range(2)
                         for c0 in range(0, n, BANK)]
                NU = len(units)
                NV = -(-CT // 2)
                RING = 6
                squares = [sp_("q_squares", [P, 2, S], bf16), sp_("k_squares", [P, 2, CTX], bf16)]
                head_ones = sp_("head_ones", [P, 2, 32], bf16)
                peaks, top = sp_("peaks", [P, 2]), sp_("top", [1, 2])
                squared, normed, peaked, peaks_turned, topped = (
                    m.sem(f"c_{n}") for n in ("squared", "lengths", "peaked", "peaks_turned", "topped"))
                ones_set = m.sem("c_ones_set")
                with nc.Block() as block:
                    @block.sync
                    def _(sp):
                        for qk, n_used in ((1, NU // 2), (0, NU)):
                            sp.wait_ge(used, n_used)
                            parts = k_parts if qk else q_parts
                            sp.dma_start(parts[0], hi[qk][:]).then_inc(kept, 16)
                            sp.dma_start(parts[1], lo[qk][:]).then_inc(kept, 16)
                        sp.wait_ge(kept, 64)

                    @block.tensor
                    def _(pe):
                        pe.wait_ge(loaded, 128)
                        for u, (qk, j, c0, n) in enumerate(units):
                            if u >= RING:
                                pe.wait_ge(acted, u - RING + 1)
                            src = cT if qk else xT
                            for k in range(DK):
                                last = nc.tensor.matmul(m.PS[:, u % RING, 0:n], w[qk][:, k, j * P:(j + 1) * P],
                                                        src[:, k, c0:c0 + n], start=(k == 0), stop=(k == DK - 1))
                            last.then_inc(projected, 1)
                        for v in range(NV):
                            u = NU + v
                            pe.wait_ge(acted, min(u - RING + 1, NU))
                            if u - RING >= NU:
                                pe.wait_ge(used, u - RING + 1)
                            if v == 2:
                                pe.wait_ge(ones_set, 1)
                                pe.wait_ge(squared, NU)
                                for qk, n in ((1, CTX), (0, S)):
                                    for c in range(4):
                                        c0 = min(c * BANK, n - BANK)
                                        for j in range(2):
                                            last = nc.tensor.matmul(
                                                m.PS[32 * c:32 * c + 32, 7 - qk, :], head_ones[:, j, :],
                                                squares[qk][:, j, c0:c0 + BANK], start=(j == 0), stop=(j == 1),
                                                tile_position=(0, 32 * c))
                                last.then_inc(normed, 1)
                            for t in range(2 * v, min(2 * v + 2, CT)):
                                rows = P if t < CT - 1 else CLAST
                                for k in range(DK):
                                    last = nc.tensor.matmul(m.PS[0:rows, u % RING, (t % 2) * D:(t % 2 + 1) * D],
                                                            cT[:, k, t * P:t * P + rows], w[2][:, k, :],
                                                            start=(k == 0), stop=(k == DK - 1))
                            last.then_inc(projected, 1)
                        pe.wait_ge(peaked, 1)
                        for c in range(2):
                            last = nc.tensor.matmul(m.PS[0:1, 6, c * P:(c + 1) * P], peaks[:, c:c + 1], m.ident[:],
                                                    start=True, stop=True)
                        last.then_inc(peaks_turned, 1)

                    @block.scalar
                    def _(act):
                        act.wait_ge(loaded, 128)
                        for u, (qk, j, c0, n) in enumerate(units):
                            act.wait_ge(projected, u + 1)
                            if u == NU // 2:
                                act.wait_ge(vcleared, 3)
                            for dst, func, sem in ((squares, ACT.Square, squared), (full, ACT.Identity, acted)):
                                nc.scalar.activation(dst[qk][:, j, c0:c0 + n], m.PS[:, u % RING, 0:n], func,
                                                     bias=bqk[:, qk, j:j + 1], scale=1.0 if qk else SCALE).then_inc(sem, 1)

                    @block.vector
                    def _(dve):
                        nc.vector.memset(V[:], 0.0)
                        nc.vector.memset(head_ones[:], 0.0).then_inc(vcleared, 1)
                        dve.wait_ge(vcleared, 1)
                        nc.vector.memset(V[:, :, :, CH_D:CH_D + 1], 1.0).then_inc(vcleared, 1)
                        for j in range(2):
                            last = nc.vector.tensor_reduce(head_ones[:, j, 8 * j:8 * j + 8],
                                                           m.ident[:].rearrange("p (h d) -> p h d", d=CH_D), AX.X, ALU.max)
                        last.then_inc(ones_set, 1)
                        dve.wait_ge(loaded, 128)
                        nc.vector.tensor_scalar(bqk[:, 0, :], bqk[:, 0, :], SCALE, None, ALU.mult).then_inc(vcleared, 1)
                        for u, (qk, j, c0, n) in enumerate(units):
                            cols = slice(c0, c0 + n)
                            dve.wait_ge(acted, u + 1)
                            nc.vector.tensor_copy(hi[qk][:, j, cols], full[qk][:, j, cols]).then_inc(split_hi, 1)
                            dve.wait_ge(split_hi, u + 1)
                            nc.vector.tensor_tensor(lo[qk][:, j, cols], full[qk][:, j, cols], hi[qk][:, j, cols],
                                                    ALU.subtract).then_inc(used, 1)
                        for v in range(NV):
                            dve.wait_ge(projected, NU + v + 1)
                            for t in range(2 * v, min(2 * v + 2, CT)):
                                rows = P if t < CT - 1 else CLAST
                                ps = m.PS[0:rows, (NU + v) % RING, (t % 2) * D:(t % 2 + 1) * D]
                                last = nc.vector.tensor_tensor(
                                    V[0:rows, t, :, 0:CH_D], ps.rearrange("p (h d) -> p h d", d=CH_D),
                                    bv[0:rows, :].rearrange("p (h d) -> p h d", d=CH_D), ALU.add)
                            last.then_inc(used, 1)
                        dve.wait_ge(normed, 1)
                        nc.vector.tensor_reduce(peaks[:], m.PS[:, 6:8, :], AX.X, ALU.max).then_inc(peaked, 1)
                        dve.wait_ge(peaks_turned, 1)
                        nc.vector.tensor_reduce(top[:], m.PS[0:1, 6, 0:2 * P].rearrange("p (c n) -> p c n", n=P),
                                                AX.X, ALU.max).then_inc(topped, 1)
                        dve.wait_ge(topped, 1)
                        nc.vector.tensor_tensor(bound[:], top[:, 0:1], top[:, 1:2], ALU.mult)

            Kop = [si(f"Kop{i}", [P, CTX], fp16) for i in range(2)]
            Qop = [si(f"Qop{i}", [P, S], fp16) for i in range(2)]
            Vh = [si(f"Vh{i}", [P, CT, 32]) for i in range(2)]
            probs = [si(f"probs{i}", [P, 2 * BANK]) for i in range(4)]
            outT = [si(f"outT{i}", [P, BANK]) for i in range(2)]
            inverse = [si(f"inverse{i}", [P, 4, 4]) for i in range(2)]
            TILES = 2 * CT
            STEP_BANKS = (0, 2, 6)
            partial, negated = si("partial", [P, 1, 2, ST]), si("negated", [P, ST])
            spans = [(0, CTX)]
            MAX_SCORED, MAX_REDUCED = ST * len(spans) + 1, ST * len(spans) + 2
            row_cleared, max_scored, max_reduced = (m.sem(f"c_{n}") for n in ("row_cleared", "max_scored", "max_reduced"))
            rows_set, rows_cleared = m.sem("c_rows_set"), m.sem("c_rows_cleared")
            ops_in = [m.sem(f"c_ops_in{i}") for i in range(2)]
            scored, exped, applied, copied = (m.sem(f"c_{n}") for n in ("scored", "exped", "applied", "copied"))
            turned, inverted, normed, values_in = (m.sem(f"c_{n}") for n in ("turned", "inverted", "normed", "values_in"))
            krows = lambda t: P if t % CT < CT - 1 else CLAST
            with nc.Block() as block:
                @block.sync
                def _(sp):
                    sp.wait_ge(rows_set, 2)
                    for h in range(CH_HEADS):
                        if h >= 2:
                            sp.wait_ge(applied, (h - 1) * CT)
                        row = 16 * (h % 8)
                        for op, parts, order in ((Kop[h % 2], k_parts, (0, 1, 0, 1)), (Qop[h % 2], q_parts, (0, 0, 1, 1))):
                            for r, part in enumerate(order):
                                sp.dma_start(op[16 * r:16 * r + 16, :],
                                             parts[part][row:row + 16, h // 8, :]).then_inc(ops_in[h % 2], 16)

                @block.gpsimd
                def _(pool):
                    for e in range(2):
                        for op in (Kop[e], Qop[e]):
                            nc.gpsimd.memset(op[MAX_ROW:P, :], 0.0).then_inc(rows_cleared, 1)
                    pool.wait_ge(rows_cleared, 4)
                    nc.gpsimd.memset(Kop[0][MAX_ROW:MAX_ROW + 1, :], 1.0).then_inc(rows_set, 1)
                    pool.wait_ge(rows_set, 1)
                    nc.gpsimd.memset(Kop[1][MAX_ROW:MAX_ROW + 1, :], 1.0).then_inc(rows_set, 1)

                @block.tensor
                def _(pe):
                    bits = pe.value_load(bound[0:1, 0:1].bitcast(int32))

                    def pair(i, first=False):
                        def score(n):
                            t, hp = n // 2, n % 2
                            e, r, c0 = t // CT, krows(t), t % CT * P
                            if t % CT == 0 and hp == 0:
                                pe.wait_ge(ops_in[e], (i + 1) * (8 * 16))
                            if n >= 3:
                                pe.wait_ge(exped, i * (2 * TILES) + (n - 2))
                            for b in range(2):
                                q0 = (2 * hp + b) * BANK
                                last = nc.tensor.matmul(m.PS[0:r, STEP_BANKS[n % 3] + b, :], Kop[e][:, c0:c0 + r],
                                                        Qop[e][:, q0:q0 + BANK], start=True, stop=True)
                            last.then_inc(scored, 1)

                        def apply(t):
                            e, r = t // CT, krows(t)
                            if t % CT == 0:
                                pe.wait_ge(values_in, i * 2 + (e + 1))
                            pe.wait_ge(exped, i * (2 * TILES) + (2 * t + 2))
                            for q in range(4):
                                last = nc.tensor.matmul(m.PS[32 * q:32 * q + 32, 4 + e, :], Vh[e][0:r, t % CT, :],
                                                        probs[2 * (t % 2) + q // 2][0:r, (q % 2) * BANK:(q % 2 + 1) * BANK],
                                                        start=(t % CT == 0), stop=(t % CT == CT - 1),
                                                        tile_position=(0, 32 * q))
                            last.then_inc(applied, 1)

                        def turn(e, n):
                            pe.wait_ge(copied, n + 1)
                            for j in range(4):
                                last = nc.tensor.transpose(m.PS[:, 4 + e, j * P:(j + 1) * P], outT[e][:, j * P:(j + 1) * P],
                                                           m.ident[:])
                            last.then_inc(turned, 1)

                        with pe.If(bits > SAFE_BITS):
                            for e in range(2):
                                score_maxima_pe(nc, m, pe, (Qop[e],), (Kop[e],), spans, negated, max_scored, max_reduced,
                                                (i * 2 + e) * MAX_REDUCED,
                                                ready=((row_cleared, i + 1), (exped, i * (2 * TILES)),
                                                       (ops_in[e], (i + 1) * (8 * 16))))
                            pe.wait_ge(max_reduced, (i + 1) * (2 * MAX_REDUCED))
                        for n in range(3):
                            score(n)
                        if not first:
                            turn(1, i * 2 - 1)
                        for t in range(TILES):
                            for n in range(2 * t + 3, min(2 * t + 5, 2 * TILES)):
                                score(n)
                            apply(t)
                            if t == CT + 1:
                                turn(0, i * 2)
                        return turn

                    pair(0, first=True)
                    with pe.Fori(0, CH_HEADS // 2 - 1) as j:
                        turn = pair(j + 1)
                    turn(1, CH_HEADS - 1)

                @block.scalar
                def _(act):
                    nc.scalar.preload_act_table(ACT.Exp)
                    with act.Fori(0, CH_HEADS // 2) as i:
                        for n in range(2 * TILES):
                            t, hp = n // 2, n % 2
                            act.wait_ge(scored, i * (2 * TILES) + (n + 1))
                            act.wait_ge(applied, i * TILES + max(t - 1, 0))
                            r = krows(t)
                            nc.scalar.activation(probs[2 * (t % 2) + hp][0:r, :],
                                                 m.PS[0:r, STEP_BANKS[n % 3]:STEP_BANKS[n % 3] + 2, :].rearrange(
                                                     "p b c -> p (b c)"), ACT.Exp).then_inc(exped, 1)

                @block.vector
                def _(dve):
                    bits = dve.value_load(bound[0:1, 0:1].bitcast(int32))

                    def pair(i, first=False):
                        def place_values(e):
                            if not first:
                                dve.wait_ge(normed, i * 2 + e - 1)
                            nc.vector.tensor_copy(Vh[e][:], V[:, :, ds(i * 2 + e, 1), :].rearrange("p t o c -> p (t o) c")
                                                  ).then_inc(values_in, 1)

                        def output(e, n):
                            dve.wait_ge(applied, n * CT + CT)
                            nc.vector.tensor_copy(outT[e][:], m.PS[:, 4 + e, :]).then_inc(copied, 1)
                            dve.wait_ge(turned, n + 1)
                            out = m.PS[:, 4 + e, :].rearrange("p (j q d) -> p j q d", q=4, d=32)
                            nc.vector.reciprocal(inverse[e][:], out[:, :, :, CH_D]).then_inc(inverted, 1)
                            dve.wait_ge(inverted, n + 1)
                            dst = attended[:, :, ds(n * CH_D, CH_D)].rearrange("p (q j) d -> p j q d", q=4)
                            nc.vector.tensor_tensor(dst, out[:, :, :, 0:CH_D],
                                                    inverse[e][:].unsqueeze(3).to_broadcast([P, 4, 4, CH_D]),
                                                    ALU.mult).then_inc(normed, 1)

                        with dve.If(bits > SAFE_BITS):
                            dve.wait_ge(rows_set, 2)
                            dve.wait_ge(applied, i * TILES)
                            for e in range(2):
                                last = nc.vector.memset(Qop[e][MAX_ROW:MAX_ROW + 1, :], 0.0)
                            last.then_inc(row_cleared, 1)
                            for e in range(2):
                                score_maxima_dve(nc, m, dve, spans, partial, negated, Qop[e][MAX_ROW:MAX_ROW + 1, :],
                                                 max_scored, max_reduced, (i * 2 + e) * MAX_SCORED, (i * 2 + e) * MAX_REDUCED)
                        place_values(0)
                        if not first:
                            output(1, i * 2 - 1)
                        place_values(1)
                        output(0, i * 2)
                        return output

                    pair(0, first=True)
                    with dve.Fori(0, CH_HEADS // 2 - 1) as j:
                        output = pair(j + 1)
                    output(1, CH_HEADS - 1)

        add_projected(nc, m, "c_out", attended, wo, bo[:].rearrange("p t d -> p (t d)"), m.gate[:, 1:2])


LH, LD = 8, 64
INNER = LH * LD
HID = 682
GT = -(-HID // P)
DEPTH = 2


def local_layer(nc, m, name, Z, t, w):
    with ExitStack() as own:
        sb = lambda n, s, d=fp32: own.enter_context(nc.sbuf_tensor(f"{name}_{n}", s, d))
        ffn_loaded = m.sem("layer_ffn_loaded")
        with ExitStack() as attn:
            sa = lambda n, s, d=fp32: attn.enter_context(nc.sbuf_tensor(f"{name}_{n}", s, d))
            kT = sa("kT", [P, 4, S + P])
            V = sa("V", [P, ST + 1, LH, LD + 1])
            qT = sa("qT", [P, 4, S])
            with ExitStack() as first:
                sf = lambda n, s, d=fp32: first.enter_context(nc.sbuf_tensor(f"{name}_{n}", s, d))
                zT = sf("zT", [P, DK, S + 1])
                wqkv = sf("wqkv", [P, DK, 3 * INNER])
                tables = sf("tables", [P, 2, ST, 2, LD])
                scales = sf("scales", [P, 2, 2, LD])
                loaded, turned, moved = m.sem("layer_loaded"), m.sem("layer_turned"), m.sem("layer_moved")
                cleared = m.sem("layer_cleared")
                with nc.Block() as block:
                    @block.sync
                    def _(sp):
                        sp.dma_start(wqkv[:], w["wqkv"]).then_inc(loaded, 16)
                        sp.dma_start(tables[:], t["rotary"]).then_inc(loaded, 16)
                        sp.dma_start(scales[:], w["scales"].partition_broadcast(P)).then_inc(loaded, 16)
                        sp.wait_ge(loaded, 48)

                    @block.tensor
                    def _(pe):
                        for g in range(ST // 4):
                            for k in range(DK):
                                for j in range(4):
                                    last = nc.tensor.transpose(m.PS[:, 2 * g + k, j * P:(j + 1) * P],
                                                               Z[:, 4 * g + j, k * P:(k + 1) * P], m.ident[:])
                                last.then_inc(turned, 1)

                    @block.scalar
                    def _(act):
                        act.wait_ge(cleared, 1)
                        for g in range(ST // 4):
                            for k in range(DK):
                                act.wait_ge(turned, 2 * g + k + 1)
                                nc.scalar.activation(zT[:, k, g * BANK + k:(g + 1) * BANK + k], m.PS[:, 2 * g + k, :],
                                                     ACT.Copy).then_inc(moved, 1)

                    @block.gpsimd
                    def _(pool):
                        nc.gpsimd.memset(V[:, 0, :, :], 0.0)
                        nc.gpsimd.memset(V[:, 1:ST + 1, :, LD:LD + 1], 1.0)

                    @block.vector
                    def _(dve):
                        nc.vector.memset(zT[:, 1, 0:1], 0.0).then_inc(cleared, 1)
                        nc.vector.memset(kT[:, :, 0:P], 0.0)
                        dve.wait_ge(loaded, 48)
                        for half in range(2):
                            for qk in range(2):
                                x = tables[:, half, :, qk, :]
                                nc.vector.tensor_tensor(
                                    x, x, scales[:, half, qk, :].unsqueeze(1).to_broadcast([P, ST, LD]), ALU.mult)

                window = [sf(f"window{i}", [P, DK, P]) for i in range(2)]
                squares, unit = sf("squares", [P, 16, LD]), sf("unit", [P, 2, LH, 2, LD // 2])
                straight, crossed = sf("straight", [P, 2, LH, LD]), sf("crossed", [P, 2, LH, 2, LD // 2])
                rotated = [sf(f"rotated{i}", [P, 2 * INNER]) for i in range(2)]
                norms = sf("norms", [P, 4, 16])
                (windowed, projected, squared, valued, summed, rooted, united, crossed_done, rotated_done, step,
                 turned2, moved2) = (m.sem(f"layer_p_{n}") for n in (
                     "windowed", "projected", "squared", "valued", "summed", "rooted", "united", "crossed", "rotated",
                     "step", "turned", "moved"))
                straightened = m.sem("layer_p_straightened")
                with nc.Block() as block:
                    @block.tensor
                    def _(pe):
                        def project(wi, e):
                            pe.wait_ge(windowed, wi + 1)
                            for c in range(3):
                                for k in range(DK):
                                    last = nc.tensor.matmul(m.PS[:, 3 * e + c, :], window[e][:, k, :],
                                                            wqkv[:, k, c * BANK:(c + 1) * BANK],
                                                            start=(k == 0), stop=(k == DK - 1))
                            last.then_inc(projected, 1)

                        def turn(wi, e):
                            pe.wait_ge(rotated_done, wi + 1)
                            pe.wait_ge(moved2, wi)
                            for c in range(8):
                                last = nc.tensor.transpose(m.PS[:, 6 + c // 4, (c % 4) * P:(c % 4 + 1) * P],
                                                           rotated[e][:, c * P:(c + 1) * P], m.ident[:])
                            last.then_inc(turned2, 1)

                        project(0, 0)
                        project(1, 1)
                        with pe.Fori(0, ST // 2 - 1) as j:
                            for e in range(2):
                                project(j * 2 + (e + 2), e)
                                turn(j * 2 + e, e)
                        turn(ST - 2, 0)
                        turn(ST - 1, 1)

                    @block.scalar
                    def _(act):
                        nc.scalar.preload_act_table(ACT.Sqrt)

                        def values(wi, e):
                            act.wait_ge(projected, wi + 1)
                            nc.scalar.activation(squares[:].rearrange("p h d -> p (h d)"),
                                                 m.PS[:, 3 * e:3 * e + 2, :].rearrange("p b c -> p (b c)"),
                                                 ACT.Square).then_inc(squared, 1)
                            nc.scalar.activation(V[:, ds(wi + 1, 1), :, 0:LD].rearrange("p o h d -> p (o h) d"),
                                                 m.PS[:, 3 * e + 2, :].rearrange("p (h d) -> p h d", d=LD),
                                                 ACT.Copy).then_inc(valued, 1)
                            act.wait_ge(summed, wi + 1)
                            nc.scalar.activation(norms[:, 1, :], norms[:, 0, :], ACT.Sqrt).then_inc(rooted, 1)

                        def move(wi):
                            act.wait_ge(turned2, wi + 1)
                            nc.scalar.activation(qT[:, :, ds(wi * P, P)], m.PS[:, 6, :].rearrange("p (c n) -> p c n", n=P),
                                                 ACT.Copy)
                            nc.scalar.activation(kT[:, :, ds(wi * P + P, P)], m.PS[:, 7, :].rearrange("p (c n) -> p c n", n=P),
                                                 ACT.Copy).then_inc(moved2, 1)

                        values(0, 0)
                        values(1, 1)
                        with act.Fori(0, ST // 2 - 1) as j:
                            for e in range(2):
                                values(j * 2 + (e + 2), e)
                                move(j * 2 + e)
                        move(ST - 2)
                        move(ST - 1)

                    @block.vector
                    def _(dve):
                        def window_in(wi, e):
                            nc.vector.tensor_copy(window[e][:], zT[:, :, ds(wi * P, P)]).then_inc(windowed, 1)

                        def sum_squares(wi):
                            dve.wait_ge(squared, wi + 1)
                            nc.vector.tensor_reduce(norms[:, 0, :], squares[:], AX.X, ALU.add).then_inc(summed, 1)

                        def rotate(wi, e, more=True, last=False):
                            dve.wait_ge(rooted, wi + 1)
                            nc.vector.tensor_scalar(norms[:, 2, :], norms[:, 1, :], 1e-12, None, ALU.max).then_inc(step, 1)
                            dve.wait_ge(step, wi * 2 + 1)
                            nc.vector.reciprocal(norms[:, 3, :], norms[:, 2, :]).then_inc(step, 1)
                            dve.wait_ge(step, wi * 2 + 2)
                            nc.vector.tensor_tensor(
                                unit[:].rearrange("p q h a d -> p (q h) (a d)"),
                                m.PS[:, 3 * e:3 * e + 2, :].rearrange("p b (h d) -> p (b h) d", d=LD),
                                norms[:, 3, :].unsqueeze(2).to_broadcast([P, 16, LD]), ALU.mult).then_inc(united, 1)
                            if more:
                                dve.wait_ge(valued, wi + 1)
                                window_in(wi + 2, e)
                            dve.wait_ge(rotated_done, wi)
                            dve.wait_ge(united, wi + 1)
                            for qk in range(2):
                                product = nc.vector.tensor_tensor(
                                    straight[:, qk], unit[:, qk].rearrange("p h a d -> p h (a d)"),
                                    tables[:, 0, ds(wi, 1), qk, :].to_broadcast([P, LH, LD]), ALU.mult)
                            product.then_inc(straightened, 1)
                            if not last:
                                sum_squares(wi + 1)
                            dve.wait_ge(straightened, wi + 1)
                            dve.wait_ge(crossed_done, wi + 1)
                            dve.wait_ge(turned2, max(wi - 1, 0) if type(wi) is int else wi - 1)
                            nc.vector.tensor_tensor(rotated[e][:], straight[:].rearrange("p q h d -> p (q h d)"),
                                                    crossed[:].rearrange("p q h a d -> p (q h a d)"),
                                                    ALU.add).then_inc(rotated_done, 1)

                        window_in(0, 0)
                        window_in(1, 1)
                        sum_squares(0)
                        rotate(0, 0)
                        with dve.Fori(0, ST // 2 - 2) as j:
                            for e in (1, 0):
                                rotate(j * 2 + (1 if e else 2), e)
                        rotate(ST - 3, 1)
                        rotate(ST - 2, 0, more=False)
                        rotate(ST - 1, 1, more=False, last=True)

                    @block.gpsimd
                    def _(pool):
                        for wi in range(ST):
                            pool.wait_ge(united, wi + 1)
                            for qk in range(2):
                                for a in range(2):
                                    last = nc.gpsimd.tensor_tensor(
                                        crossed[:, qk, :, a, :], unit[:, qk, :, 1 - a, :],
                                        tables[:, 1, wi, qk, a * 32:a * 32 + 32].unsqueeze(1).to_broadcast([P, LH, LD // 2]),
                                        ALU.mult)
                            last.then_inc(crossed_done, 1)

            masks = sa("masks", [P, 2, 2 * P])
            wo = sa("wo", [P, 4, D])
            qstat = sa("qstat", [P, LH, P])
            scores, probs = sa("scores", [P, LH, 2 * P]), sa("probs", [P, LH, 2 * P])
            probsT = sa("probsT", [P, LH, 2, P])
            minus_max, inverse = sa("minus_max", [P, LH]), sa("inverse", [P, LH])
            heads_out, heads_outT = sa("heads_out", [P, INNER]), sa("heads_outT", [P, 4, P])
            (wloaded, qcleared, queried, scored, masked, maxed, exped, turned3, moved3, applied, inverted, normed,
             turned4, moved4, mixed, added) = (m.sem(f"layer_a_{n}") for n in (
                 "loaded", "qcleared", "queried", "scored", "masked", "maxed", "exped", "turned", "moved", "applied",
                 "inverted", "normed", "oturned", "omoved", "mixed", "added"))
            with nc.Block() as block:
                @block.sync
                def _(sp):
                    sp.dma_start(masks[:], t["masks"]).then_inc(wloaded, 16)
                    sp.dma_start(wo[:], w["wo"]).then_inc(wloaded, 16)
                    sp.wait_ge(wloaded, 32)

                @block.tensor
                def _(pe):
                    def score(wi):
                        pe.wait_ge(queried, wi + 1)
                        pe.wait_ge(masked, wi)
                        for h in range(LH):
                            last = nc.tensor.matmul(m.PS[:, h // 2, (h % 2) * D:(h % 2 + 1) * D], qstat[:, h, :],
                                                    kT[:, h // 2, ds(wi * P, 2 * P)], start=True, stop=True)
                        last.then_inc(scored, 1)

                    def turn_probs(wi, c):
                        if c == 0:
                            pe.wait_ge(exped, wi + 1)
                        else:
                            pe.wait_ge(added, wi)
                        for h in range(4 * c, 4 * c + 4):
                            for kt in range(2):
                                last = nc.tensor.transpose(
                                    m.PS[:, 4 + h // 2, (h % 2 * 2 + kt) * P:(h % 2 * 2 + kt + 1) * P],
                                    probs[:, h, kt * P:(kt + 1) * P], m.ident[:])
                        last.then_inc(turned3, 1)

                    def apply(wi, c):
                        pe.wait_ge(moved3, wi * 2 + (c + 1))
                        for h in range(4 * c, 4 * c + 4):
                            for kt in range(2):
                                last = nc.tensor.matmul(
                                    m.PS[:, 4 + c, (h % 4) * (LD + 1):(h % 4 + 1) * (LD + 1)], probsT[:, h, kt, :],
                                    V[:, ds(wi + kt, 1), h, :].rearrange("p o d -> p (o d)"),
                                    start=(kt == 0), stop=(kt == 1))
                        if c:
                            last.then_inc(applied, 1)

                    def turn_outputs(wi):
                        pe.wait_ge(normed, wi + 1)
                        for c in range(4):
                            last = nc.tensor.transpose(m.PS[:, 6, c * P:(c + 1) * P], heads_out[:, c * P:(c + 1) * P], m.ident[:])
                        last.then_inc(turned4, 1)

                    def mix(wi):
                        pe.wait_ge(moved4, wi + 1)
                        for c in range(4):
                            last = nc.tensor.matmul(m.PS[:, 7, 0:D], heads_outT[:, c, :], wo[:, c, :],
                                                    start=(c == 0), stop=(c == 3))
                        last.then_inc(mixed, 1)

                    def window(wi, before=True, after=True):
                        if after:
                            score(wi + 1)
                        if before:
                            turn_outputs(wi - 1)
                        turn_probs(wi, 0)
                        if before:
                            mix(wi - 1)
                        turn_probs(wi, 1)
                        apply(wi, 0)
                        apply(wi, 1)

                    pe.wait_ge(wloaded, 32)
                    score(0)
                    window(0, before=False)
                    with pe.Fori(0, ST - 2) as j:
                        window(j + 1)
                    window(ST - 1, after=False)
                    turn_outputs(ST - 1)
                    mix(ST - 1)

                @block.scalar
                def _(act):
                    nc.scalar.preload_act_table(ACT.Exp)

                    def expo(wi):
                        act.wait_ge(maxed, wi + 1)
                        for h in range(LH):
                            last = nc.scalar.activation(probs[:, h, :], scores[:, h, :], ACT.Exp, bias=minus_max[:, h:h + 1])
                        last.then_inc(exped, 1)

                    def move(wi):
                        for c in range(2):
                            act.wait_ge(turned3, wi * 2 + (c + 1))
                            nc.scalar.activation(probsT[:, 4 * c:4 * c + 4].rearrange("p h k n -> p (h k n)"),
                                                 m.PS[:, 4 + 2 * c:6 + 2 * c, :].rearrange("p b n -> p (b n)"),
                                                 ACT.Copy).then_inc(moved3, 1)

                    def move_outputs(wi):
                        act.wait_ge(turned4, wi + 1)
                        nc.scalar.activation(heads_outT[:].rearrange("p c n -> p (c n)"), m.PS[:, 6, :],
                                             ACT.Copy).then_inc(moved4, 1)

                    expo(0)
                    move(0)
                    expo(1)
                    with act.Fori(0, ST - 2) as j:
                        move_outputs(j)
                        move(j + 1)
                        expo(j + 2)
                    move_outputs(ST - 2)
                    move(ST - 1)
                    move_outputs(ST - 1)

                @block.vector
                def _(dve):
                    nc.vector.memset(qstat[:], 0.0).then_inc(qcleared, 1)
                    dve.wait_ge(qcleared, 1)
                    dve.wait_ge(wloaded, 32)

                    def queries(wi):
                        for e in range(2):
                            rows = slice(64 * e, 64 * e + 64)
                            last = nc.vector.tensor_copy(
                                qstat[rows].rearrange("p (c e) n -> p c e n", e=2)[:, :, e, :], qT[rows, :, ds(wi * P, P)])
                        last.then_inc(queried, 1)

                    def mask(wi):
                        kind = 0 if type(wi) is int and wi == 0 else 1
                        dve.wait_ge(scored, wi + 1)
                        dve.wait_ge(exped, wi)
                        nc.vector.tensor_tensor(scores[:], m.PS[:, 0:4, :].rearrange("p b (e n) -> p (b e) n", e=2),
                                                masks[:, kind:kind + 1, :].to_broadcast([P, LH, 2 * P]),
                                                ALU.add).then_inc(masked, 1)

                    def maxima(wi):
                        dve.wait_ge(masked, wi + 1)
                        nc.vector.tensor_reduce(minus_max[:], scores[:], AX.X, ALU.max, negate=True).then_inc(maxed, 1)

                    def normalize(wi):
                        dve.wait_ge(applied, wi + 1)
                        acc = m.PS[:, 4:6, 0:4 * (LD + 1)].rearrange("p b (h d) -> p b h d", d=LD + 1)
                        nc.vector.reciprocal(inverse[:].rearrange("p (b h) -> p b h", b=2), acc[:, :, :, LD]).then_inc(inverted, 1)
                        dve.wait_ge(inverted, wi + 1)
                        for c in range(2):
                            last = nc.vector.tensor_tensor(
                                heads_out[:, c * D:(c + 1) * D].rearrange("p (h d) -> p h d", d=LD), acc[:, c, :, 0:LD],
                                inverse[:, 4 * c:4 * c + 4].unsqueeze(2).to_broadcast([P, 4, LD]), ALU.mult)
                        last.then_inc(normed, 1)

                    def add(wi):
                        dve.wait_ge(mixed, wi + 1)
                        z = Z[:, ds(wi, 1), :].rearrange("p o d -> p (o d)")
                        nc.vector.tensor_tensor(z, z, m.PS[:, 7, 0:D], ALU.add).then_inc(added, 1)

                    queries(0)
                    mask(0)
                    maxima(0)
                    queries(1)
                    mask(1)
                    maxima(1)
                    queries(2)
                    normalize(0)
                    with dve.Fori(0, ST - 3) as j:
                        mask(j + 2)
                        add(j)
                        maxima(j + 2)
                        queries(j + 3)
                        normalize(j + 1)
                    mask(ST - 1)
                    add(ST - 3)
                    maxima(ST - 1)
                    normalize(ST - 2)
                    add(ST - 2)
                    normalize(ST - 1)
                    add(ST - 1)

        hT = sb("hT", [P, DK, S])
        w1, w2 = sb("w1", [P, DK, 2, GT, P]), sb("w2", [P, GT, D])
        b1, b2, aff = sb("b1", [P, 2, GT]), sb("b2", [P, 2, D]), sb("aff", [P, 2, DK])
        own_shifted = ExitStack()
        shifted = own_shifted.enter_context(nc.sbuf_tensor(f"{name}_shifted", [P, ST, D], fp32))
        moved, zeroed = m.sem("layer_shifted"), m.sem("layer_zeroed")
        with nc.Block() as block:
            @block.gpsimd
            def _(pool):
                nc.gpsimd.memset(shifted[0:1, 0, P:D], 0.0).then_inc(zeroed, 1)

            @block.sync
            def _(sp):
                sp.dma_start(shifted[1:P, :, P:D], Z[0:P - 1, :, P:D]).then_inc(moved, 16)
                sp.dma_start(shifted[0:1, 1:ST, P:D], Z[P - 1:P, 0:ST - 1, P:D]).then_inc(moved, 16)
                sp.dma_start(aff[:], w["aff"]).then_inc(moved, 16)
                for dst, src in ((w1, "w1"), (w2, "w2"), (b1, "b1")):
                    sp.dma_start(dst[:], w[src]).then_inc(ffn_loaded, 16)
                sp.dma_start(b2[:], w["b2"].partition_broadcast(P)).then_inc(ffn_loaded, 16)
                sp.wait_ge(moved, 16 * 3)

            @block.vector
            def _(dve):
                nc.vector.tensor_copy(shifted[:, :, 0:P], Z[:, :, 0:P])

        layernorm_transposed(nc, m, f"{name}_ln", shifted, hT, 0, 4, (aff[:, 0, :], aff[:, 1, :]), sems="layer_ln")

        own_shifted.close()
        hidden = [sb(f"hidden{i}", [P, BANK]) for i in range(2)]
        hidden_hi, hidden_lo = ([sb(f"hidden_{part}{i}", [P, GT, BANK]) for i in range(2)] for part in ("hi", "lo"))
        w1_hi, w2_hi, hT_hi = sb("w1_hi", [P, DK, 2, GT, P]), sb("w2_hi", [P, GT, D]), sb("hT_hi", [P, DK, S])
        w1_lo, w2_lo, hT_lo = sb("w1_lo", [P, DK, 2, GT, P]), sb("w2_lo", [P, GT, D]), sb("hT_lo", [P, DK, S])
        gelus = [sb(f"gelu{i}", [P, BANK]) for i in range(2)]
        out_b = [sb(f"out{i}", [P, BANK]) for i in range(2)]
        CH = S // BANK
        up, acted, gated, hidden_split, down, biased, added = (m.sem(f"layer_f_{n}") for n in (
            "up", "acted", "gated", "hidden_split", "down", "biased", "added"))
        w_hi, w_split, h_hi, h_split, hid_hi = (m.sem(f"layer_f_{n}") for n in
                                                ("w_hi", "w_split", "h_hi", "h_split", "hid_hi"))
        with nc.Block() as block:
            @block.gpsimd
            def _(pool):
                pool.wait_ge(w_hi, 1)
                for t in range(GT):
                    take_lo(nc.gpsimd, w1_lo[:, :, :, t, :], w1[:, :, :, t, :], w1_hi[:, :, :, t, :]).then_inc(w_split, 1)
                pool.wait_ge(w_hi, 2)
                take_lo(nc.gpsimd, w2_lo[:], w2[:], w2_hi[:]).then_inc(w_split, 1)

            @block.tensor
            def _(pe):
                def raise_tiles(c, e, tiles):
                    pe.wait_ge(h_split, c + 1)
                    for t in tiles:
                        pe.wait_ge(w_split, t + 1)
                        if t > 1 or type(c) is not int or c:
                            pe.wait_ge(gated, c * GT + (t - 1))
                        for ag in (1, 0):
                            for k in range(DK):
                                tokens = ds(c * BANK, BANK)
                                last = split_matmul(nc, m.PS[:, 2 * (t % 2) + ag, :],
                                                    (w1_hi[:, k, ag, t, :], w1_lo[:, k, ag, t, :]),
                                                    (hT_hi[:, k, tokens], hT_lo[:, k, tokens]), k == 0, k == DK - 1)
                            last.then_inc(up, 1)

                def chunk(c, e, more):
                    raise_tiles(c, e, range(LEAD, GT))
                    if more:
                        raise_tiles(c + 1, 1 - e, range(LEAD))
                    pe.wait_ge(w_split, GT + 1)
                    for u in range(2):
                        pe.wait_ge(hidden_split, (c + 1) * GT)
                        pe.wait_ge(biased, c * 2)
                        for t in range(2):
                            tokens = slice((2 * u + t) * P, (2 * u + t + 1) * P)
                            for h in range(GT):
                                last = split_matmul(nc, m.PS[:, 4 + u, t * D:(t + 1) * D],
                                                    (hidden_hi[e][:, h, tokens], hidden_lo[e][:, h, tokens]),
                                                    (w2_hi[:, h, :], w2_lo[:, h, :]), h == 0, h == GT - 1)
                        last.then_inc(down, 1)

                chunk_loop(pe, CH, lambda c, e: raise_tiles(c, e, range(LEAD)), chunk)

            @block.scalar
            def _(act):
                nc.scalar.preload_act_table(ACT.Gelu)
                with act.Fori(0, CH) as c:
                    for t in range(GT):
                        act.wait_ge(up, c * (2 * GT) + (2 * t + 1))
                        act.wait_ge(gated, c * GT + max(t - 1, 0))
                        nc.scalar.activation(gelus[t % 2][:], m.PS[:, 2 * (t % 2) + 1, :], ACT.Gelu,
                                             bias=b1[:, 1, t:t + 1]).then_inc(acted, 1)

            @block.vector
            def _(dve):
                dve.wait_ge(ffn_loaded, 64)
                take_hi(nc.vector, w1_hi[:], w1[:]).then_inc(w_hi, 1)
                for c in range(CH):
                    tokens = slice(c * BANK, (c + 1) * BANK)
                    take_hi(nc.vector, hT_hi[:, :, tokens], hT[:, :, tokens]).then_inc(h_hi, 1)
                    dve.wait_ge(h_hi, c + 1)
                    take_lo(nc.vector, hT_lo[:, :, tokens], hT[:, :, tokens], hT_hi[:, :, tokens]).then_inc(h_split, 1)
                    if c == 1:
                        take_hi(nc.vector, w2_hi[:], w2[:]).then_inc(w_hi, 1)

                def split_hidden(c, e, t):
                    dve.wait_ge(gated, c * GT + (t + 1))
                    take_hi(nc.vector, hidden_hi[e][:, t, :], hidden[t % 2][:]).then_inc(hid_hi, 1)
                    dve.wait_ge(hid_hi, c * GT + (t + 1))
                    take_lo(nc.vector, hidden_lo[e][:, t, :], hidden[t % 2][:],
                            hidden_hi[e][:, t, :]).then_inc(hidden_split, 1)

                def gate_tiles(c, e, tiles):
                    for t in tiles:
                        dve.wait_ge(up, c * (2 * GT) + (2 * t + 2))
                        dve.wait_ge(acted, c * GT + (t + 1))
                        dve.wait_ge(hidden_split, c * GT + max(t - 1, 0))
                        nc.vector.scalar_tensor_tensor(out=hidden[t % 2][:], in0=m.PS[:, 2 * (t % 2), :],
                                                       scalar=b1[:, 0, t:t + 1], in1=gelus[t % 2][:],
                                                       op0=ALU.add, op1=ALU.mult).then_inc(gated, 1)
                        split_hidden(c, e, t)

                def chunk(c, e, more):
                    gate_tiles(c, e, range(LEAD, GT))
                    if more:
                        gate_tiles(c + 1, 1 - e, range(LEAD))
                    for u in range(2):
                        dve.wait_ge(down, c * 2 + (u + 1))
                        dve.wait_ge(added, c * 2)
                        nc.vector.tensor_tensor(out_b[u][:], m.PS[:, 4 + u, :],
                                                b2[:].rearrange("p t d -> p (t d)"), ALU.add).then_inc(biased, 1)
                    for u in range(2):
                        dve.wait_ge(biased, c * 2 + (u + 1))
                        z = Z[:, ds(c * 4 + 2 * u, 2), :].rearrange("p t d -> p (t d)")
                        nc.vector.tensor_tensor(z, z, out_b[u][:], ALU.add).then_inc(added, 1)

                chunk_loop(dve, CH, lambda c, e: gate_tiles(c, e, range(LEAD)), chunk)


def local_transformer(nc, m, tables, layers, out_d):
    token_statistics(nc, m, "d_ln", m.X, ST)
    with nc.sbuf_tensor("Z", [P, ST, D], fp32) as Z:
        with nc.Block() as block:
            @block.vector
            def _(dve):
                for t in range(ST):
                    nc.vector.tensor_scalar(Z[:, t, :], m.X[:, t, :], m.mean[:, t:t + 1], m.rstd[:, t:t + 1],
                                            ALU.subtract, ALU.mult)
        for l, w in enumerate(layers):
            m.give_back("layer_" if l else "a_")
            local_layer(nc, m, f"d{l}", Z, tables, w)
        mixed_in, stored = m.sem("d_mixed_in"), m.sem("d_stored")
        with nc.Block() as block:
            @block.vector
            def _(dve):
                for c in range(4):
                    x = m.X[:, 4 * c:4 * c + 4, :].rearrange("p t d -> p (t d)")
                    nc.vector.scalar_tensor_tensor(out=x, in0=Z[:, 4 * c:4 * c + 4, :].rearrange("p t d -> p (t d)"),
                                                   scalar=m.gate[:, 3:4], in1=x, op0=ALU.mult,
                                                   op1=ALU.add).then_inc(mixed_in, 1)

            @block.sync
            def _(sp):
                for c in range(4):
                    sp.wait_ge(mixed_in, c + 1)
                    sp.dma_start(out_d[4 * c * P:4 * (c + 1) * P, :].rearrange("(t p) d -> p t d", p=P),
                                 m.X[:, 4 * c:4 * c + 4, :]).then_inc(stored, 16)
                sp.wait_ge(stored, 64)


LAYER_INPUTS = ("wqkv", "scales", "wo", "w1", "b1", "w2", "b2", "aff")


def flamingo_blocks(nc, d):
    q_parts = [nc.dram_tensor(f"q_part{i}", (P, DK, S), fp16, kind="Internal").ap() for i in range(2)]
    k_parts = [nc.dram_tensor(f"k_part{i}", (P, DK, CTX), fp16, kind="Internal").ap() for i in range(2)]
    layers = [{n: d[f"l1f_{n}{l}"] for n in LAYER_INPUTS} for l in range(DEPTH)]
    with ExitStack() as ctx:
        m = Memory(nc, ctx)
        setup(nc, m, d["x"], d["ident"], d["gates"])
        context_attention(nc, m, d["ctx"], d["mask"], d["l0x_aff"], d["l0x_wq"], d["l0x_wk"], d["l0x_wv"], d["l0x_wo"])
        lora_ffn(nc, m, d["l0f_w1"], d["l0f_b1"], d["l0f_w2"], d["l0f_b2"], d["l0f_scale"])
        narrow_attention(nc, m, d["ctxT"], d["l1x_wq"], d["l1x_wk"], d["l1x_wv"], d["l1x_wo"],
                         d["l1x_bqk"], d["l1x_bv"], d["l1x_bo"], q_parts, k_parts)
        local_transformer(nc, m, dict(rotary=d["rotary"], masks=d["masks"]), layers, d["out"])


def rotary_tables():
    f = np.float32
    half = np.arange(0, LD, 2, dtype=f)
    inv_freq = (f(1.0) / f(10000.0) ** (half / f(LD))).astype(f)
    pos = np.arange(S, dtype=f)
    angle = np.tile((pos[:, None] * inv_freq[None, :]).astype(f), 2)
    base = ((half + f(0.4 * LD)) / f(1.4 * LD)).astype(f)
    power = ((pos - S // 2) / f(P // 2)).astype(f)
    scale = np.tile((base[None, :] ** power[:, None]).astype(f), 2)
    cos, sin = np.cos(angle), np.sin(angle) * np.repeat(np.array([-1, 1], f), LD // 2)
    table = np.stack([np.stack([8 * cos * scale, cos / scale], 1), np.stack([8 * sin * scale, sin / scale], 1)])
    return table.astype(f).reshape(2, ST, P, 2, LD).transpose(2, 0, 1, 3, 4)


def window_masks():
    i, j = np.arange(P)[:, None], np.arange(P)[None, :]
    big = np.float32(-1e30)
    mask = np.zeros((P, 2, 2 * P), np.float32)
    mask[:, :, 0:P] = np.where(j < i, big, 0)[:, None]
    mask[:, 0, 0:P] = big
    mask[:, :, P:] = np.where(j > i, big, 0)[:, None]
    return mask


def lay_out(a):
    rows = lambda w, n: w.reshape(n, P, -1).transpose(1, 0, 2)
    col = lambda v: v.reshape(-1, P).T
    twice = lambda v: np.stack([v, v])
    d = dict(x=a["x"][0], ident=np.eye(P, dtype=np.float32), gates=np.concatenate([a["g_xattn"], a["g_ffn"]]),
             ctx=a["ctx_1024"][0], mask=a["mask_BxS2_bf1"].view(np.uint8), ctxT=rows(a["ctx_1024"][0].T, DK),
             rotary=rotary_tables(), masks=window_masks())
    d["l0x_aff"] = np.stack([col(a[f"L0_xattn_{n}"]) for n in ("gm", "bm", "gl", "bl")], 1)
    for n in "qkv":
        d[f"l0x_w{n}"] = a[f"L0_xattn_W{n}"].reshape(DK, P, PAIRS, P).transpose(2, 1, 0, 3)
    d["l0x_wo"] = a["L0_xattn_Wo"].reshape(PAIRS, P, D)
    d["l0f_w1"], d["l0f_b1"] = rows(a["L0_ffn_W1"].T, DK), col(a["L0_ffn_b1"])
    d["l0f_w2"], d["l0f_b2"] = rows(a["L0_ffn_W2"].T, HT), twice(a["L0_ffn_b2"])
    d["l0f_scale"] = a["L0_ffn_scale"].reshape(1)
    for n in "qkvo":
        d[f"l1x_w{n}"] = rows(a[f"L1_xattn_W{n}"], DK)
    d["l1x_bqk"] = np.stack([col(a["L1_xattn_bq"]), col(a["L1_xattn_bk"])], 1)
    d["l1x_bv"], d["l1x_bo"] = a["L1_xattn_bv"], twice(a["L1_xattn_bo"])
    for l in range(DEPTH):
        g = lambda n: a[f"L1_ffn_{n}"][l]
        swapped = lambda v: np.concatenate([v[LD // 2:], v[:LD // 2]])
        w1, b1 = np.zeros((D, 2, GT * P), np.float32), np.zeros((2, GT * P), np.float32)
        w2 = np.zeros((GT * P, D), np.float32)
        w1[:, :, :HID], b1[:, :HID], w2[:HID] = g("w1").reshape(D, 2, HID), g("b1").reshape(2, HID), g("w2")
        qk_scales = [g("q_scale"), g("k_scale")]
        layer = dict(wqkv=rows(g("wqkv"), DK), scales=np.stack([np.stack(qk_scales), np.stack([swapped(v) for v in qk_scales])]),
                     wo=rows(g("wo"), INNER // P), w1=w1.reshape(DK, P, 2, GT, P).transpose(1, 0, 2, 3, 4),
                     b1=b1.reshape(2, GT, P).transpose(2, 0, 1), w2=rows(w2, GT), b2=twice(g("b2")),
                     aff=np.stack([col(g("ln_g")), col(g("ln_b"))], 1))
        d.update({f"l1f_{n}{l}": v for n, v in layer.items()})
    return {n: np.ascontiguousarray(v) for n, v in d.items()}


def kernel(**inputs):
    import concourse.bacc as bacc
    from concourse.bass_utils import run_bass_kernel_spmd

    nc = bacc.Bacc("TRN2", target_bir_lowering=False, num_devices=1)
    arrays = lay_out({n: np.asarray(v) for n, v in inputs.items()})
    d = {n: nc.dram_tensor(f"in_{n}_dram", v.shape, mybir.dt.from_np(v.dtype), kind="ExternalInput").ap()
         for n, v in arrays.items()}
    d["out"] = nc.dram_tensor("out_0_dram", (S, D), fp32, kind="ExternalOutput").ap()
    flamingo_blocks(nc, d)
    r = run_bass_kernel_spmd(nc, [{f"in_{n}_dram": v for n, v in arrays.items()}], core_ids=[0])
    return np.asarray(r.results[0]["out_0_dram"]).reshape(1, S, D)
```
